# Optimizing a Trainium2 kernel written in Bass

```python
import numpy as np
import jax
import jax.numpy as jnp

def _softmax(x, axis=-1):
    return jax.nn.softmax(x, axis=axis)

def _gelu(x):
    return jax.nn.gelu(x, approximate=True)

def _silu(x):
    return jax.nn.silu(x)

def _sigmoid(x):
    return jax.nn.sigmoid(x)

def _layernorm(x, axis=-1, eps=1e-05):
    m = jnp.mean(x, axis=axis, keepdims=True)
    v = jnp.var(x, axis=axis, keepdims=True)
    return (x - m) / jnp.sqrt(v + eps)

def _scatter_add(tgt, idx, src, axis=0):
    return tgt.at[idx].add(src)

def _segment_sum(src, seg, n):
    return jax.ops.segment_sum(src, seg, n)
kernel_name = 'mk_adaln_ffn_d2_seqx_r4_baebee'

def setup_inputs(seed: int=0):
    np.random.seed(seed)
    _w = jnp.asarray

    def _rec_inputs():
        import jax
        import jax.numpy as jnp
        _rk = jax.random.key(seed)
        x = -0.000125 + 0.9999 * jax.random.normal(jax.random.fold_in(_rk, 1), (64, 64, 256), jnp.float32)
        _lenS = 64 - jax.random.randint(jax.random.fold_in(_rk, 7), (64,), 0, max(1, 64 // 4) + 1, jnp.int32)
        _lenS2 = 64 - jax.random.randint(jax.random.fold_in(_rk, 8), (64,), 0, max(1, 64 // 4) + 1, jnp.int32)
        cond_256 = -0.0209273 + 1.04763 * jax.random.normal(jax.random.fold_in(_rk, 11), (64, 64), jnp.float32)
        cond_64 = 0.0223021 + 1.01123 * jax.random.normal(jax.random.fold_in(_rk, 12), (64, 64), jnp.float32)
        _validS = jnp.arange(64)[None, :] < _lenS[:, None]
        _validS2 = jnp.arange(64)[None, :] < _lenS2[:, None]
        _causal = jnp.tril(jnp.ones((64, 64), dtype=bool))
        mask_SxS_bk1 = jnp.broadcast_to(_validS[0:1, :], (64, 64))
        return (x, cond_256, cond_64, mask_SxS_bk1)
    x, cond_256, cond_64, mask_SxS_bk1 = _rec_inputs()

    def _L0_cond_setup():
        import math
        import jax, jax.numpy as jnp
        import numpy as np
        from jax.scipy.linalg import cholesky, solve_triangular
        B, S, D, O, K, R = (4, 2048, 256, 256, 64, 64)

        def build_dct_basis(dim: int, num_bases: int) -> np.ndarray:
            num_bases = min(num_bases, dim)
            positions = np.arange(dim, dtype=np.float32)[None, :]
            modes = np.arange(num_bases, dtype=np.float32)[:, None]
            basis = np.cos(math.pi / float(dim) * (positions + 0.5) * modes)
            basis[0] = basis[0] / math.sqrt(2.0)
            basis = basis * math.sqrt(2.0 / float(dim))
            return basis.astype(np.float32)

        def _orthogonalize_mode_to_rank(raw: jnp.ndarray) -> jnp.ndarray:
            raw = raw.astype(jnp.float32)
            gram = raw.T @ raw
            eye = jnp.eye(raw.shape[1], dtype=jnp.float32)
            chol = cholesky(gram + 0.0001 * eye, lower=True)
            inv_chol = solve_triangular(chol, eye, lower=True)
            q = raw @ inv_chol.T
            signs = jnp.sign(jnp.sum(q * raw, axis=0, keepdims=True))
            signs = jnp.where(signs == 0, jnp.ones_like(signs), signs)
            return q * signs
        key = jax.random.key(seed)
        k1, k2, k3, k4, k5 = jax.random.split(key, 5)
        x = jax.random.normal(k1, (B, S, D), dtype=jnp.float32)
        spectral_coeff = jax.random.normal(k2, (B, K), dtype=jnp.float32)
        rank_coeff = jax.random.normal(k3, (B, R), dtype=jnp.float32)
        input_basis = jnp.asarray(build_dct_basis(D, K))
        diag = min(K, R)
        mode_to_rank = 0.02 * jax.random.normal(k4, (K, R), dtype=jnp.float32)
        mode_to_rank = mode_to_rank.at[:diag, :diag].add(jnp.eye(diag, dtype=jnp.float32))
        output_basis = 0.02 * jax.random.normal(k5, (R, O), dtype=jnp.float32)
        return {'x': x, 'spectral_coeff': spectral_coeff, 'rank_coeff': rank_coeff, 'input_basis': input_basis, 'mode_to_rank': mode_to_rank, 'output_basis': output_basis}
    _L0_cond_all = _L0_cond_setup()
    _L0_cond_in = {k: v for k, v in _L0_cond_all.items() if k in ('input_basis', 'mode_to_rank', 'output_basis')}
    del _L0_cond_all

    def _L0_ffn_setup():
        import jax, jax.numpy as jnp
        import numpy as np
        D_MODEL = 256
        D_FF = 1024
        N_EXPERTS = 8
        TOP_K = 2
        D_FF_PER = D_FF // N_EXPERTS
        B, T = (4, 512)
        key = jax.random.key(seed)
        ks = jax.random.split(key, 7)
        b1_bound = 1.0 / np.sqrt(D_MODEL)
        b2_bound = 1.0 / np.sqrt(D_FF_PER)
        return {'x': jax.random.normal(ks[0], (B, T, D_MODEL), dtype=jnp.float32), 'router_w': jax.random.uniform(ks[1], (D_MODEL, N_EXPERTS), minval=-b1_bound, maxval=b1_bound, dtype=jnp.float32), 'router_b': jax.random.uniform(ks[2], (N_EXPERTS,), minval=-b1_bound, maxval=b1_bound, dtype=jnp.float32), 'W1': jax.random.uniform(ks[3], (N_EXPERTS, D_MODEL, D_FF_PER), minval=-b1_bound, maxval=b1_bound, dtype=jnp.float32), 'b1': jax.random.uniform(ks[4], (N_EXPERTS, D_FF_PER), minval=-b1_bound, maxval=b1_bound, dtype=jnp.float32), 'W2': jax.random.uniform(ks[5], (N_EXPERTS, D_FF_PER, D_MODEL), minval=-b2_bound, maxval=b2_bound, dtype=jnp.float32), 'b2': jax.random.uniform(ks[6], (N_EXPERTS, D_MODEL), minval=-b2_bound, maxval=b2_bound, dtype=jnp.float32)}
    _L0_ffn_all = _L0_ffn_setup()
    _L0_ffn_in = {k: v for k, v in _L0_ffn_all.items() if k in ('router_w', 'router_b', 'W1', 'b1', 'W2', 'b2')}
    del _L0_ffn_all

    def _L1_cond_setup():
        import jax, jax.numpy as jnp
        import numpy as np
        EPS = 1e-06
        key = jax.random.key(seed)
        ks = jax.random.split(key, 8)
        B, S, E, C = (2, 512, 256, 64)
        x = jax.random.normal(ks[0], (B, S, E), dtype=jnp.float32)
        mask = jnp.triu(jnp.ones((S, S), dtype=bool), k=1)
        conditioning = jax.random.normal(ks[1], (B, C), dtype=jnp.float32)
        sc = 1.0 / np.sqrt(E)
        Wq = jax.random.normal(ks[2], (E, E), dtype=jnp.float32) * sc
        Wk = jax.random.normal(ks[3], (E, E), dtype=jnp.float32) * sc
        Wv = jax.random.normal(ks[4], (E, E), dtype=jnp.float32) * sc
        Wo = jax.random.normal(ks[5], (E, E), dtype=jnp.float32) * sc
        rms_scale = jnp.ones((E,), dtype=jnp.float32)
        Wc = jax.random.normal(ks[6], (2 * E, C), dtype=jnp.float32) * 0.02
        bc = jax.random.normal(ks[7], (2 * E,), dtype=jnp.float32) * 0.02
        return {'x': x, 'mask': mask, 'conditioning': conditioning, 'Wq': Wq, 'Wk': Wk, 'Wv': Wv, 'Wo': Wo, 'rms_scale': rms_scale, 'Wc': Wc, 'bc': bc}
    _L1_cond_all = _L1_cond_setup()
    _L1_cond_in = {k: v for k, v in _L1_cond_all.items() if k in ('Wq', 'Wk', 'Wv', 'Wo', 'rms_scale', 'Wc', 'bc')}
    del _L1_cond_all

    def _L1_ffn_setup():
        import jax, jax.numpy as jnp
        import numpy as np
        QMAX = 127.0

        def _ste_round(v):
            return v + jax.lax.stop_gradient(jnp.round(v) - v)

        def _act_fake_quant(x, clip_factor):
            scale = jax.nn.sigmoid(clip_factor) * jnp.max(jnp.abs(x)) / QMAX
            return jnp.clip(_ste_round(x / scale), -QMAX - 1.0, QMAX) * scale

        def _weight_fake_quant(w):
            scale = jnp.max(jnp.abs(w), axis=1, keepdims=True) / QMAX
            return jnp.clip(_ste_round(w / scale), -QMAX - 1.0, QMAX) * scale
        key = jax.random.key(seed)
        k1, k2, k3, k4 = jax.random.split(key, 4)
        B, S, H, I = (8, 2048, 256, 704)
        return {'x': jax.random.normal(k1, (B, S, H), dtype=jnp.float32), 'clip_x': jnp.full((1,), 4.0, dtype=jnp.float32), 'clip_down': jnp.full((1,), 4.0, dtype=jnp.float32), 'w_gate': jax.random.normal(k2, (I, H), dtype=jnp.float32) * 0.02, 'w_up': jax.random.normal(k3, (I, H), dtype=jnp.float32) * 0.02, 'w_down': jax.random.normal(k4, (H, I), dtype=jnp.float32) * 0.02}
    _L1_ffn_all = _L1_ffn_setup()
    _L1_ffn_in = {k: v for k, v in _L1_ffn_all.items() if k in ('clip_x', 'clip_down', 'w_gate', 'w_up', 'w_down')}
    del _L1_ffn_all
    return {'x': x, 'cond_256': cond_256, 'cond_64': cond_64, 'mask_SxS_bk1': mask_SxS_bk1, 'L0_cond_input_basis': _L0_cond_in['input_basis'], 'L0_cond_mode_to_rank': _L0_cond_in['mode_to_rank'], 'L0_cond_output_basis': _L0_cond_in['output_basis'], 'L0_ffn_router_w': _L0_ffn_in['router_w'], 'L0_ffn_router_b': _L0_ffn_in['router_b'], 'L0_ffn_W1': _L0_ffn_in['W1'], 'L0_ffn_b1': _L0_ffn_in['b1'], 'L0_ffn_W2': _L0_ffn_in['W2'], 'L0_ffn_b2': _L0_ffn_in['b2'], 'L1_cond_Wq': _L1_cond_in['Wq'], 'L1_cond_Wk': _L1_cond_in['Wk'], 'L1_cond_Wv': _L1_cond_in['Wv'], 'L1_cond_Wo': _L1_cond_in['Wo'], 'L1_cond_rms_scale': _L1_cond_in['rms_scale'], 'L1_cond_Wc': _L1_cond_in['Wc'], 'L1_cond_bc': _L1_cond_in['bc'], 'L1_ffn_clip_x': _L1_ffn_in['clip_x'], 'L1_ffn_clip_down': _L1_ffn_in['clip_down'], 'L1_ffn_w_gate': _L1_ffn_in['w_gate'], 'L1_ffn_w_up': _L1_ffn_in['w_up'], 'L1_ffn_w_down': _L1_ffn_in['w_down']}

def reference(x, cond_256, cond_64, mask_SxS_bk1, L0_cond_input_basis, L0_cond_mode_to_rank, L0_cond_output_basis, L0_ffn_router_w, L0_ffn_router_b, L0_ffn_W1, L0_ffn_b1, L0_ffn_W2, L0_ffn_b2, L1_cond_Wq, L1_cond_Wk, L1_cond_Wv, L1_cond_Wo, L1_cond_rms_scale, L1_cond_Wc, L1_cond_bc, L1_ffn_clip_x, L1_ffn_clip_down, L1_ffn_w_gate, L1_ffn_w_up, L1_ffn_w_down):
    import jax
    import jax.numpy as jnp

    def _L0_cond_ref(x, spectral_coeff, rank_coeff, input_basis, mode_to_rank, output_basis):
        import math
        import jax, jax.numpy as jnp
        import numpy as np
        from jax.scipy.linalg import cholesky, solve_triangular
        B, S, D, O, K, R = (4, 2048, 256, 256, 64, 64)

        def build_dct_basis(dim: int, num_bases: int) -> np.ndarray:
            num_bases = min(num_bases, dim)
            positions = np.arange(dim, dtype=np.float32)[None, :]
            modes = np.arange(num_bases, dtype=np.float32)[:, None]
            basis = np.cos(math.pi / float(dim) * (positions + 0.5) * modes)
            basis[0] = basis[0] / math.sqrt(2.0)
            basis = basis * math.sqrt(2.0 / float(dim))
            return basis.astype(np.float32)

        def _orthogonalize_mode_to_rank(raw: jnp.ndarray) -> jnp.ndarray:
            raw = raw.astype(jnp.float32)
            gram = raw.T @ raw
            eye = jnp.eye(raw.shape[1], dtype=jnp.float32)
            chol = cholesky(gram + 0.0001 * eye, lower=True)
            inv_chol = solve_triangular(chol, eye, lower=True)
            q = raw @ inv_chol.T
            signs = jnp.sign(jnp.sum(q * raw, axis=0, keepdims=True))
            signs = jnp.where(signs == 0, jnp.ones_like(signs), signs)
            return q * signs
        mtr = _orthogonalize_mode_to_rank(mode_to_rank).astype(x.dtype)
        proj = jnp.einsum('bsd,kd->bsk', x, input_basis.astype(x.dtype))
        proj = proj * spectral_coeff[:, None, :]
        hidden = jnp.einsum('bsk,kr->bsr', proj, mtr)
        hidden = hidden * rank_coeff[:, None, :]
        out = jnp.einsum('bsr,ro->bso', hidden, output_basis.astype(x.dtype))
        return out

    def _L0_ffn_ref(x, router_w, router_b, W1, b1, W2, b2):
        import jax, jax.numpy as jnp
        import numpy as np
        D_MODEL = 256
        D_FF = 1024
        N_EXPERTS = 8
        TOP_K = 2
        D_FF_PER = D_FF // N_EXPERTS
        B, T = (4, 512)
        router_logits = x @ router_w + router_b
        routing_weights = jax.nn.softmax(router_logits, axis=-1)
        top_k_weights, top_k_indices = jax.lax.top_k(routing_weights, TOP_K)
        top_k_weights = top_k_weights / jnp.sum(top_k_weights, axis=-1, keepdims=True)
        routing_mask = jnp.zeros_like(routing_weights)
        routing_mask = jnp.take_along_axis(routing_mask, top_k_indices, axis=-1)
        b_idx = jnp.arange(x.shape[0])[:, None, None]
        t_idx = jnp.arange(x.shape[1])[None, :, None]
        routing_mask = jnp.zeros_like(routing_weights).at[b_idx, t_idx, top_k_indices].set(top_k_weights)
        h1 = jnp.einsum('btd,nde->btne', x, W1) + b1
        h1 = jax.nn.gelu(h1, approximate=False)
        out_per_expert = jnp.einsum('btne,nef->btnf', h1, W2) + b2
        output = jnp.sum(out_per_expert * routing_mask[..., None], axis=-2)
        return output

    def _L1_cond_ref(x, mask, conditioning, Wq, Wk, Wv, Wo, rms_scale, Wc, bc):
        import jax, jax.numpy as jnp
        import numpy as np
        EPS = 1e-06
        B, S, E = x.shape
        H = 16
        D = E // H
        scale = D ** (-0.5)

        def proj(W):
            return (x @ W.T).reshape(B, S, H, D).transpose(0, 2, 1, 3)
        q, k, v = (proj(Wq), proj(Wk), proj(Wv))
        scores = jnp.einsum('bhsd,bhtd->bhst', q, k) * scale
        scores = jnp.where(mask[None, None, :, :], -jnp.inf, scores)
        attn = jax.nn.softmax(scores, axis=-1)
        out = jnp.einsum('bhst,bhtd->bhsd', attn, v)
        out = out.transpose(0, 2, 1, 3).reshape(B, S, E)
        out = out @ Wo.T
        rms = jnp.sqrt(jnp.mean(out * out, axis=-1, keepdims=True) + EPS)
        xn = out / rms * rms_scale
        mod = jax.nn.silu(conditioning) @ Wc.T + bc
        shift, sc = jnp.split(mod, 2, axis=-1)
        xn = xn * (1.0 + sc[:, None, :]) + shift[:, None, :]
        return xn

    def _L1_ffn_ref(x, clip_x, clip_down, w_gate, w_up, w_down):
        import jax, jax.numpy as jnp
        import numpy as np
        QMAX = 127.0

        def _ste_round(v):
            return v + jax.lax.stop_gradient(jnp.round(v) - v)

        def _act_fake_quant(x, clip_factor):
            scale = jax.nn.sigmoid(clip_factor) * jnp.max(jnp.abs(x)) / QMAX
            return jnp.clip(_ste_round(x / scale), -QMAX - 1.0, QMAX) * scale

        def _weight_fake_quant(w):
            scale = jnp.max(jnp.abs(w), axis=1, keepdims=True) / QMAX
            return jnp.clip(_ste_round(w / scale), -QMAX - 1.0, QMAX) * scale
        xq = _act_fake_quant(x, clip_x[0])
        gate = jnp.einsum('bsh,ih->bsi', xq, _weight_fake_quant(w_gate))
        up = jnp.einsum('bsh,ih->bsi', xq, _weight_fake_quant(w_up))
        h = _act_fake_quant(jax.nn.silu(gate) * up, clip_down[0])
        return jnp.einsum('bsi,hi->bsh', h, _weight_fake_quant(w_down))
    x = x + _L0_ffn_ref(_L0_cond_ref(x, cond_256, cond_64, L0_cond_input_basis, L0_cond_mode_to_rank, L0_cond_output_basis), L0_ffn_router_w, L0_ffn_router_b, L0_ffn_W1, L0_ffn_b1, L0_ffn_W2, L0_ffn_b2)
    x = x + _L1_ffn_ref(_L1_cond_ref(x, mask_SxS_bk1, cond_256, L1_cond_Wq, L1_cond_Wk, L1_cond_Wv, L1_cond_Wo, L1_cond_rms_scale, L1_cond_Wc, L1_cond_bc), L1_ffn_clip_x, L1_ffn_clip_down, L1_ffn_w_gate, L1_ffn_w_up, L1_ffn_w_down)
    return x

_drawn_inputs = setup_inputs


def setup_inputs(seed=0):
    import zlib

    import numpy as np

    out = dict(_drawn_inputs(seed))
    spreads = {'L1_cond_rms_scale': (1.0, 0.6)}
    factors = {'L0_ffn_W1': 2.977,
     'L0_ffn_b1': 7.865,
     'L0_ffn_W2': 2.763,
     'L1_cond_Wq': 2.702,
     'L1_cond_Wk': 2.685,
     'L1_cond_Wc': 8.0,
     'L1_cond_bc': 22.478}
    for name, (base, spread) in spreads.items():
        noise = np.random.default_rng([zlib.crc32(name.encode()), seed]).standard_normal(out[name].shape)
        drawn = base * np.exp(spread * noise) if base else spread * noise
        out[name] = jnp.asarray(drawn.astype(out[name].dtype))
    for name, factor in factors.items():
        out[name] = (out[name] * factor).astype(out[name].dtype)
    return out
```

```python
from contextlib import ExitStack

import concourse.bass as bass
from concourse import mybir

F32 = mybir.dt.float32
F32R = mybir.dt.float32r
BF16 = mybir.dt.bfloat16
U8 = mybir.dt.uint8
ALU = mybir.AluOpType
ACT = mybir.ActivationFunctionType
AX_X = mybir.AxisListType.X
RMAX = bass.bass_isa.ReduceOp.max
RADD = bass.bass_isa.ReduceOp.add

P = 128
D = 256
KT = D // P
BATCH = 64
SEQ = 64
TOK = BATCH * SEQ
CH = 512
CHUNKS = TOK // CH
CB = CH // SEQ
TILES = CH // P
R = 64
NE = 8
HEADS = 16
DH = D // HEADS
HH = HEADS // KT
HP = HH // 2
PAIRS = BATCH // 2
FF = 704
MT = -(-FF // P)
TAIL = FF - (MT - 1) * P
EPS_GRAM = 1e-4
EPS_RMS = 1e-6
SCALE = DH ** -0.5
QMAX = 127.0
MAGIC = 12582912.0
MASKED = -2.0 ** 127


class Order:

    def __init__(self, engine, sem, base=0):
        self.engine, self.sem, self.base, self.n = engine, sem, base, 0

    def add(self, instruction):
        self.n += 1
        instruction.then_inc(self.sem, 1)
        return self.n

    def wait(self, n=None):
        self.engine.wait_ge(self.sem, self.base + (self.n if n is None else n))

    def link(self, instruction):
        self.add(instruction)
        self.wait()


def need(engine, sem, value):
    if not isinstance(value, int) or value > 0:
        engine.wait_ge(sem, value)


def bcast_mid(ap, n):
    return ap.unsqueeze(1).to_broadcast([ap.shape[0], n, ap.shape[1]])


def bcast_last(ap, n):
    return ap.unsqueeze(2).to_broadcast([ap.shape[0], ap.shape[1], n])


class Memory:

    def __init__(self, nc, scope, prefix):
        self.nc, self.scope, self.prefix = nc, scope, prefix

    def sb(self, name, shape, dt=F32):
        return self.scope.enter_context(self.nc.sbuf_tensor(self.prefix + name, shape, dt))

    def banks(self, n):
        return [self.scope.enter_context(self.nc.psum_tensor(f"{self.prefix}bank{i}", [P, CH], F32)) for i in range(n)]

    def sem(self, name):
        return self.scope.enter_context(self.nc.semaphore(self.prefix + name))


def prepare(nc, w, io):
    with ExitStack() as scope:
        s = Memory(nc, scope, "prep_")
        bank = s.banks(8)
        raw, raw_t = s.sb("raw", [R, R]), s.sb("raw_t", [R, R])
        elim = s.sb("elim", [R, 2 * R])
        col = s.sb("col", [R, 8])
        q_t = s.sb("q_t", [R, 2, R])
        inv_t = s.sb("inv_t", [R, R])
        scratch = s.sb("scratch", [R, R])
        ib_t = s.sb("ib_t", [P, KT, 2, R])
        ob_t = s.sb("ob_t", [P, KT, 2, R])
        proj = s.sb("proj", [P, CH])
        b2_pad = s.sb("b2_pad", [P, D])
        cond = s.sb("cond", [R, BATCH])
        wc_t = s.sb("wc_t", [R, 4, P])
        bc = s.sb("bc", [P, 4])
        rms_w = s.sb("rms_w", [P, KT])
        mask8 = s.sb("mask8", [P, SEQ], U8)
        maskf = s.sb("maskf", [P, SEQ])
        count = s.sb("count", [P, 2])
        w1 = w["big"][:, 9216:9216 + KT * NE * P].rearrange("p (k n) -> p k n", k=KT)
        select = w["big"][:, 11264:11264 + NE * P]
        rw = w["big"][:, 12288:12288 + KT * P].rearrange("p (k n) -> p k n", k=KT)
        rows_gu = w["big"][:, 0:2 * MT * D].rearrange("p (m h) -> p m h", h=D)
        rows_d = w["big"][:, 4096:4096 + KT * FF].rearrange("p (m h) -> p m h", h=FF)
        int_gu = w["big"][:, 6144:6144 + MT * D].bitcast(BF16).rearrange("p (m h) -> p m h", h=D)
        int_d = w["big"][:, 8192:8192 + MT * P].bitcast(BF16).rearrange("p (m i) -> p m i", m=KT)
        absmax = s.sb("absmax", [P, 2 * MT + KT])
        inv = s.sb("inv", [P, 2 * MT + KT])

        ld_chol, ld_const, ld_proj, ld_fold = s.sem("ld_chol"), s.sem("ld_const"), s.sem("ld_proj"), s.sem("ld_fold")
        ld_raw_t, ld_b2 = s.sem("ld_raw_t"), s.sem("ld_b2")
        ld_mod, ld_ffn, ld_late = s.sem("ld_mod"), s.sem("ld_ffn"), s.sem("ld_late")
        ld_x = [s.sem(f"ld_x{c}") for c in range(CHUNKS)]
        pads_set, b2_set = s.sem("pads_set"), s.sem("b2_set")
        dve = s.sem("dve")
        gram_ready, row_ready, row_used = s.sem("gram_ready"), s.sem("row_ready"), s.sem("row_used")
        proj_ready, proj_scaled, proj_high, proj_low = (s.sem(n) for n in ("proj_ready", "proj_scaled", "proj_high", "proj_low"))
        fold_ready, fold_high, fold_used = s.sem("fold_ready"), s.sem("fold_high"), s.sem("fold_used")
        silu_ready, mod_ready = s.sem("silu_ready"), s.sem("mod_ready")
        inv_ready, shifted, ints_ready, turned, turned_used = (
            s.sem(n) for n in ("inv_ready", "shifted", "ints_ready", "turned", "turned_used"))
        chol_done, root_ready, m_turned, m_copied, q_ready, q_signed, q_turned = (
            s.sem(n) for n in ("chol_done", "root_ready", "m_turned", "m_copied", "q_ready", "q_signed", "q_turned"))
        ident = w["ident"]

        with nc.Block() as block:

            @block.sync
            def _(sp):
                sp.dma_start(raw[:, :], io["raw"]).then_inc(ld_chol, 16)
                sp.dma_start(ident[:, :], io["ident"]).then_inc(ld_chol, 16)
                sp.dma_start(w["below"][:, :], io["below"]).then_inc(ld_chol, 16)
                sp.dma_start(raw_t[:, :], io["raw_t"]).then_inc(ld_raw_t, 16)
                for i in range(2):
                    half = slice(i * R, (i + 1) * R)
                    sp.dma_start(ib_t[:, :, i, :], io["ib_t"]).then_inc(ld_proj, 16)
                    sp.dma_start(w["spec"][half, :], io["cond_t"]).then_inc(ld_proj, 16)
                for c in range(CHUNKS):
                    sp.dma_start(w["x"][:, :, c * CH:(c + 1) * CH], io["x"][c]).then_inc(ld_x[c], 16)
                sp.dma_start(w["wq"][:, :, :], io["wq"]).then_inc(ld_late, 16)
                sp.dma_start(w["wk"][:, :, :], io["wk"]).then_inc(ld_late, 16)
                sp.dma_start(w["wv"][:, :, :], io["wv"]).then_inc(ld_late, 16)
                sp.dma_start(w["wo"][:, :, :], io["wo"]).then_inc(ld_late, 16)
                sp.dma_start(w["w2"][:, :, :], io["w2"]).then_inc(ld_late, 16)
                sp.wait_ge(ld_late, 16 * 5)

            @block.gpsimd
            def _(pool):
                nc.gpsimd.memset(b2_pad[:, :], 0.0).then_inc(b2_set, 1)
                nc.gpsimd.memset(w["rb"][:, :], 0.0).then_inc(pads_set, 1)
                nc.gpsimd.memset(rw[:, :, :], 0.0).then_inc(pads_set, 1)
                nc.gpsimd.memset(rows_gu[:, MT - 1, :], 1.0).then_inc(pads_set, 1)
                nc.gpsimd.memset(rows_gu[:, 2 * MT - 1, :], 1.0).then_inc(pads_set, 1)
                nc.gpsimd.memset(int_d[:, :, FF:MT * P], 0.0).then_inc(pads_set, 1)
                nc.gpsimd.memset(w["magic"][:, :], MAGIC).then_inc(pads_set, 1)
                nc.gpsimd.memset(w["mask_pad"][:, :, :, :], 0.0).then_inc(pads_set, 1)
                pool.wait_ge(b2_set, 1)
                for g in range(4):
                    pool.dma_start(b2_pad[32 * g:32 * g + NE, :], io["b2"]).then_inc(ld_b2, 16)

            @block.scalar
            def _(act):
                act.wait_ge(pads_set, 7)
                for i in range(2):
                    half = slice(i * R, (i + 1) * R)
                    act.dma_start(w["rank"][half, :], io["rank_t"]).then_inc(ld_const, 16)
                    act.dma_start(ob_t[:, :, i, :], io["ob_t"]).then_inc(ld_fold, 16)
                act.dma_start(rw[:, :, 0:NE], io["rw"]).then_inc(ld_fold, 16)
                act.dma_start(w1[:, :, :], io["w1"]).then_inc(ld_fold, 16)
                act.dma_start(select, io["select"]).then_inc(ld_const, 16)
                act.dma_start(w["rb"][0:NE, :], io["rb"]).then_inc(ld_const, 16)
                act.dma_start(w["b1"][:, :], io["b1"]).then_inc(ld_const, 16)
                act.dma_start(w["heads"][:, :], io["heads"]).then_inc(ld_const, 16)
                act.dma_start(w["prio"][:, :], io["prio"]).then_inc(ld_const, 16)
                act.dma_start(cond[:, :], io["cond_t"]).then_inc(ld_mod, 16)
                act.dma_start(wc_t[:, :, :], io["wc_t"]).then_inc(ld_mod, 16)
                act.dma_start(bc[:, :], io["bc"]).then_inc(ld_mod, 16)
                act.dma_start(rms_w[:, :], io["rms_w"]).then_inc(ld_mod, 16)
                act.dma_start(w["clips"][:, :], io["clips"].partition_broadcast(P)).then_inc(ld_mod, 16)
                act.dma_start(rows_gu[:, 0:MT - 1, :], io["gate"]).then_inc(ld_ffn, 16)
                act.dma_start(rows_gu[0:TAIL, MT - 1, :], io["gate_tail"]).then_inc(ld_ffn, 16)
                act.dma_start(rows_gu[:, MT:2 * MT - 1, :], io["up"]).then_inc(ld_ffn, 16)
                act.dma_start(rows_gu[0:TAIL, 2 * MT - 1, :], io["up_tail"]).then_inc(ld_ffn, 16)
                act.dma_start(rows_d, io["down"]).then_inc(ld_ffn, 16)
                for i in range(2):
                    act.dma_start(mask8[i * SEQ:(i + 1) * SEQ, :], io["mask"]).then_inc(ld_ffn, 16)

                def project(c):
                    act.wait_ge(proj_scaled, c + 1)
                    nc.scalar.activation(w["hid"][:, c * CH:(c + 1) * CH], proj[:, :], ACT.Copy).then_inc(proj_high, 1)

                def fold(i):
                    act.wait_ge(fold_ready, i + 1)
                    n = P if i == 0 else CH
                    high = w["rw_high"][:, :] if i == 0 else w["w1_high"][:, (i - 1) * CH:i * CH]
                    nc.scalar.activation(high, bank[2 + i][:, 0:n], ACT.Copy).then_inc(fold_high, 1)

                for i in range(3):
                    project(i)
                    fold(i)
                act.wait_ge(ld_mod, 16 * 5)
                nc.scalar.activation(cond[:, :], cond[:, :], ACT.Silu).then_inc(silu_ready, 1)
                nc.scalar.activation(w["clips"][:, :], w["clips"][:, :], ACT.Sigmoid).then_inc(silu_ready, 1)
                project(3)
                act.wait_ge(inv_ready, 1)
                for i in range(2 * MT):
                    if i == MT:
                        project(4)
                    nc.scalar.activation(rows_gu[:, i, :], rows_gu[:, i, :], ACT.Identity,
                                         scale=inv[:, i:i + 1], bias=w["magic"][:, 0:1]).then_inc(shifted, 1)
                for i in range(KT):
                    k = 2 * MT + i
                    nc.scalar.activation(rows_d[:, i, :], rows_d[:, i, :], ACT.Identity,
                                         scale=inv[:, k:k + 1], bias=w["magic"][:, 0:1]).then_inc(shifted, 1)

                def turned_copy(i):
                    act.wait_ge(turned, i + 1)
                    n = 1024 if i < 4 else 512
                    dst = w["gu_t"][:, i * 1024:i * 1024 + n] if i < 3 else w["down_t"][:, (i - 3) * 1024:(i - 3) * 1024 + n]
                    nc.scalar.activation(dst, bank[5 + i % 2][:, 0:n // 2].bitcast(BF16), ACT.Copy).then_inc(turned_used, 1)

                project(5)
                turned_copy(0)
                project(6)
                turned_copy(1)
                turned_copy(2)
                project(7)
                turned_copy(3)
                turned_copy(4)
                act.wait_ge(chol_done, 1)
                nc.scalar.activation(col[:, 4:5], col[:, 3:4], ACT.Sqrt).then_inc(root_ready, 1)

            @block.tensor
            def _(pe):
                def project(c):
                    pe.wait_ge(ld_x[c], 16)
                    if c == 0:
                        pe.wait_ge(ld_proj, 16 * 4)
                    else:
                        pe.wait_ge(proj_scaled, c)
                    for k in range(KT):
                        last = nc.tensor.matmul(bank[1][:, :], ib_t[:, k, :, :].rearrange("p a r -> p (a r)"),
                                                w["x"][:, k, c * CH:(c + 1) * CH], start=k == 0, stop=k == KT - 1)
                    last.then_inc(proj_ready, 1)

                def fold(i):
                    if i == 0:
                        pe.wait_ge(ld_fold, 16 * 4)
                    for k in range(KT):
                        rhs = rw[:, k, :] if i == 0 else w1[:, k, (i - 1) * CH:i * CH]
                        n = P if i == 0 else CH
                        last = nc.tensor.matmul(bank[2 + i][:, 0:n], ob_t[:, k, :, :].rearrange("p a r -> p (a r)"), rhs,
                                                start=k == 0, stop=k == KT - 1)
                    last.then_inc(fold_ready, 1)

                def modulation():
                    pe.wait_ge(silu_ready, 1)
                    for i in range(4):
                        last = nc.tensor.matmul(bank[7][:, i * BATCH:(i + 1) * BATCH], wc_t[:, i, :], cond[:, :],
                                                start=True, stop=True)
                    last.then_inc(mod_ready, 1)

                def turn(i):
                    pe.wait_ge(ints_ready, 1 if i < 3 else 2)
                    if i >= 2:
                        pe.wait_ge(turned_used, i - 1)
                    out = bank[5 + i % 2][:, :].bitcast(BF16)
                    for b in range(8 if i < 4 else 4):
                        n = 8 * i + b
                        if i < 3:
                            src = int_gu[:, n % (2 * MT), (n // (2 * MT)) * P:(n // (2 * MT) + 1) * P]
                        else:
                            n -= 24
                            src = int_d[:, n % KT, (n // KT) * P:(n // KT + 1) * P]
                        last = nc.tensor.transpose(out[:, b * P:(b + 1) * P], src, w["ident_b"][:, :])
                    last.then_inc(turned, 1)

                pe.wait_ge(ld_chol, 16 * 3)
                nc.tensor.matmul(bank[0][0:R, 0:R], raw[:, :], raw[:, :], start=True, stop=True).then_inc(gram_ready, 1)
                for j in range(R):
                    pe.wait_ge(row_used, j + 1)
                    nc.tensor.matmul(bank[0][0:R, 0:R + 1], ident[0:R, j:j + 1].to_broadcast([R, R]),
                                     elim[:, j:j + R + 1], start=True, stop=True).then_inc(row_ready, 1)
                    if j % 8 == 0:
                        project(j // 8)
                    if j % 8 == 4 and j < 24:
                        fold(j // 8)
                    if j == 28:
                        modulation()
                    if j % 4 == 2 and j >= 46:
                        turn((j - 46) // 4)
                pe.wait_ge(m_copied, 1)
                nc.tensor.transpose(bank[0][0:R, 0:R], elim[:, R:2 * R], ident[0:R, 0:R]).then_inc(m_turned, 1)
                pe.wait_ge(m_copied, 2)
                nc.tensor.matmul(bank[1][0:R, 0:R], inv_t[:, :], raw_t[:, :], start=True, stop=True).then_inc(q_ready, 1)
                pe.wait_ge(q_signed, 1)
                nc.tensor.transpose(bank[2][:, 0:R], q_t[:, :, :].rearrange("p a r -> p (a r)"),
                                    ident[0:R, 0:R]).then_inc(q_turned, 1)

            @block.vector
            def _(v):
                me = Order(v, dve)

                def scale(c):
                    v.wait_ge(proj_ready, c + 1)
                    if c:
                        v.wait_ge(proj_low, c)
                    nc.vector.tensor_tensor(proj[:, :].rearrange("p (b t) -> p b t", t=SEQ),
                                            bank[1][:, :].rearrange("p (b t) -> p b t", t=SEQ),
                                            bcast_last(w["spec"][:, c * CB:(c + 1) * CB], SEQ),
                                            ALU.mult).then_inc(proj_scaled, 1)

                def low(c):
                    v.wait_ge(proj_high, c + 1)
                    part = w["hid"][R:P, c * CH:(c + 1) * CH]
                    nc.vector.tensor_tensor(part, proj[R:P, :], part.bitcast(F32), ALU.subtract).then_inc(proj_low, 1)

                def fold_low(i):
                    v.wait_ge(fold_high, i + 1)
                    n = P if i == 0 else CH
                    high = w["rw_high"][:, :] if i == 0 else w["w1_high"][:, (i - 1) * CH:i * CH]
                    out = w["rw_low"][:, :] if i == 0 else w["w1_low"][:, (i - 1) * CH:i * CH]
                    me.add(nc.vector.tensor_tensor(out, bank[2 + i][:, 0:n], high.bitcast(F32), ALU.subtract))

                def modulation():
                    v.wait_ge(mod_ready, 1)
                    for i in range(KT):
                        nc.vector.tensor_scalar(w["shift"][:, i, :], bank[7][:, i * BATCH:(i + 1) * BATCH], bc[:, i:i + 1],
                                                None, ALU.add)
                        me.link(nc.vector.tensor_scalar(w["gain"][:, i, :], bank[7][:, (KT + i) * BATCH:(KT + i + 1) * BATCH],
                                                        bc[:, KT + i:KT + i + 1], 1.0, ALU.add, ALU.add))
                        me.link(nc.vector.tensor_scalar(w["gain"][:, i, :], w["gain"][:, i, :], rms_w[:, i:i + 1], None,
                                                        ALU.mult))

                def masks():
                    me.link(nc.vector.tensor_copy(maskf[:, :], mask8[:, :]))
                    me.add(nc.vector.tensor_scalar(w["mask_neg"][:, :], maskf[:, :], MASKED, None, ALU.mult))
                    me.link(nc.vector.tensor_reduce(count[:, 0:1], maskf[:, :], AX_X, ALU.add))
                    me.link(nc.vector.tensor_scalar(count[:, 0:1], count[:, 0:1], -1.0, float(SEQ), ALU.mult, ALU.add))
                    me.link(nc.vector.reciprocal(count[:, 1:2], count[:, 0:1]))
                    me.link(nc.vector.tensor_scalar(w["no_key"][:, :], count[:, 1:2], 0.0, None, ALU.mult))

                def side(j):
                    if j % 8 == 2:
                        scale(j // 8)
                    if j % 8 == 5:
                        low(j // 8)
                    if j % 8 == 7 and j < 24:
                        fold_low(j // 8)
                    if j == 26:
                        v.wait_ge(ld_ffn, 16 * 7)
                        me.add(nc.vector.tensor_reduce(absmax[:, 0:2 * MT], rows_gu, AX_X, ALU.max,
                                                       apply_absolute_value=True))
                    if j == 27:
                        me.link(nc.vector.tensor_reduce(absmax[:, 2 * MT:], rows_d, AX_X, ALU.max,
                                                        apply_absolute_value=True))
                        me.link(nc.vector.tensor_scalar(w["row_scale"][:, :], absmax[:, :], 1.0 / QMAX, None, ALU.mult))
                        nc.vector.reciprocal(inv[:, :], w["row_scale"][:, :]).then_inc(inv_ready, 1)
                    if j == 31:
                        modulation()
                    if j == 32:
                        masks()
                    if j in (38, 39):
                        i = j - 38
                        v.wait_ge(shifted, MT * (i + 1))
                        part = rows_gu[:, MT * i:MT * (i + 1), :]
                        me.link(nc.vector.tensor_scalar(part, part, MAGIC + QMAX, MAGIC - QMAX - 1, ALU.min, ALU.max))
                        me.add(nc.vector.tensor_scalar(int_gu[:, MT * i:MT * (i + 1), :], part, MAGIC, None, ALU.subtract))
                    if j == 40:
                        v.wait_ge(shifted, 2 * MT + KT)
                        me.wait()
                        nc.vector.sem_inc(ints_ready, 1)
                        me.link(nc.vector.tensor_scalar(rows_d, rows_d, MAGIC + QMAX, MAGIC - QMAX - 1, ALU.min, ALU.max))
                        nc.vector.tensor_scalar(int_d[:, :, 0:FF], rows_d, MAGIC, None, ALU.subtract).then_inc(ints_ready, 1)

                v.wait_ge(ld_chol, 16 * 3)
                me.add(nc.vector.tensor_copy(w["ident_b"][:, :], ident[:, :]))
                me.add(nc.vector.tensor_copy(elim[:, R:2 * R], ident[0:R, 0:R]))
                v.wait_ge(gram_ready, 1)
                nc.vector.scalar_tensor_tensor(elim[:, 0:R], ident[0:R, 0:R], EPS_GRAM, bank[0][0:R, 0:R],
                                               ALU.mult, ALU.add).then_inc(row_used, 1)
                me.wait()
                for j in range(R):
                    v.wait_ge(row_ready, j + 1)
                    if j == 2:
                        v.wait_ge(ld_const, 16 * 7)
                        v.wait_ge(ld_b2, 16 * 4)
                        v.wait_ge(ld_raw_t, 16)
                        v.wait_ge(ld_proj, 16 * 4)
                        me.add(nc.vector.tensor_copy(w["select"][:, :, :].rearrange("p n m -> p (n m)"), select))
                    if j == 3:
                        me.add(nc.vector.tensor_copy(w["b2_high"][:, :], b2_pad[:, :]))
                    if j == 4:
                        me.wait()
                        for g in (1, 3):
                            q = slice(32 * g, 32 * g + 32)
                            me.add(nc.vector.tensor_tensor(w["b2_high"][q, :], b2_pad[q, :],
                                                           w["b2_high"][q, :].bitcast(F32), ALU.subtract))
                    me.link(nc.vector.reciprocal(col[:, 0:1], bank[0][0:R, 0:1]))
                    me.link(nc.vector.scalar_tensor_tensor(col[:, 1:2], elim[:, j:j + 1], col[:, 0:1],
                                                           w["below"][:, j:j + 1], ALU.mult, ALU.mult))
                    nc.vector.scalar_tensor_tensor(elim[:, j:j + R + 1], bank[0][0:R, 0:R + 1], col[:, 1:2],
                                                   elim[:, j:j + R + 1], ALU.mult, ALU.add).then_inc(row_used, 1)
                    side(j)
                    v.wait_ge(row_used, j + 2)
                me.link(nc.vector.tensor_tensor(scratch[:, :], elim[:, 0:R], ident[0:R, 0:R], ALU.mult))
                nc.vector.tensor_reduce(col[:, 3:4], scratch[:, :], AX_X, ALU.add).then_inc(chol_done, 1)
                nc.vector.sem_inc(m_copied, 1)
                v.wait_ge(m_turned, 1)
                nc.vector.tensor_copy(inv_t[:, :], bank[0][0:R, 0:R]).then_inc(m_copied, 1)
                v.wait_ge(root_ready, 1)
                me.link(nc.vector.reciprocal(col[:, 5:6], col[:, 4:5]))
                me.link(nc.vector.scalar_tensor_tensor(col[:, 6:7], col[:, 3:4], col[:, 5:6], col[:, 4:5], ALU.mult, ALU.add))
                me.link(nc.vector.tensor_scalar(col[:, 6:7], col[:, 6:7], 0.5, None, ALU.mult))
                me.link(nc.vector.reciprocal(col[:, 5:6], col[:, 6:7]))
                v.wait_ge(q_ready, 1)
                me.link(nc.vector.tensor_scalar(q_t[:, 0, :], bank[1][0:R, 0:R], col[:, 5:6], None, ALU.mult))
                me.link(nc.vector.tensor_tensor(scratch[:, :], q_t[:, 0, :], raw_t[:, :], ALU.mult))
                me.link(nc.vector.tensor_reduce(col[:, 7:8], scratch[:, :], AX_X, ALU.add))
                me.link(nc.vector.tensor_scalar(col[:, 7:8], col[:, 7:8], 0.0, 2.0, ALU.is_ge, ALU.mult))
                me.link(nc.vector.tensor_scalar(col[:, 7:8], col[:, 7:8], -1.0, None, ALU.add))
                me.link(nc.vector.tensor_scalar(q_t[:, 1, :], q_t[:, 0, :], col[:, 7:8], None, ALU.mult))
                nc.vector.tensor_copy(q_t[:, 0, :], q_t[:, 1, :]).then_inc(q_signed, 1)
                v.wait_ge(q_turned, 1)
                high = w["mix_high"][:, :].rearrange("p (a r) -> p a r", a=2)
                me.link(nc.vector.tensor_copy(high, bcast_mid(bank[2][:, 0:R], 2)))
                me.link(nc.vector.tensor_tensor(w["mix_low"][:, :].rearrange("p (a r) -> p a r", a=2),
                                                bcast_mid(bank[2][:, 0:R], 2), high.bitcast(F32), ALU.subtract))


def route(nc, w):
    with ExitStack() as scope:
        s = Memory(nc, scope, "route_")
        bank = s.banks(4)
        hid32 = s.sb("hid32", [P, CH])
        logit_t = s.sb("logit_t", [P, CH])
        n_t = CHUNKS * TILES
        logits = s.sb("logits", [P, n_t, NE])
        a, b, pick1, pick2 = (s.sb(n, [P, n_t, NE]) for n in ("a", "b", "pick1", "pick2"))
        max1, max2, top, wt1, wt2 = (s.sb(n, [P, n_t]) for n in ("max1", "max2", "top", "wt1", "wt2"))
        hid_ready, hid_scaled, hid_high, hid_low = (s.sem(n) for n in ("hid_ready", "hid_scaled", "hid_high", "hid_low"))
        logit_ready, logit_copied, turned, turned_used = (
            s.sem(n) for n in ("logit_ready", "logit_copied", "turned", "turned_used"))
        dve, gap_ready, exp_ready = s.sem("dve"), s.sem("gap_ready"), s.sem("exp_ready")

        with nc.Block() as block:

            @block.tensor
            def _(pe):
                def hidden(c, first):
                    if not first:
                        pe.wait_ge(hid_scaled, c)
                    rhs = w["hid"][:, bass.ds(c * CH, CH)]
                    nc.tensor.matmul(bank[0][:, :], w["mix_high"][:, :], rhs, start=True, stop=False)
                    nc.tensor.matmul(bank[0][:, :], w["mix_low"][:, :], rhs, start=False, stop=True).then_inc(hid_ready, 1)

                def logit(c, first):
                    pe.wait_ge(hid_low, c + 1)
                    if not first:
                        pe.wait_ge(logit_copied, c)
                    rhs = w["hid"][:, bass.ds(c * CH, CH)]
                    nc.tensor.matmul(bank[1][:, :], w["rw_high"][:, :], rhs, start=True, stop=False)
                    nc.tensor.matmul(bank[1][:, :], w["rw_low"][:, :], rhs, start=False, stop=True).then_inc(logit_ready, 1)

                def turn(c, first):
                    pe.wait_ge(logit_copied, c + 1)
                    if not first:
                        pe.wait_ge(turned_used, c)
                    for t in range(TILES):
                        last = nc.tensor.transpose(bank[2][:, t * P:(t + 1) * P], logit_t[:, t * P:(t + 1) * P],
                                                   w["ident"][:, :])
                    last.then_inc(turned, 1)

                hidden(0, True)
                hidden(1, False)
                logit(0, True)
                turn(0, True)
                with pe.Fori(2, CHUNKS) as c:
                    hidden(c, False)
                    logit(c - 1, False)
                    turn(c - 1, False)
                logit(CHUNKS - 1, False)
                turn(CHUNKS - 1, False)

            @block.scalar
            def _(act):
                def high(c):
                    act.wait_ge(hid_scaled, c + 1)
                    nc.scalar.activation(w["hid"][:, bass.ds(c * CH, CH)], hid32[:, :], ACT.Copy).then_inc(hid_high, 1)

                def logit(c, first):
                    act.wait_ge(logit_ready, c + 1)
                    if not first:
                        act.wait_ge(turned, c)
                    nc.scalar.activation(logit_t[:, :], bank[1][:, :], ACT.Identity, bias=w["rb"][:, 0:1]).then_inc(logit_copied, 1)

                high(0)
                high(1)
                logit(0, True)
                with act.Fori(2, CHUNKS) as c:
                    high(c)
                    logit(c - 1, False)
                logit(CHUNKS - 1, False)
                act.wait_ge(gap_ready, 1)
                nc.scalar.activation(wt2[:, :], top[:, :], ACT.Exp).then_inc(exp_ready, 1)

            @block.vector
            def _(v):
                def scale(c, first):
                    v.wait_ge(hid_ready, c + 1)
                    if not first:
                        v.wait_ge(hid_low, c)
                    nc.vector.tensor_tensor(hid32[:, :].rearrange("p (b t) -> p b t", t=SEQ),
                                            bank[0][:, :].rearrange("p (b t) -> p b t", t=SEQ),
                                            bcast_last(w["rank"][:, bass.ds(c * CB, CB)], SEQ), ALU.mult).then_inc(hid_scaled, 1)
                    v.wait_ge(hid_high, c + 1)
                    part = w["hid"][R:P, bass.ds(c * CH, CH)]
                    nc.vector.tensor_tensor(part, hid32[R:P, :], part.bitcast(F32), ALU.subtract).then_inc(hid_low, 1)

                def gather(c):
                    v.wait_ge(turned, c + 1)
                    nc.vector.tensor_copy(logits[:, bass.ds(c * TILES, TILES), :],
                                          bank[2][:, :].rearrange("p (t n) -> p t n", n=P)[:, :, 0:NE]).then_inc(turned_used, 1)

                scale(0, True)
                scale(1, False)
                gather(0)
                with v.Fori(2, CHUNKS) as c:
                    scale(c, False)
                    gather(c - 1)
                gather(CHUNKS - 1)

                me = Order(v, dve)
                v.wait_ge(turned_used, CHUNKS)
                prio = bcast_mid(w["prio"][:, :], n_t)

                def best(values, maximum, pick):
                    me.link(nc.vector.tensor_reduce(maximum[:, :], values[:, :, :], AX_X, ALU.max))
                    me.link(nc.vector.tensor_tensor(a[:, :, :], values[:, :, :], bcast_last(maximum[:, :], NE), ALU.is_equal))
                    me.link(nc.vector.tensor_tensor(a[:, :, :], a[:, :, :], prio, ALU.mult))
                    me.link(nc.vector.tensor_reduce(top[:, :], a[:, :, :], AX_X, ALU.max))
                    me.link(nc.vector.tensor_tensor(pick[:, :, :], a[:, :, :], bcast_last(top[:, :], NE), ALU.is_equal))

                best(logits, max1, pick1)
                me.link(nc.vector.scalar_tensor_tensor(b[:, :, :], pick1[:, :, :], -3.0e38, logits[:, :, :], ALU.mult, ALU.add))
                best(b, max2, pick2)
                me.link(nc.vector.tensor_tensor(top[:, :], max2[:, :], max1[:, :], ALU.subtract))
                nc.vector.sem_inc(gap_ready, 1)
                v.wait_ge(exp_ready, 1)
                me.link(nc.vector.tensor_scalar(wt1[:, :], wt2[:, :], 1.0, None, ALU.add))
                me.link(nc.vector.reciprocal(wt1[:, :], wt1[:, :]))
                me.link(nc.vector.tensor_tensor(wt2[:, :], wt2[:, :], wt1[:, :], ALU.mult))
                me.link(nc.vector.tensor_tensor(pick1[:, :, :], pick1[:, :, :], bcast_last(wt1[:, :], NE), ALU.mult))
                me.link(nc.vector.tensor_tensor(pick2[:, :, :], pick2[:, :, :], bcast_last(wt2[:, :], NE), ALU.mult))
                me.link(nc.vector.tensor_tensor(a[:, :, :], pick1[:, :, :], pick2[:, :, :], ALU.add))
                me.link(nc.vector.tensor_copy(w["gate_high"][:, :, :], a[:, :, :]))
                me.link(nc.vector.tensor_tensor(w["gate_low"][:, :, :], a[:, :, :], w["gate_high"][:, :, :].bitcast(F32), ALU.subtract))


def experts(nc, w):
    with ExitStack() as scope:
        s = Memory(nc, scope, "moe_")
        bank = s.banks(8)
        out_bank, h1_bank, gate_bank, qkv_bank = bank[0:2], bank[2:4], bank[4:6], bank[6:8]
        gate_t = s.sb("gate_t", [P, CH], F32R)
        act_h = s.sb("act_h", [P, 2, CH])
        gated = s.sb("gated", [P, 2, CH])
        x2 = s.sb("x2", [P, KT, CH])
        names = ("mask_ready", "mask_turned", "gate_copied", "h1_ready", "h1_used", "act_ready", "gate_ready",
                 "gated_ready", "gated_used", "out_ready", "x2_ready", "x2_kept", "qkv_ready", "qk_copied", "v_copied")
        (mask_ready, mask_turned, gate_copied, h1_ready, h1_used, act_ready, gate_ready,
         gated_ready, gated_used, out_ready, x2_ready, x2_kept, qkv_ready, qk_copied, v_copied) = (s.sem(n) for n in names)
        big = w["big"]
        q_all = big[:, 0:KT * TOK].rearrange("p (t k n) -> p t k n", t=PAIRS, k=KT)
        k_all = big[:, KT * TOK:2 * KT * TOK].rearrange("p (t k n) -> p t k n", t=PAIRS, k=KT)
        v_all = big[:, 2 * KT * TOK:3 * KT * TOK].rearrange("p (t b h d) -> p t b h d", t=PAIRS, b=2, d=DH)

        def main_loop(engine, body):
            body(0, True, True)
            body(1, False, True)
            with engine.Fori(2, CHUNKS) as c:
                body(c, False, True)
            body(CHUNKS, False, False)

        with nc.Block() as block:

            @block.tensor
            def _(pe):
                def h1(c, n):
                    need(pe, act_ready, c * NE + n - 1)
                    rhs = w["hid"][:, bass.ds(c * CH, CH)]
                    nc.tensor.matmul(h1_bank[n % 2][:, :], w["w1_high"][:, n * P:(n + 1) * P], rhs, start=True, stop=False)
                    nc.tensor.matmul(h1_bank[n % 2][:, :], w["w1_low"][:, n * P:(n + 1) * P], rhs,
                                     start=False, stop=True).then_inc(h1_ready, 1)

                def gate(c, n):
                    if n == 0:
                        pe.wait_ge(gate_copied, c + 1)
                    need(pe, gated_ready, c * NE + n - 1)
                    nc.tensor.matmul(gate_bank[n % 2][:, :], w["select"][:, n, :], gate_t[:, :],
                                     start=True, stop=True).then_inc(gate_ready, 1)

                def w2(c, n):
                    if n == 0:
                        need(pe, x2_ready, c * KT)
                    pe.wait_ge(gated_ready, c * NE + n + 1)
                    for f in range(KT):
                        last = nc.tensor.matmul(out_bank[f][:, :], w["w2"][:, n, f * P:(f + 1) * P], gated[:, n % 2, :],
                                                start=n == 0, stop=False, skip_group_check=True)
                    last.then_inc(gated_used, 1)

                def qkv(c, more):
                    pe.wait_ge(x2_ready, c * KT + KT)
                    for i in range(6):
                        if more and i == 0:
                            pe.wait_ge(gate_copied, c + 2)
                        elif i == 0:
                            need(pe, v_copied, c * 2 - 1)
                        if i == 1:
                            need(pe, v_copied, c * 2)
                        if 2 <= i:
                            pe.wait_ge(qk_copied, c * 4 + i - 1)
                        for k in range(KT):
                            if i < 4:
                                weight = (w["wq"], w["wk"])[i // 2]
                                last = nc.tensor.matmul(qkv_bank[i % 2][:, :], weight[:, k, (i % 2) * P:(i % 2 + 1) * P],
                                                        x2[:, k, :], start=k == 0, stop=k == KT - 1)
                        if i >= 4:
                            for t in range(2):
                                for k in range(KT):
                                    at = (2 * (i - 4) + t) * P
                                    last = nc.tensor.matmul(qkv_bank[i % 2][:, t * D:(t + 1) * D], x2[:, k, at:at + P],
                                                            w["wv"][:, k, :], start=k == 0, stop=k == KT - 1)
                        last.then_inc(qkv_ready, 1)

                def body(c, first, more):
                    if more:
                        pe.wait_ge(mask_ready, c + 1)
                        need(pe, v_copied, (c - 1) * 2)
                        for t in range(TILES):
                            last = nc.tensor.transpose(qkv_bank[0][:, t * P:(t + 1) * P],
                                                       w["mask_pad"][:, t, :, :].rearrange("p g n -> p (g n)"), w["ident"][:, :])
                        last.then_inc(mask_turned, 1)
                        h1(c, 0)
                        h1(c, 1)
                    if not first:
                        qkv(c - 1, more)
                    if more:
                        gate(c, 0)
                        gate(c, 1)
                        for n in range(NE):
                            w2(c, n)
                            if n + 2 < NE:
                                h1(c, n + 2)
                                gate(c, n + 2)
                        for f in range(KT):
                            last = nc.tensor.matmul(out_bank[f][:, :], w["b2_high"][:, f * P:(f + 1) * P], gate_t[:, :],
                                                    start=False, stop=True, skip_group_check=True)
                        last.then_inc(out_ready, 1)

                main_loop(pe, body)

            @block.scalar
            def _(act):
                def body(c, first, more):
                    if more:
                        act.wait_ge(mask_turned, c + 1)
                        need(act, out_ready, c)
                        nc.scalar.activation(gate_t[:, :], qkv_bank[0][:, :], ACT.Copy).then_inc(gate_copied, 1)
                        gelu(c, 0)
                        gelu(c, 1)
                    if not first:
                        for i in range(4):
                            act.wait_ge(qkv_ready, (c - 1) * 6 + i + 1)
                            dst = (q_all, k_all)[i // 2][:, bass.ds((c - 1) * TILES, TILES), i % 2, :]
                            nc.scalar.activation(dst, qkv_bank[i % 2][:, :].rearrange("p (t n) -> p t n", n=P),
                                                 ACT.Copy).then_inc(qk_copied, 1)
                    if more:
                        for n in range(2, NE):
                            gelu(c, n)

                def gelu(c, n):
                    act.wait_ge(h1_ready, c * NE + n + 1)
                    need(act, gated_ready, c * NE + n - 1)
                    nc.scalar.activation(act_h[:, n % 2, :], h1_bank[n % 2][:, :], ACT.Gelu,
                                         bias=w["b1"][:, n:n + 1]).then_inc(act_ready, 1)

                main_loop(act, body)

            @block.vector
            def _(v):
                def masks(c):
                    need(v, mask_turned, c)
                    for part, g in ((w["gate_high"], 0), (w["gate_low"], 2)):
                        src = part[:, bass.ds(c * TILES, TILES), :].bitcast(F32)
                        for i in range(2):
                            last = nc.vector.tensor_copy(w["mask_pad"][:, :, g + i, 0:NE], src)
                    last.then_inc(mask_ready, 1)

                def body(c, first, more):
                    if more:
                        masks(c)
                    if not first:
                        for i in range(2):
                            v.wait_ge(qkv_ready, (c - 1) * 6 + 5 + i)
                            src = qkv_bank[i % 2][:, :].rearrange("p (t h j d) -> p t h j d", t=2, j=2, d=DH)
                            for b in range(2):
                                for j in range(2):
                                    dst = v_all[j * SEQ:(j + 1) * SEQ, bass.ds((c - 1) * TILES + 2 * i, 2), b, :, :]
                                    last = nc.vector.tensor_copy(dst, src[b * SEQ:(b + 1) * SEQ, :, :, j, :])
                            last.then_inc(v_copied, 1)
                    if more:
                        for n in range(NE):
                            v.wait_ge(act_ready, c * NE + n + 1)
                            v.wait_ge(gate_ready, c * NE + n + 1)
                            need(v, gated_used, c * NE + n - 1)
                            nc.vector.tensor_tensor(gated[:, n % 2, :], act_h[:, n % 2, :], gate_bank[n % 2][:, :],
                                                    ALU.mult).then_inc(gated_ready, 1)
                        v.wait_ge(out_ready, c + 1)
                        if not first:
                            v.wait_ge(qkv_ready, c * 6)
                            v.wait_ge(x2_kept, c)
                        for f in range(KT):
                            nc.vector.tensor_tensor(x2[:, f, :], out_bank[f][:, :], w["x"][:, f, bass.ds(c * CH, CH)],
                                                    ALU.add).then_inc(x2_ready, 1)

                main_loop(v, body)

            @block.gpsimd
            def _(pool):
                with pool.Fori(0, CHUNKS) as c:
                    pool.wait_ge(x2_ready, c * KT + KT)
                    nc.gpsimd.tensor_copy(w["x"][:, :, bass.ds(c * CH, CH)], x2[:, :, :]).then_inc(x2_kept, 1)


def attention(nc, w):
    with ExitStack() as scope:
        s = Memory(nc, scope, "att_")
        bank = s.banks(8)
        score_bank, prob_bank, val_bank, proj_bank = bank[0:2], bank[2:4], bank[4:6], bank[6]
        q_s = s.sb("q_s", [P, KT, P])
        k_bd = s.sb("k_bd", [P, KT, 2, HH, SEQ])
        v_bd = s.sb("v_bd", [P, KT, 2, HP, 2, DH])
        neg_max = s.sb("neg_max", [P, KT, HH], BF16)
        probs = s.sb("probs", [P, KT, CH])
        sums = s.sb("sums", [P, KT, HH])
        inv = s.sb("inv", [P, KT, HH])
        normed = s.sb("normed", [P, KT, CH])
        probs_t = s.sb("probs_t", [P, KT, CH])
        heads_t = s.sb("heads_t", [P, KT, P])
        squares = s.sb("squares", [P, D])
        names = ("q_copied", "k_ready_v", "k_ready_g", "v_copied", "v_cleared", "score_ready", "max_ready", "shift_ready",
                 "exp_ready", "sum_ready", "inv_ready", "norm_ready", "turned", "turned_copied", "val_ready",
                 "heads_v", "heads_a", "out_ready", "out_copied", "squared")
        (q_copied, k_ready_v, k_ready_g, v_copied, v_cleared, score_ready, max_ready, shift_ready,
         exp_ready, sum_ready, inv_ready, norm_ready, turned, turned_copied, val_ready,
         heads_v, heads_a, out_ready, out_copied, squared) = (s.sem(n) for n in names)
        big = w["big"]
        q_all = big[:, 0:KT * TOK].rearrange("p (t k n) -> p t k n", t=PAIRS, k=KT)
        out_all = big[:, 0:KT * TOK].rearrange("p (t n) -> p t n", t=PAIRS)
        k_all = big[:, KT * TOK:2 * KT * TOK].rearrange("p (t k b n) -> p t k b n", t=PAIRS, k=KT, b=2)
        v_all = big[:, 2 * KT * TOK:3 * KT * TOK].rearrange("p (t b h d) -> p t b h d", t=PAIRS, b=2, d=DH)
        lag = 3

        def live(t):
            return not isinstance(t, int) or 0 <= t < PAIRS

        def every_pair(engine, step):
            for t in range(lag):
                step(t)
            with engine.Fori(lag, PAIRS - 1) as t:
                step(t)
            for t in range(PAIRS - 1, PAIRS + lag):
                step(t)

        def unit(t, h):
            return 2 * t + h + 1

        def k_of(t, h, b):
            return k_all[:, bass.ds(t, 1), h, b, :].rearrange("p a n -> p (a n)")

        def value_part(h, i):
            return val_bank[h][:, :].rearrange("p (b i q) -> p i b q", b=2, i=HP)[32 * i:32 * i + 32, i, :, :]

        def heads_part(h, i):
            return heads_t[32 * i:32 * i + 32, h, :].rearrange("p (b q) -> p b q", b=2)

        with nc.Block() as block:

            @block.tensor
            def _(pe):
                def scores(t, h):
                    pe.wait_ge(q_copied, unit(t, h))
                    pe.wait_ge(k_ready_v if h == 0 else k_ready_g, t + 1)
                    need(pe, exp_ready, unit(t - 1, h))
                    for b in range(2):
                        half = slice(b * SEQ, (b + 1) * SEQ)
                        nc.tensor.matmul(score_bank[h][half, :], q_s[:, h, half],
                                         k_bd[:, h, b, :, :].rearrange("p h n -> p (h n)"),
                                         start=True, stop=False, skip_group_check=True)
                    nc.tensor.matmul(score_bank[h][:, :], w["ident_b"][:, :], bcast_mid(w["mask_neg"][:, :], HH),
                                     start=False, stop=False, skip_group_check=True).then_inc(score_ready, 1)

                def shift(t, h):
                    pe.wait_ge(max_ready, unit(t, h))
                    nc.tensor.matmul(score_bank[h][:, :], w["ident_b"][:, :], bcast_last(neg_max[:, h, :], SEQ),
                                     start=False, stop=True, skip_group_check=True).then_inc(shift_ready, 1)

                def turn(t, h):
                    pe.wait_ge(norm_ready, unit(t, h))
                    need(pe, turned_copied, unit(t - 1, h))
                    for i in range(HP):
                        last = nc.tensor.transpose(prob_bank[h][:, i * P:(i + 1) * P], normed[:, h, i * P:(i + 1) * P],
                                                   w["ident"][:, :])
                    last.then_inc(turned, 1)

                def values(t, h):
                    pe.wait_ge(turned_copied, unit(t, h))
                    pe.wait_ge(v_copied, unit(t, h))
                    need(pe, heads_v, unit(t - 1, h))
                    need(pe, heads_a, unit(t - 1, h))
                    prob = probs_t[:, h, :].rearrange("p (i b q) -> p b i q", i=HP, b=2)
                    for b in range(2):
                        last = nc.tensor.matmul(val_bank[h][:, b * 256:(b + 1) * 256],
                                                v_bd[:, h, b, :, :, :].rearrange("p i j d -> p (i j d)"),
                                                prob[:, b, :, :], start=True, stop=True)
                    last.then_inc(val_ready, 1)

                def project(t):
                    pe.wait_ge(heads_v, unit(t, 1))
                    pe.wait_ge(heads_a, unit(t, 1))
                    need(pe, squared, t)
                    for h in range(KT):
                        last = nc.tensor.matmul(proj_bank[:, 0:D], heads_t[:, h, :], w["wo"][:, h, :],
                                                start=h == 0, stop=h == KT - 1)
                    last.then_inc(out_ready, 1)

                def step(t):
                    if live(t):
                        scores(t, 0)
                    if live(t - 3):
                        project(t - 3)
                    if live(t - 1):
                        shift(t - 1, 1)
                    if live(t - 2):
                        turn(t - 2, 1)
                        values(t - 2, 0)
                    if live(t):
                        scores(t, 1)
                        shift(t, 0)
                    if live(t - 1):
                        turn(t - 1, 0)
                    if live(t - 2):
                        values(t - 2, 1)

                every_pair(pe, step)

            @block.vector
            def _(v):
                def keys(t):
                    need(v, score_ready, unit(t - 1, 0))
                    for b in range(2):
                        last = nc.vector.tensor_tensor(k_bd[:, 0, b, :, :], bcast_mid(k_of(t, 0, b), HH),
                                                       bcast_last(w["heads"][:, :], SEQ), ALU.mult)
                    last.then_inc(k_ready_v, 1)

                def maximum(t, h):
                    v.wait_ge(score_ready, unit(t, h))
                    need(v, shift_ready, unit(t - 1, h))
                    nc.vector.tensor_reduce(neg_max[:, h, :], score_bank[h][:, :].rearrange("p (h n) -> p h n", n=SEQ),
                                            AX_X, ALU.max, negate=True).then_inc(max_ready, 1)

                def sum_up(t, h):
                    v.wait_ge(exp_ready, unit(t, h))
                    nc.vector.tensor_reduce(sums[:, h, :], probs[:, h, :].rearrange("p (h n) -> p h n", n=SEQ),
                                            AX_X, ALU.add).then_inc(sum_ready, 1)
                    v.wait_ge(sum_ready, unit(t, h))
                    need(v, norm_ready, unit(t - 1, h))
                    nc.vector.reciprocal(inv[:, h, :], sums[:, h, :]).then_inc(inv_ready, 1)

                def heads(t, h):
                    v.wait_ge(val_ready, unit(t, h))
                    need(v, out_ready, t)
                    for i in range(2):
                        last = nc.vector.tensor_copy(heads_part(h, i), value_part(h, i))
                    last.then_inc(heads_v, 1)

                def keep(t):
                    v.wait_ge(out_ready, t + 1)
                    v.wait_ge(q_copied, unit(t, 1))
                    nc.vector.tensor_copy(out_all[:, bass.ds(t, 1), :].rearrange("p a n -> p (a n)"),
                                          proj_bank[:, 0:D]).then_inc(out_copied, 1)

                def step(t):
                    if live(t):
                        maximum(t, 0)
                    if live(t + 1):
                        keys(t + 1)
                    if live(t - 1):
                        sum_up(t - 1, 1)
                    if live(t - 3):
                        keep(t - 3)
                    if live(t - 2):
                        heads(t - 2, 0)
                    if live(t):
                        maximum(t, 1)
                        sum_up(t, 0)
                    if live(t - 2):
                        heads(t - 2, 1)

                keys(0)
                every_pair(v, step)

            @block.gpsimd
            def _(pool):
                def keys(t):
                    need(pool, score_ready, unit(t - 1, 1))
                    for b in range(2):
                        last = nc.gpsimd.tensor_tensor(k_bd[:, 1, b, :, :], bcast_mid(k_of(t, 1, b), HH),
                                                       bcast_last(w["heads"][:, :], SEQ), ALU.mult)
                    last.then_inc(k_ready_g, 1)

                def normalise(t, h):
                    pool.wait_ge(inv_ready, unit(t, h))
                    need(pool, turned, unit(t - 1, h))
                    nc.gpsimd.tensor_tensor(normed[:, h, :].rearrange("p (h n) -> p h n", n=SEQ),
                                            probs[:, h, :].rearrange("p (h n) -> p h n", n=SEQ),
                                            bcast_last(inv[:, h, :], SEQ), ALU.mult).then_inc(norm_ready, 1)

                def step(t):
                    if live(t - 1):
                        normalise(t - 1, 1)
                    if live(t):
                        normalise(t, 0)
                    if live(t + 1):
                        keys(t + 1)

                keys(0)
                nc.gpsimd.memset(v_bd[:, :, :, :, :, :], 0.0).then_inc(v_cleared, 1)
                every_pair(pool, step)

            @block.scalar
            def _(act):
                def queries(t, h):
                    need(act, score_ready, unit(t - 1, h))
                    nc.scalar.activation(q_s[:, h, :], q_all[:, bass.ds(t, 1), h, :].rearrange("p a n -> p (a n)"),
                                         ACT.Copy).then_inc(q_copied, 1)

                def values(t, h):
                    need(act, val_ready, unit(t - 1, h))
                    for j in range(2):
                        half = slice(j * SEQ, (j + 1) * SEQ)
                        for b in range(2):
                            src = v_all[half, bass.ds(t, 1), b, h * HP:(h + 1) * HP, :].rearrange("p a i d -> p (a i) d")
                            last = nc.scalar.activation(v_bd[half, h, b, :, j, :], src, ACT.Copy)
                    last.then_inc(v_copied, 1)

                def exponent(t, h):
                    act.wait_ge(shift_ready, unit(t, h))
                    need(act, norm_ready, unit(t - 1, h))
                    nc.scalar.activation(probs[:, h, :], score_bank[h][:, :], ACT.Exp, scale=SCALE).then_inc(exp_ready, 1)

                def turned_copy(t, h):
                    act.wait_ge(turned, unit(t, h))
                    need(act, val_ready, unit(t - 1, h))
                    nc.scalar.activation(probs_t[:, h, :], prob_bank[h][:, :], ACT.Copy).then_inc(turned_copied, 1)

                def heads(t, h):
                    act.wait_ge(val_ready, unit(t, h))
                    need(act, out_ready, t)
                    for i in range(2, HP):
                        last = nc.scalar.activation(heads_part(h, i), value_part(h, i), ACT.Copy)
                    last.then_inc(heads_a, 1)

                def square(t):
                    act.wait_ge(out_copied, t + 1)
                    need(act, squared, t)
                    nc.scalar.activation(squares[:, :], proj_bank[:, 0:D], ACT.Square,
                                         accum_out=w["sq_sum"][:, bass.ds(t, 1)]).then_inc(squared, 1)

                def step(t):
                    if live(t - 1):
                        exponent(t - 1, 1)
                    if live(t + 1):
                        queries(t + 1, 0)
                    if live(t - 3):
                        square(t - 3)
                    if live(t - 2):
                        turned_copy(t - 2, 1)
                        heads(t - 2, 0)
                    if live(t - 1):
                        values(t - 1, 0)
                    if live(t):
                        exponent(t, 0)
                    if live(t + 1):
                        queries(t + 1, 1)
                    if live(t - 1):
                        turned_copy(t - 1, 0)
                    if live(t - 2):
                        heads(t - 2, 1)
                    if live(t - 1):
                        values(t - 1, 1)

                queries(0, 0)
                queries(0, 1)
                act.wait_ge(v_cleared, 1)
                every_pair(act, step)


def normalise(nc, w):
    with ExitStack() as scope:
        s = Memory(nc, scope, "norm_")
        bank = s.banks(4)
        ms, root, inv = s.sb("ms", [P, PAIRS]), s.sb("root", [P, PAIRS]), s.sb("inv", [P, PAIRS])
        scaled = s.sb("scaled", [P, 2, TILES, D])
        gained = s.sb("gained", [P, KT, CH])
        part_max = s.sb("part_max", [P, CHUNKS])
        top = s.sb("top", [P, 2])
        nan_sum = s.sb("nan_sum", [P, 1])
        names = ("dve", "ms_ready", "root_ready", "inv_ready", "scaled_ready", "turned", "gained_ready", "shifted",
                 "max_ready", "top_ready", "all_ready")
        (dve, ms_ready, root_ready, inv_ready, scaled_ready, turned, gained_ready, shifted,
         max_ready, top_ready, all_ready) = (s.sem(n) for n in names)
        big = w["big"]
        out_all = big[:, 0:KT * TOK].rearrange("p (t n) -> p t n", t=PAIRS)
        xn = big[:, 2 * KT * TOK:3 * KT * TOK].rearrange("p (c k n) -> p c k n", c=CHUNKS, k=KT)

        def chunks(engine, body):
            body(0, 0)
            body(1, 1)
            with engine.Fori(1, CHUNKS // 2) as i:
                body(2 * i, 0)
                body(2 * i + 1, 1)

        with nc.Block() as block:

            @block.scalar
            def _(act):
                act.wait_ge(ms_ready, 1)
                nc.scalar.activation(root[:, :], ms[:, :], ACT.Sqrt).then_inc(root_ready, 1)
                act.wait_ge(inv_ready, 1)

                def body(c, k):
                    need(act, turned, (c - 1) * KT)
                    for t in range(TILES):
                        at = c * TILES + t
                        last = nc.scalar.activation(scaled[:, k, t, :], out_all[:, bass.ds(at, 1), :].rearrange("p a n -> p (a n)"),
                                                    ACT.Copy, scale=inv[:, bass.ds(at, 1)])
                    last.then_inc(scaled_ready, 1)

                chunks(act, body)

            @block.tensor
            def _(pe):
                def body(c, k):
                    pe.wait_ge(scaled_ready, c + 1)
                    for f in range(KT):
                        need(pe, gained_ready, (c - 2) * KT + f + 1)
                        for t in range(TILES):
                            last = nc.tensor.transpose(bank[2 * k + f][:, t * P:(t + 1) * P], scaled[:, k, t, f * P:(f + 1) * P],
                                                       w["ident"][:, :])
                        last.then_inc(turned, 1)

                chunks(pe, body)

            @block.vector
            def _(v):
                me = Order(v, dve)
                nc.vector.tensor_scalar(ms[:, :], w["sq_sum"][:, :], 1.0 / D, EPS_RMS, ALU.mult, ALU.add).then_inc(ms_ready, 1)
                v.wait_ge(root_ready, 1)
                me.link(nc.vector.reciprocal(inv[:, :], root[:, :]))
                me.link(nc.vector.tensor_tensor(ms[:, :], ms[:, :], inv[:, :], ALU.mult))
                me.link(nc.vector.tensor_tensor(root[:, :], root[:, :], ms[:, :], ALU.add))
                me.link(nc.vector.tensor_scalar(root[:, :], root[:, :], 0.5, None, ALU.mult))
                me.link(nc.vector.reciprocal(inv[:, :], root[:, :]))
                nc.vector.tensor_scalar(inv[:, :], inv[:, :], w["no_key"][:, 0:1], None, ALU.add).then_inc(inv_ready, 1)

                def body(c, k):
                    for f in range(KT):
                        v.wait_ge(turned, c * KT + f + 1)
                        need(v, shifted, (c - 1) * KT + f + 1)
                        nc.vector.tensor_tensor(gained[:, f, :].rearrange("p (b t) -> p b t", t=SEQ),
                                                bank[2 * k + f][:, :].rearrange("p (b t) -> p b t", t=SEQ),
                                                bcast_last(w["gain"][:, f, bass.ds(c * CB, CB)], SEQ),
                                                ALU.mult).then_inc(gained_ready, 1)
                    v.wait_ge(shifted, (c + 1) * KT)
                    nc.vector.tensor_reduce(part_max[:, bass.ds(c, 1)], xn[:, bass.ds(c, 1), :, :].rearrange("p a k n -> p (a k n)"),
                                            AX_X, ALU.max, apply_absolute_value=True).then_inc(max_ready, 1)

                chunks(v, body)
                v.wait_ge(max_ready, CHUNKS)
                nc.vector.tensor_reduce(top[:, 0:1], part_max[:, :], AX_X, ALU.max).then_inc(top_ready, 1)
                v.wait_ge(all_ready, 2)
                me.link(nc.vector.tensor_tensor(top[:, 1:2], top[:, 1:2], nan_sum[:, :], ALU.add))
                quant_scale(nc, me, w, top[:, 1:2], 0)

            @block.gpsimd
            def _(pool):
                def body(c, k):
                    for f in range(KT):
                        pool.wait_ge(gained_ready, c * KT + f + 1)
                        nc.gpsimd.tensor_tensor(xn[:, bass.ds(c, 1), f, :].rearrange("p a (b t) -> p (a b) t", t=SEQ),
                                                gained[:, f, :].rearrange("p (b t) -> p b t", t=SEQ),
                                                bcast_last(w["shift"][:, f, bass.ds(c * CB, CB)], SEQ),
                                                ALU.add).then_inc(shifted, 1)

                chunks(pool, body)
                nc.gpsimd.partition_all_reduce(nan_sum[:, :], w["no_key"][:, :], P, RADD).then_inc(all_ready, 1)
                pool.wait_ge(top_ready, 1)
                nc.gpsimd.partition_all_reduce(top[:, 1:2], top[:, 0:1], P, RMAX).then_inc(all_ready, 1)


def quant_scale(nc, me, w, largest, which):
    scale, inv = w["quant"][:, 2 * which:2 * which + 1], w["quant"][:, 2 * which + 1:2 * which + 2]
    me.link(nc.vector.tensor_scalar(scale, largest, w["clips"][:, which:which + 1], 1.0 / QMAX, ALU.mult, ALU.mult))
    me.link(nc.vector.reciprocal(inv, scale))
    at = slice(0, 2 * MT) if which == 0 else slice(2 * MT, 2 * MT + KT)
    me.link(nc.vector.tensor_scalar(w["out_scale"][:, at], w["row_scale"][:, at], scale, None, ALU.mult))


def ffn_in(nc, w):
    with ExitStack() as scope:
        s = Memory(nc, scope, "ffi_")
        bank = s.banks(6)
        gate_bank, up_bank = bank[0:3], bank[3:6]
        shifted = s.sb("shifted", [P, KT, CH])
        xq = s.sb("xq", [P, 2, KT, CH], BF16)
        silu = s.sb("silu", [P, 3, CH])
        part_max = s.sb("part_max", [P, CHUNKS, MT])
        top = s.sb("top", [P, 2])
        names = ("magic_added", "clipped", "xq_ready", "gate_ready", "up_ready", "silu_ready",
                 "h_ready", "max_ready", "top_ready", "all_ready", "dve")
        (magic_added, clipped, xq_ready, gate_ready, up_ready, silu_ready,
         h_ready, max_ready, top_ready, all_ready, dve) = (s.sem(n) for n in names)
        big = w["big"]
        h_all = big[:, :].rearrange("p (c m n) -> p c m n", c=CHUNKS, m=MT)
        xn = big[:, 2 * KT * TOK:3 * KT * TOK].rearrange("p (c k n) -> p c k n", c=CHUNKS, k=KT)

        def rows(i):
            return P if i < MT - 1 else TAIL

        def live(c):
            return not isinstance(c, int) or c < CHUNKS

        def chunks(engine, body):
            body(0, 0)
            body(1, 1)
            with engine.Fori(1, CHUNKS // 2 - 1) as i:
                body(2 * i, 0)
                body(2 * i + 1, 1)
            body(CHUNKS - 2, 0)
            body(CHUNKS - 1, 1)

        with nc.Block() as block:

            @block.scalar
            def _(act):
                def quantise(c):
                    need(act, xq_ready, c)
                    nc.scalar.activation(shifted[:, :, :], xn[:, bass.ds(c, 1), :, :].rearrange("p a k n -> p (a k) n"),
                                         ACT.Identity, scale=w["quant"][:, 1:2], bias=w["magic"][:, 0:1]).then_inc(magic_added, 1)

                def body(c, k):
                    for i in range(MT):
                        act.wait_ge(gate_ready, c * MT + i + 1)
                        need(act, h_ready, c * MT + i - 2)
                        nc.scalar.activation(silu[0:rows(i), i % 3, :], gate_bank[i % 3][0:rows(i), :], ACT.Silu,
                                             scale=w["out_scale"][0:rows(i), i:i + 1]).then_inc(silu_ready, 1)
                        if i == 1 and live(c + 1):
                            quantise(c + 1)

                quantise(0)
                chunks(act, body)

            @block.tensor
            def _(pe):
                def body(c, k):
                    pe.wait_ge(xq_ready, c + 1)
                    for i in range(MT):
                        for side, out, ready, used in ((0, gate_bank, gate_ready, silu_ready), (1, up_bank, up_ready, h_ready)):
                            need(pe, used, c * MT + i - 2)
                            for f in range(KT):
                                at = (f * 2 * MT + side * MT + i) * P
                                last = nc.tensor.matmul(out[i % 3][0:rows(i), :], w["gu_t"][:, at:at + rows(i)],
                                                        xq[:, k, f, :], start=f == 0, stop=f == KT - 1)
                            last.then_inc(ready, 1)

                chunks(pe, body)

            @block.vector
            def _(v):
                def quantise(c, k):
                    v.wait_ge(magic_added, c + 1)
                    nc.vector.tensor_scalar(shifted[:, :, :], shifted[:, :, :], MAGIC + QMAX, MAGIC - QMAX - 1,
                                            ALU.min, ALU.max).then_inc(clipped, 1)
                    v.wait_ge(clipped, c + 1)
                    need(v, up_ready, (c - 1) * MT)
                    nc.vector.tensor_scalar(xq[:, k, :, :], shifted[:, :, :], MAGIC, None, ALU.subtract).then_inc(xq_ready, 1)

                def body(c, k):
                    for i in range(MT):
                        v.wait_ge(silu_ready, c * MT + i + 1)
                        v.wait_ge(up_ready, c * MT + i + 1)
                        h = h_all[0:rows(i), bass.ds(c, 1), i, :].rearrange("p a n -> p (a n)")
                        nc.vector.scalar_tensor_tensor(h, up_bank[i % 3][0:rows(i), :],
                                                       w["out_scale"][0:rows(i), MT + i:MT + i + 1], silu[0:rows(i), i % 3, :],
                                                       ALU.mult, ALU.mult).then_inc(h_ready, 1)
                        if i == 2 and live(c + 1):
                            quantise(c + 1, 1 - k)
                        v.wait_ge(h_ready, c * MT + i + 1)
                        nc.vector.tensor_reduce(part_max[0:rows(i), bass.ds(c, 1), i], h, AX_X, ALU.max,
                                                apply_absolute_value=True).then_inc(max_ready, 1)

                me = Order(v, dve)
                me.link(nc.vector.memset(part_max[:, :, :], 0.0))
                quantise(0, 0)
                chunks(v, body)
                v.wait_ge(max_ready, CHUNKS * MT)
                nc.vector.tensor_reduce(top[:, 0:1], part_max[:, :, :].rearrange("p c m -> p (c m)"), AX_X,
                                        ALU.max).then_inc(top_ready, 1)
                v.wait_ge(all_ready, 1)
                quant_scale(nc, me, w, top[:, 1:2], 1)

            @block.gpsimd
            def _(pool):
                pool.wait_ge(top_ready, 1)
                nc.gpsimd.partition_all_reduce(top[:, 1:2], top[:, 0:1], P, RMAX).then_inc(all_ready, 1)


def ffn_out(nc, w, out):
    with ExitStack() as scope:
        s = Memory(nc, scope, "ffo_")
        bank = s.banks(4)
        hq = s.sb("hq", [P, 2, MT, CH], BF16)
        y = s.sb("y", [P, 2, KT, CH])
        names = ("magic_added", "clipped", "hq_ready", "down_ready", "y_ready")
        magic_added, clipped, hq_ready, down_ready, y_ready = (s.sem(n) for n in names)
        stored = [s.sem("stored0"), s.sem("stored1")]
        h_all = w["big"][:, :].rearrange("p (c m n) -> p c m n", c=CHUNKS, m=MT)

        def h_of(c):
            return h_all[:, bass.ds(c, 1), :, :].rearrange("p a m n -> p (a m) n")

        def chunks(engine, body):
            body(0, 0, 0)
            body(1, 1, 0)
            with engine.Fori(1, CHUNKS // 2) as i:
                body(2 * i, 0, i)
                body(2 * i + 1, 1, i)

        with nc.Block() as block:

            @block.scalar
            def _(act):
                with act.Fori(0, CHUNKS) as c:
                    h = h_of(c)
                    nc.scalar.activation(h, h, ACT.Identity, scale=w["quant"][:, 3:4],
                                         bias=w["magic"][:, 0:1]).then_inc(magic_added, 1)

            @block.vector
            def _(v):
                def quantise(c, k):
                    v.wait_ge(magic_added, c + 1)
                    h = h_of(c)
                    nc.vector.tensor_scalar(h, h, MAGIC + QMAX, MAGIC - QMAX - 1, ALU.min, ALU.max).then_inc(clipped, 1)
                    v.wait_ge(clipped, c + 1)
                    need(v, down_ready, (c - 1) * KT)
                    nc.vector.tensor_scalar(hq[:, k, :, :], h, MAGIC, None, ALU.subtract).then_inc(hq_ready, 1)

                def finish(c, k, i):
                    need(v, stored[k], 16 * i)
                    for f in range(KT):
                        v.wait_ge(down_ready, c * KT + f + 1)
                        at = 2 * MT + f
                        nc.vector.scalar_tensor_tensor(y[:, k, f, :], bank[2 * k + f][:, :], w["out_scale"][:, at:at + 1],
                                                       w["x"][:, f, bass.ds(c * CH, CH)], ALU.mult, ALU.add).then_inc(y_ready, 1)

                quantise(0, 0)
                quantise(1, 1)
                finish(0, 0, 0)
                quantise(2, 0)
                finish(1, 1, 0)
                quantise(3, 1)
                finish(2, 0, 1)
                with v.Fori(2, CHUNKS // 2) as i:
                    quantise(2 * i, 0)
                    finish(2 * i - 1, 1, i - 1)
                    quantise(2 * i + 1, 1)
                    finish(2 * i, 0, i)
                finish(CHUNKS - 1, 1, CHUNKS // 2 - 1)

            @block.tensor
            def _(pe):
                def body(c, k, i):
                    pe.wait_ge(hq_ready, c + 1)
                    for f in range(KT):
                        need(pe, y_ready, (c - 2) * KT + f + 1)
                        for j in range(MT):
                            at = (j * KT + f) * P
                            last = nc.tensor.matmul(bank[2 * k + f][:, :], w["down_t"][:, at:at + P], hq[:, k, j, :],
                                                    start=j == 0, stop=j == MT - 1)
                        last.then_inc(down_ready, 1)

                chunks(pe, body)

            @block.sync
            def _(sp):
                def body(c, k, i):
                    sp.wait_ge(y_ready, (c + 1) * KT)
                    sp.dma_start(out[bass.ds(c, 1)].rearrange("a p k n -> p (a k) n"), y[:, k, :, :]).then_inc(stored[k], 16)

                chunks(sp, body)
                sp.wait_ge(stored[0], 16 * CHUNKS // 2)
                sp.wait_ge(stored[1], 16 * CHUNKS // 2)


def build(nc, io, out):
    with ExitStack() as whole:
        m = Memory(nc, whole, "")
        w = {
            "x": m.sb("x_all", [P, KT, TOK]),
            "big": m.sb("big", [P, CHUNKS * MT * CH]),
            "ident": m.sb("ident", [P, P]),
            "ident_b": m.sb("ident_b", [P, P], BF16),
            "magic": m.sb("magic", [P, 1]),
            "clips": m.sb("clips", [P, 2]),
            "quant": m.sb("quant", [P, 4]),
            "row_scale": m.sb("row_scale", [P, 2 * MT + KT]),
            "out_scale": m.sb("out_scale", [P, 2 * MT + KT]),
            "gain": m.sb("gain", [P, KT, BATCH]),
            "shift": m.sb("shift", [P, KT, BATCH]),
            "no_key": m.sb("no_key", [P, 1]),
            "mask_neg": m.sb("mask_neg", [P, SEQ], BF16),
            "heads": m.sb("heads", [P, HH]),
            "sq_sum": m.sb("sq_sum", [P, PAIRS]),
            "gu_t": m.sb("gu_t", [P, KT * 2 * MT * P], BF16),
            "down_t": m.sb("down_t", [P, MT * KT * P], BF16),
            "wo": m.sb("wo", [P, KT, D]),
        }
        with ExitStack() as first:
            f = Memory(nc, first, "")
            w |= {
                "hid": f.sb("hid", [P, TOK], F32R),
                "mix_high": f.sb("mix_high", [P, P], F32R),
                "mix_low": f.sb("mix_low", [P, P], F32R),
                "rw_high": f.sb("rw_high", [P, P], F32R),
                "rw_low": f.sb("rw_low", [P, P], F32R),
                "w1_high": f.sb("w1_high", [P, NE * P], F32R),
                "w1_low": f.sb("w1_low", [P, NE * P], F32R),
                "w2": f.sb("w2", [P, NE, D]),
                "b1": f.sb("b1", [P, NE]),
                "rb": f.sb("rb", [P, 1]),
                "b2_high": f.sb("b2_high", [P, D], F32R),
                "select": f.sb("select", [P, NE, P], F32R),
                "gate_high": f.sb("gate_high", [P, CHUNKS * TILES, NE], F32R),
                "gate_low": f.sb("gate_low", [P, CHUNKS * TILES, NE], F32R),
                "mask_pad": f.sb("mask_pad", [P, TILES, 4, 32]),
                "spec": f.sb("spec", [P, BATCH]),
                "rank": f.sb("rank", [P, BATCH]),
                "prio": f.sb("prio", [P, NE]),
                "below": f.sb("below", [R, R]),
                "wq": f.sb("wq", [P, KT, D]),
                "wk": f.sb("wk", [P, KT, D]),
                "wv": f.sb("wv", [P, KT, D]),
            }
            prepare(nc, w, io)
            route(nc, w)
            experts(nc, w)
        attention(nc, w)
        normalise(nc, w)
        ffn_in(nc, w)
        ffn_out(nc, w, out)


def kernel(**inputs):
    import numpy as np
    import concourse.bacc as bacc
    from concourse.bass_utils import run_bass_kernel_spmd

    a = {name: np.asarray(value) for name, value in inputs.items()}

    def tiles(x):
        return x.reshape(-1, P, x.shape[-1]).transpose(1, 0, 2)

    main = (MT - 1) * P
    gate, up = a["L1_ffn_w_gate"], a["L1_ffn_w_up"]
    row = np.arange(P)
    select = np.zeros((P, NE, P), np.float32)
    for n in range(NE):
        select[[n, 64 + n], n, :] = 1.0
    arrays = {
        "x": a["x"].reshape(CHUNKS, CH, KT, P).transpose(0, 3, 2, 1),
        "cond_t": a["cond_256"].T,
        "rank_t": a["cond_64"].T,
        "raw": a["L0_cond_mode_to_rank"],
        "raw_t": a["L0_cond_mode_to_rank"].T,
        "ib_t": tiles(a["L0_cond_input_basis"].T),
        "ob_t": tiles(a["L0_cond_output_basis"].T),
        "rw": tiles(a["L0_ffn_router_w"]),
        "rb": a["L0_ffn_router_b"].reshape(NE, 1),
        "w1": tiles(a["L0_ffn_W1"].transpose(1, 0, 2).reshape(D, NE * P)),
        "b1": a["L0_ffn_b1"].T,
        "w2": a["L0_ffn_W2"].transpose(1, 0, 2),
        "b2": a["L0_ffn_b2"],
        "wq": tiles(a["L1_cond_Wq"].T),
        "wk": tiles(a["L1_cond_Wk"].T),
        "wv": tiles(a["L1_cond_Wv"].T),
        "wo": tiles(a["L1_cond_Wo"].T),
        "wc_t": a["L1_cond_Wc"].T.reshape(R, 4, P),
        "bc": a["L1_cond_bc"].reshape(4, P).T,
        "rms_w": a["L1_cond_rms_scale"].reshape(KT, P).T,
        "mask": a["mask_SxS_bk1"],
        "clips": np.concatenate([a["L1_ffn_clip_x"], a["L1_ffn_clip_down"]]),
        "gate": tiles(gate[:main]),
        "gate_tail": gate[main:],
        "up": tiles(up[:main]),
        "up_tail": up[main:],
        "down": tiles(a["L1_ffn_w_down"]),
        "ident": np.eye(P, dtype=np.float32),
        "below": -np.tril(np.ones((R, R), np.float32), -1),
        "heads": (row[:, None] // DH == np.arange(HH)[None, :]).astype(np.float32),
        "prio": np.ascontiguousarray(np.broadcast_to(np.arange(NE, 0, -1, dtype=np.float32), (P, NE))),
        "select": select.reshape(P, NE * P),
    }
    nc = bacc.Bacc("TRN2", target_bir_lowering=False, num_devices=1)
    arrays = {f"in_{name}": np.ascontiguousarray(value) for name, value in arrays.items()}
    io = {name[3:]: nc.dram_tensor(name, v.shape, mybir.dt.from_np(v.dtype), kind="ExternalInput").ap()
          for name, v in arrays.items()}
    out = nc.dram_tensor("out", (CHUNKS, P, KT, CH), F32, kind="ExternalOutput").ap()
    build(nc, io, out)
    r = run_bass_kernel_spmd(nc, [arrays], core_ids=[0])
    y = r.results[0]["out"]
    return y.transpose(0, 3, 2, 1).reshape(BATCH, SEQ, D)
```

```python
from contextlib import ExitStack

import concourse.bass as bass
from concourse import mybir

F32 = mybir.dt.float32
F32R = mybir.dt.float32r
BF16 = mybir.dt.bfloat16
U8 = mybir.dt.uint8
ALU = mybir.AluOpType
ACT = mybir.ActivationFunctionType
AX_X = mybir.AxisListType.X
RMAX = bass.bass_isa.ReduceOp.max
RADD = bass.bass_isa.ReduceOp.add

P = 128
D = 256
KT = D // P
BATCH = 64
SEQ = 64
TOK = BATCH * SEQ
CH = 512
CHUNKS = TOK // CH
CB = CH // SEQ
TILES = CH // P
R = 64
NE = 8
HEADS = 16
DH = D // HEADS
HH = HEADS // KT
HP = HH // 2
PAIRS = BATCH // 2
FF = 704
MT = -(-FF // P)
TAIL = FF - (MT - 1) * P
EPS_GRAM = 1e-4
EPS_RMS = 1e-6
SCALE = DH ** -0.5
QMAX = 127.0
MAGIC = 12582912.0
MASKED = -2.0 ** 127


class Order:

    def __init__(self, engine, sem, base=0):
        self.engine, self.sem, self.base, self.n = engine, sem, base, 0

    def add(self, instruction):
        self.n += 1
        instruction.then_inc(self.sem, 1)
        return self.n

    def wait(self, n=None):
        self.engine.wait_ge(self.sem, self.base + (self.n if n is None else n))

    def link(self, instruction):
        self.add(instruction)
        self.wait()


def need(engine, sem, value):
    if not isinstance(value, int) or value > 0:
        engine.wait_ge(sem, value)


def bcast_mid(ap, n):
    return ap.unsqueeze(1).to_broadcast([ap.shape[0], n, ap.shape[1]])


def bcast_last(ap, n):
    return ap.unsqueeze(2).to_broadcast([ap.shape[0], ap.shape[1], n])


class Memory:

    def __init__(self, nc, scope, prefix):
        self.nc, self.scope, self.prefix = nc, scope, prefix

    def sb(self, name, shape, dt=F32):
        return self.scope.enter_context(self.nc.sbuf_tensor(self.prefix + name, shape, dt))

    def banks(self, n):
        return [self.scope.enter_context(self.nc.psum_tensor(f"{self.prefix}bank{i}", [P, CH], F32)) for i in range(n)]

    def sem(self, name):
        return self.scope.enter_context(self.nc.semaphore(self.prefix + name))


def prepare(nc, w, io):
    with ExitStack() as scope:
        s = Memory(nc, scope, "prep_")
        bank = s.banks(8)
        raw, raw_t = s.sb("raw", [R, R]), s.sb("raw_t", [R, R])
        elim = s.sb("elim", [R, 2 * R])
        col = s.sb("col", [R, 8])
        q_t = s.sb("q_t", [R, 2, R])
        inv_t = s.sb("inv_t", [R, R])
        scratch = s.sb("scratch", [R, R])
        ib_t = s.sb("ib_t", [P, KT, 2, R])
        ob_t = s.sb("ob_t", [P, KT, 2, R])
        proj = s.sb("proj", [P, CH])
        b2_pad = s.sb("b2_pad", [P, D])
        cond = s.sb("cond", [R, BATCH])
        wc_t = s.sb("wc_t", [R, 4, P])
        bc = s.sb("bc", [P, 4])
        rms_w = s.sb("rms_w", [P, KT])
        mask8 = s.sb("mask8", [P, SEQ], U8)
        maskf = s.sb("maskf", [P, SEQ])
        count = s.sb("count", [P, 2])
        w1 = w["big"][:, 9216:9216 + KT * NE * P].rearrange("p (k n) -> p k n", k=KT)
        select = s.sb("select", [P, NE])
        rw = w["big"][:, 12288:12288 + KT * P].rearrange("p (k n) -> p k n", k=KT)
        rows_gu = w["big"][:, 0:2 * MT * D].rearrange("p (m h) -> p m h", h=D)
        rows_d = w["big"][:, 4096:4096 + KT * FF].rearrange("p (m h) -> p m h", h=FF)
        int_gu = w["big"][:, 6144:6144 + MT * D].bitcast(BF16).rearrange("p (m h) -> p m h", h=D)
        int_d = w["big"][:, 8192:8192 + MT * P].bitcast(BF16).rearrange("p (m i) -> p m i", m=KT)
        w2_raw = w["big"][:, 16384:16384 + NE * D].rearrange("p (n d) -> p n d", n=NE)
        qkv_raw = w["big"][:, 18432:18432 + 3 * KT * D].rearrange("p (i k n) -> p i k n", i=3, k=KT)
        absmax = s.sb("absmax", [P, 2 * MT + KT])
        inv = s.sb("inv", [P, 2 * MT + KT])

        ld_chol, ld_const, ld_proj, ld_fold = s.sem("ld_chol"), s.sem("ld_const"), s.sem("ld_proj"), s.sem("ld_fold")
        ld_raw_t, ld_b2, ld_split = s.sem("ld_raw_t"), s.sem("ld_b2"), s.sem("ld_split")
        split_high, split_low = s.sem("split_high"), s.sem("split_low")
        ld_mod, ld_ffn, ld_late = s.sem("ld_mod"), s.sem("ld_ffn"), s.sem("ld_late")
        ld_x = [s.sem(f"ld_x{c}") for c in range(CHUNKS)]
        pads_set, b2_set = s.sem("pads_set"), s.sem("b2_set")
        dve = s.sem("dve")
        gram_ready, row_ready, row_used = s.sem("gram_ready"), s.sem("row_ready"), s.sem("row_used")
        proj_ready, proj_scaled, proj_high, proj_low = (s.sem(n) for n in ("proj_ready", "proj_scaled", "proj_high", "proj_low"))
        fold_ready, fold_high, fold_used = (s.sem(n) for n in ("fold_ready", "fold_high", "fold_used"))
        silu_ready, mod_ready = s.sem("silu_ready"), s.sem("mod_ready")
        inv_ready, shifted, clipped, ints_ready, turned, turned_used = (
            s.sem(n) for n in ("inv_ready", "shifted", "clipped", "ints_ready", "turned", "turned_used"))
        chol_done, root_ready, m_turned, m_copied, q_ready, q_signed, q_turned = (
            s.sem(n) for n in ("chol_done", "root_ready", "m_turned", "m_copied", "q_ready", "q_signed", "q_turned"))
        ident = w["ident"]
        proj_bank = (bank[1], bank[7])
        quant_parts = [(rows_gu[:, 4 * i:4 * i + 4, :], int_gu[:, 4 * i:4 * i + 4, :], 4 * i + 4) for i in range(3)]
        quant_parts += [(rows_d[:, i, :], int_d[:, i, 0:FF], 2 * MT + i + 1) for i in range(KT)]
        slots = [("project", 0), ("project", 1), ("fold", 0), ("fold", 1), ("project", 2), ("fold", 2), ("modulation", 0),
                 ("project", 3), ("project", 4), ("project", 5), ("project", 6), ("project", 7)]
        at, slot_of = 8, {}
        for kind, n in slots:
            slot_of[kind, n] = at
            at += 1 if kind == "modulation" or (kind, n) == ("fold", 0) else TILES
        for i in range(5):
            slot_of["turn", i] = at + i

        with nc.Block() as block:

            @block.sync
            def _(sp):
                sp.dma_start(raw[:, :], io["raw"]).then_inc(ld_chol, 16)
                sp.dma_start(ident[:, :], io["ident"]).then_inc(ld_chol, 16)
                sp.dma_start(w["below"][:, :], io["below"]).then_inc(ld_chol, 16)
                for i in range(2):
                    half = slice(i * R, (i + 1) * R)
                    sp.dma_start(ib_t[:, :, i, :], io["ib_t"]).then_inc(ld_proj, 16)
                    sp.dma_start(w["spec"][half, :], io["cond_t"]).then_inc(ld_proj, 16)
                for c in range(CHUNKS):
                    if c == 2:
                        sp.dma_start(raw_t[:, :], io["raw_t"]).then_inc(ld_raw_t, 16)
                        sp.wait_ge(ld_ffn, 16 * 7)
                    sp.dma_start(w["x"][:, :, c * CH:(c + 1) * CH], io["x"][c]).then_inc(ld_x[c], 16)
                sp.dma_start(w2_raw, io["w2"]).then_inc(ld_split, 16)
                for i, name in enumerate(("wq", "wk", "wv")):
                    sp.dma_start(qkv_raw[:, i, :, :], io[name]).then_inc(ld_split, 16)
                sp.dma_start(w["wo"][:, :, :], io["wo"]).then_inc(ld_late, 16)
                sp.wait_ge(ld_late, 16)

            @block.gpsimd
            def _(pool):
                nc.gpsimd.memset(b2_pad[:, :], 0.0).then_inc(b2_set, 1)
                nc.gpsimd.memset(w["rb"][:, :], 0.0).then_inc(pads_set, 1)
                nc.gpsimd.memset(rw[:, :, :], 0.0).then_inc(pads_set, 1)
                nc.gpsimd.memset(rows_gu[:, MT - 1, :], 1.0).then_inc(pads_set, 1)
                nc.gpsimd.memset(rows_gu[:, 2 * MT - 1, :], 1.0).then_inc(pads_set, 1)
                nc.gpsimd.memset(int_d[:, :, FF:MT * P], 0.0).then_inc(pads_set, 1)
                nc.gpsimd.memset(w["magic"][:, :], MAGIC).then_inc(pads_set, 1)
                nc.gpsimd.memset(w["mask_pad"][:, :, :, :], 0.0).then_inc(pads_set, 1)
                pool.wait_ge(b2_set, 1)
                for g in range(4):
                    pool.dma_start(b2_pad[32 * g:32 * g + NE, :], io["b2"]).then_inc(ld_b2, 16)
                pool.wait_ge(split_high, 1)
                nc.gpsimd.tensor_tensor(w["w2_low"][:, :, :], w2_raw, w["w2_high"][:, :, :].bitcast(F32),
                                        ALU.subtract).then_inc(split_low, 1)
                for i, name in enumerate(("wq", "wk", "wv")):
                    pool.wait_ge(split_high, 2 + i)
                    nc.gpsimd.tensor_tensor(w[name][:, 1, :, :], qkv_raw[:, i, :, :], w[name][:, 0, :, :].bitcast(F32),
                                            ALU.subtract).then_inc(split_low, 1)

            @block.scalar
            def _(act):
                act.wait_ge(pads_set, 7)
                for i in range(2):
                    half = slice(i * R, (i + 1) * R)
                    act.dma_start(w["rank"][half, :], io["rank_t"]).then_inc(ld_const, 16)
                    act.dma_start(ob_t[:, :, i, :], io["ob_t"]).then_inc(ld_fold, 16)
                act.dma_start(rw[:, :, 0:NE], io["rw"]).then_inc(ld_fold, 16)
                act.dma_start(w1[:, :, :], io["w1"]).then_inc(ld_fold, 16)
                act.dma_start(select[:, :], io["select"]).then_inc(ld_const, 16)
                act.dma_start(w["rb"][0:NE, :], io["rb"]).then_inc(ld_const, 16)
                act.dma_start(w["b1"][:, :], io["b1"]).then_inc(ld_const, 16)
                act.dma_start(w["heads"][:, :], io["heads"]).then_inc(ld_const, 16)
                act.dma_start(w["prio"][:, :], io["prio"]).then_inc(ld_const, 16)
                act.dma_start(cond[:, :], io["cond_t"]).then_inc(ld_mod, 16)
                act.dma_start(wc_t[:, :, :], io["wc_t"]).then_inc(ld_mod, 16)
                act.dma_start(bc[:, :], io["bc"]).then_inc(ld_mod, 16)
                act.dma_start(rms_w[:, :], io["rms_w"]).then_inc(ld_mod, 16)
                act.dma_start(w["clips"][:, :], io["clips"].partition_broadcast(P)).then_inc(ld_mod, 16)
                act.dma_start(rows_gu[:, 0:MT - 1, :], io["gate"]).then_inc(ld_ffn, 16)
                act.dma_start(rows_gu[0:TAIL, MT - 1, :], io["gate_tail"]).then_inc(ld_ffn, 16)
                act.dma_start(rows_gu[:, MT:2 * MT - 1, :], io["up"]).then_inc(ld_ffn, 16)
                act.dma_start(rows_gu[0:TAIL, 2 * MT - 1, :], io["up_tail"]).then_inc(ld_ffn, 16)
                act.dma_start(rows_d, io["down"]).then_inc(ld_ffn, 16)
                for i in range(2):
                    act.dma_start(mask8[i * SEQ:(i + 1) * SEQ, :], io["mask"]).then_inc(ld_ffn, 16)

                def project(c):
                    act.wait_ge(proj_scaled, c + 1)
                    nc.scalar.activation(w["hid"][:, c * CH:(c + 1) * CH], proj[:, :], ACT.Copy).then_inc(proj_high, 1)

                def fold(i):
                    act.wait_ge(fold_ready, i + 1)
                    n = P if i == 0 else CH
                    high = w["rw_high"][:, :] if i == 0 else w["w1_high"][:, (i - 1) * CH:i * CH]
                    nc.scalar.activation(high, bank[2 + i][:, 0:n], ACT.Copy).then_inc(fold_high, 1)

                def shift(tiles):
                    act.wait_ge(inv_ready, 1)
                    for i in tiles:
                        rows = rows_gu[:, i, :] if i < 2 * MT else rows_d[:, i - 2 * MT, :]
                        nc.scalar.activation(rows, rows, ACT.Identity, scale=inv[:, i:i + 1],
                                             bias=w["magic"][:, 0:1]).then_inc(shifted, 1)

                def integers(i):
                    rows, ints, _ = quant_parts[i]
                    act.wait_ge(clipped, i + 1)
                    nc.scalar.activation(ints, rows, ACT.Copy, bias=-MAGIC).then_inc(ints_ready, 1)

                project(0)
                project(1)
                fold(0)
                act.wait_ge(ld_mod, 16 * 5)
                nc.scalar.activation(cond[:, :], cond[:, :], ACT.Silu).then_inc(silu_ready, 1)
                nc.scalar.activation(w["clips"][:, :], w["clips"][:, :], ACT.Sigmoid).then_inc(silu_ready, 1)
                fold(1)
                project(2)
                fold(2)
                shift(range(0, 6))
                project(3)
                shift(range(6, 2 * MT))
                project(4)
                shift(range(2 * MT, 2 * MT + KT))
                act.wait_ge(ld_split, 16 * 4)
                nc.scalar.activation(w["w2_high"][:, :, :], w2_raw, ACT.Copy).then_inc(split_high, 1)
                project(5)
                integers(0)
                integers(1)
                project(6)
                integers(2)
                integers(3)
                integers(4)
                project(7)
                for i, name in enumerate(("wq", "wk", "wv")):
                    nc.scalar.activation(w[name][:, 0, :, :], qkv_raw[:, i, :, :], ACT.Copy).then_inc(split_high, 1)

                def turned_copy(i):
                    act.wait_ge(turned, i + 1)
                    n = 1024 if i < 4 else 512
                    dst = w["gu_t"][:, i * 1024:i * 1024 + n] if i < 3 else w["down_t"][:, (i - 3) * 1024:(i - 3) * 1024 + n]
                    nc.scalar.activation(dst, bank[5 + i % 2][:, 0:n // 2].bitcast(BF16), ACT.Copy).then_inc(turned_used, 1)

                for i in range(5):
                    turned_copy(i)
                act.wait_ge(chol_done, 1)
                nc.scalar.activation(col[:, 4:5], col[:, 3:4], ACT.Sqrt).then_inc(root_ready, 1)

            @block.tensor
            def _(pe):
                def project(c, q):
                    if q == 0:
                        pe.wait_ge(ld_x[c], 16)
                        if c == 0:
                            pe.wait_ge(ld_proj, 16 * 4)
                        need(pe, proj_scaled, c - 1)
                    cols = slice(q * P, (q + 1) * P)
                    for k in range(KT):
                        last = nc.tensor.matmul(proj_bank[c % 2][:, cols], ib_t[:, k, :, :].rearrange("p a r -> p (a r)"),
                                                w["x"][:, k, c * CH + q * P:c * CH + (q + 1) * P], start=k == 0, stop=k == KT - 1)
                    if q == TILES - 1:
                        last.then_inc(proj_ready, 1)

                def fold(i, q):
                    if i == 0:
                        pe.wait_ge(ld_fold, 16 * 4)
                    cols = slice(q * P, (q + 1) * P)
                    for k in range(KT):
                        rhs = rw[:, k, :] if i == 0 else w1[:, k, (i - 1) * CH + q * P:(i - 1) * CH + (q + 1) * P]
                        last = nc.tensor.matmul(bank[2 + i][:, cols], ob_t[:, k, :, :].rearrange("p a r -> p (a r)"), rhs,
                                                start=k == 0, stop=k == KT - 1)
                    if i == 0 or q == TILES - 1:
                        last.then_inc(fold_ready, 1)

                def modulation():
                    pe.wait_ge(fold_used, 1)
                    pe.wait_ge(silu_ready, 1)
                    for i in range(4):
                        last = nc.tensor.matmul(bank[2][:, i * BATCH:(i + 1) * BATCH], wc_t[:, i, :], cond[:, :],
                                                start=True, stop=True)
                    last.then_inc(mod_ready, 1)

                def turn(i):
                    pe.wait_ge(ints_ready, (2, 3, 3, 5, 5)[i])
                    if i >= 2:
                        pe.wait_ge(turned_used, i - 1)
                    out = bank[5 + i % 2][:, :].bitcast(BF16)
                    for b in range(8 if i < 4 else 4):
                        n = 8 * i + b
                        if i < 3:
                            src = int_gu[:, n % (2 * MT), (n // (2 * MT)) * P:(n // (2 * MT) + 1) * P]
                        else:
                            n -= 24
                            src = int_d[:, n % KT, (n // KT) * P:(n // KT + 1) * P]
                        last = nc.tensor.transpose(out[:, b * P:(b + 1) * P], src, w["ident_b"][:, :])
                    last.then_inc(turned, 1)

                pe.wait_ge(ld_chol, 16 * 3)
                nc.tensor.matmul(bank[0][0:R, 0:R], raw[:, :], raw[:, :], start=True, stop=True).then_inc(gram_ready, 1)
                for j in range(R):
                    pe.wait_ge(row_used, j + 1)
                    nc.tensor.matmul(bank[0][0:R, 0:R + 1], ident[0:R, j:j + 1].to_broadcast([R, R]),
                                     elim[:, j:j + R + 1], start=True, stop=True).then_inc(row_ready, 1)
                    for c in range(CHUNKS):
                        if 0 <= j - slot_of["project", c] < TILES:
                            project(c, j - slot_of["project", c])
                    for i in range(3):
                        if 0 <= j - slot_of["fold", i] < (TILES if i else 1):
                            fold(i, j - slot_of["fold", i])
                    if j == slot_of["modulation", 0]:
                        modulation()
                    for i in range(5):
                        if j == slot_of["turn", i]:
                            turn(i)
                pe.wait_ge(m_copied, 1)
                nc.tensor.transpose(bank[0][0:R, 0:R], elim[:, R:2 * R], ident[0:R, 0:R]).then_inc(m_turned, 1)
                pe.wait_ge(m_copied, 2)
                nc.tensor.matmul(bank[1][0:R, 0:R], inv_t[:, :], raw_t[:, :], start=True, stop=True).then_inc(q_ready, 1)
                pe.wait_ge(q_signed, 1)
                nc.tensor.transpose(bank[2][:, 0:R], q_t[:, :, :].rearrange("p a r -> p (a r)"),
                                    ident[0:R, 0:R]).then_inc(q_turned, 1)

            @block.vector
            def _(v):
                me = Order(v, dve)

                def scale(c):
                    v.wait_ge(proj_ready, c + 1)
                    if c:
                        v.wait_ge(proj_low, c)
                    nc.vector.tensor_tensor(proj[:, :].rearrange("p (b t) -> p b t", t=SEQ),
                                            proj_bank[c % 2][:, :].rearrange("p (b t) -> p b t", t=SEQ),
                                            bcast_last(w["spec"][:, c * CB:(c + 1) * CB], SEQ),
                                            ALU.mult).then_inc(proj_scaled, 1)

                def low(c):
                    v.wait_ge(proj_high, c + 1)
                    part = w["hid"][R:P, c * CH:(c + 1) * CH]
                    nc.vector.tensor_tensor(part, proj[R:P, :], part.bitcast(F32), ALU.subtract).then_inc(proj_low, 1)

                def fold_low(i):
                    v.wait_ge(fold_high, i + 1)
                    n = P if i == 0 else CH
                    high = w["rw_high"][:, :] if i == 0 else w["w1_high"][:, (i - 1) * CH:i * CH]
                    out = w["rw_low"][:, :] if i == 0 else w["w1_low"][:, (i - 1) * CH:i * CH]
                    nc.vector.tensor_tensor(out, bank[2 + i][:, 0:n], high.bitcast(F32), ALU.subtract).then_inc(fold_used, 1)

                def modulation():
                    v.wait_ge(mod_ready, 1)
                    for i in range(KT):
                        nc.vector.tensor_scalar(w["shift"][:, i, :], bank[2][:, i * BATCH:(i + 1) * BATCH], bc[:, i:i + 1],
                                                None, ALU.add)
                        me.link(nc.vector.tensor_scalar(w["gain"][:, i, :], bank[2][:, (KT + i) * BATCH:(KT + i + 1) * BATCH],
                                                        bc[:, KT + i:KT + i + 1], 1.0, ALU.add, ALU.add))
                        me.link(nc.vector.tensor_scalar(w["gain"][:, i, :], w["gain"][:, i, :], rms_w[:, i:i + 1], None,
                                                        ALU.mult))

                def masks():
                    me.link(nc.vector.tensor_copy(maskf[:, :], mask8[:, :]))
                    me.add(nc.vector.tensor_scalar(w["mask_neg"][:, :], maskf[:, :], MASKED, None, ALU.mult))
                    me.link(nc.vector.tensor_reduce(count[:, 0:1], maskf[:, :], AX_X, ALU.add))
                    me.link(nc.vector.tensor_scalar(count[:, 0:1], count[:, 0:1], -1.0, float(SEQ), ALU.mult, ALU.add))
                    me.link(nc.vector.reciprocal(count[:, 1:2], count[:, 0:1]))
                    me.link(nc.vector.tensor_scalar(w["no_key"][:, :], count[:, 1:2], 0.0, None, ALU.mult))

                def largest(i):
                    if i == 0:
                        v.wait_ge(ld_ffn, 16 * 7)
                    out, rows = ((absmax[:, 2 * i:2 * i + 2], rows_gu[:, 2 * i:2 * i + 2, :]) if i < MT
                                 else (absmax[:, MT + i:MT + i + 1], rows_d[:, i - MT, :]))
                    me.add(nc.vector.tensor_reduce(out, rows, AX_X, ALU.max, apply_absolute_value=True))

                def row_scales():
                    me.wait()
                    me.link(nc.vector.tensor_scalar(w["row_scale"][:, :], absmax[:, :], 1.0 / QMAX, None, ALU.mult))
                    nc.vector.reciprocal(inv[:, :], w["row_scale"][:, :]).then_inc(inv_ready, 1)

                def clip(i):
                    rows, _, tiles = quant_parts[i]
                    v.wait_ge(shifted, tiles)
                    nc.vector.tensor_scalar(rows, rows, MAGIC + QMAX, MAGIC - QMAX - 1, ALU.min, ALU.max).then_inc(clipped, 1)

                def constants(i):
                    if i == 0:
                        v.wait_ge(ld_const, 16 * 7)
                        v.wait_ge(ld_b2, 16 * 4)
                        v.wait_ge(ld_raw_t, 16)
                        v.wait_ge(ld_proj, 16 * 4)
                        me.add(nc.vector.tensor_copy(w["select"][:, :], select[:, :]))
                        me.add(nc.vector.tensor_copy(w["b2_high"][:, :], b2_pad[:, :]))
                    else:
                        me.wait()
                        q = slice(32 * (2 * i - 1), 32 * 2 * i)
                        me.add(nc.vector.tensor_tensor(w["b2_high"][q, :], b2_pad[q, :],
                                                       w["b2_high"][q, :].bitcast(F32), ALU.subtract))

                def side(j):
                    for c in range(CHUNKS):
                        if j == slot_of["project", c] + TILES:
                            scale(c)
                        if j == slot_of["project", c] + TILES + 2:
                            low(c)
                    for i in range(3):
                        if j == slot_of["fold", i] + (TILES if i else 1) + 2:
                            fold_low(i)
                    if j in CONSTANT_STEPS:
                        constants(CONSTANT_STEPS.index(j))
                    if j in LARGEST_STEPS:
                        largest(LARGEST_STEPS.index(j))
                    if j == LARGEST_STEPS[-1] + 2:
                        row_scales()
                    if j in CLIP_STEPS:
                        clip(CLIP_STEPS.index(j))
                    if j == 39:
                        modulation()
                    if j == 45:
                        masks()

                CONSTANT_STEPS = (8, 9, 10)
                LARGEST_STEPS = (13, 15, 17, 20, 21, 22, 24, 26)
                CLIP_STEPS = (33, 35, 37, 41, 43)

                v.wait_ge(ld_chol, 16 * 3)
                me.add(nc.vector.tensor_copy(w["ident_b"][:, :], ident[:, :]))
                me.add(nc.vector.tensor_copy(elim[:, R:2 * R], ident[0:R, 0:R]))
                v.wait_ge(gram_ready, 1)
                nc.vector.scalar_tensor_tensor(elim[:, 0:R], ident[0:R, 0:R], EPS_GRAM, bank[0][0:R, 0:R],
                                               ALU.mult, ALU.add).then_inc(row_used, 1)
                me.wait()
                for j in range(R):
                    v.wait_ge(row_ready, j + 1)
                    me.link(nc.vector.reciprocal(col[:, 0:1], bank[0][0:R, 0:1]))
                    me.link(nc.vector.scalar_tensor_tensor(col[:, 1:2], elim[:, j:j + 1], col[:, 0:1],
                                                           w["below"][:, j:j + 1], ALU.mult, ALU.mult))
                    nc.vector.scalar_tensor_tensor(elim[:, j:j + R + 1], bank[0][0:R, 0:R + 1], col[:, 1:2],
                                                   elim[:, j:j + R + 1], ALU.mult, ALU.add).then_inc(row_used, 1)
                    side(j)
                    v.wait_ge(row_used, j + 2)
                me.link(nc.vector.tensor_tensor(scratch[:, :], elim[:, 0:R], ident[0:R, 0:R], ALU.mult))
                nc.vector.tensor_reduce(col[:, 3:4], scratch[:, :], AX_X, ALU.add).then_inc(chol_done, 1)
                nc.vector.sem_inc(m_copied, 1)
                v.wait_ge(m_turned, 1)
                nc.vector.tensor_copy(inv_t[:, :], bank[0][0:R, 0:R]).then_inc(m_copied, 1)
                v.wait_ge(root_ready, 1)
                me.link(nc.vector.reciprocal(col[:, 5:6], col[:, 4:5]))
                me.link(nc.vector.scalar_tensor_tensor(col[:, 6:7], col[:, 3:4], col[:, 5:6], col[:, 4:5], ALU.mult, ALU.add))
                me.link(nc.vector.tensor_scalar(col[:, 6:7], col[:, 6:7], 0.5, None, ALU.mult))
                me.link(nc.vector.reciprocal(col[:, 5:6], col[:, 6:7]))
                v.wait_ge(q_ready, 1)
                me.link(nc.vector.tensor_scalar(q_t[:, 0, :], bank[1][0:R, 0:R], col[:, 5:6], None, ALU.mult))
                me.link(nc.vector.tensor_tensor(scratch[:, :], q_t[:, 0, :], raw_t[:, :], ALU.mult))
                me.link(nc.vector.tensor_reduce(col[:, 7:8], scratch[:, :], AX_X, ALU.add))
                me.link(nc.vector.tensor_scalar(col[:, 7:8], col[:, 7:8], 0.0, 2.0, ALU.is_ge, ALU.mult))
                me.link(nc.vector.tensor_scalar(col[:, 7:8], col[:, 7:8], -1.0, None, ALU.add))
                me.link(nc.vector.tensor_scalar(q_t[:, 1, :], q_t[:, 0, :], col[:, 7:8], None, ALU.mult))
                nc.vector.tensor_copy(q_t[:, 0, :], q_t[:, 1, :]).then_inc(q_signed, 1)
                v.wait_ge(q_turned, 1)
                high = w["mix_high"][:, :].rearrange("p (a r) -> p a r", a=2)
                me.link(nc.vector.tensor_copy(high, bcast_mid(bank[2][:, 0:R], 2)))
                me.link(nc.vector.tensor_tensor(w["mix_low"][:, :].rearrange("p (a r) -> p a r", a=2),
                                                bcast_mid(bank[2][:, 0:R], 2), high.bitcast(F32), ALU.subtract))


def route(nc, w):
    with ExitStack() as scope:
        s = Memory(nc, scope, "route_")
        bank = s.banks(4)
        hid32 = s.sb("hid32", [P, CH])
        logit_t = s.sb("logit_t", [P, CH])
        n_t = CHUNKS * TILES
        logits = s.sb("logits", [P, n_t, NE])
        a, b, pick1, pick2 = (s.sb(n, [P, n_t, NE]) for n in ("a", "b", "pick1", "pick2"))
        max1, max2, top, wt1, wt2 = (s.sb(n, [P, n_t]) for n in ("max1", "max2", "top", "wt1", "wt2"))
        hid_ready, hid_scaled, hid_high, hid_low = (s.sem(n) for n in ("hid_ready", "hid_scaled", "hid_high", "hid_low"))
        logit_ready, logit_copied, turned, turned_used = (
            s.sem(n) for n in ("logit_ready", "logit_copied", "turned", "turned_used"))
        dve, gap_ready, exp_ready = s.sem("dve"), s.sem("gap_ready"), s.sem("exp_ready")

        with nc.Block() as block:

            @block.tensor
            def _(pe):
                def hidden(c, first):
                    if not first:
                        pe.wait_ge(hid_scaled, c)
                    rhs = w["hid"][:, bass.ds(c * CH, CH)]
                    nc.tensor.matmul(bank[0][:, :], w["mix_high"][:, :], rhs, start=True, stop=False)
                    nc.tensor.matmul(bank[0][:, :], w["mix_low"][:, :], rhs, start=False, stop=True).then_inc(hid_ready, 1)

                def logit(c, first):
                    pe.wait_ge(hid_low, c + 1)
                    if not first:
                        pe.wait_ge(logit_copied, c)
                    rhs = w["hid"][:, bass.ds(c * CH, CH)]
                    nc.tensor.matmul(bank[1][:, :], w["rw_high"][:, :], rhs, start=True, stop=False)
                    nc.tensor.matmul(bank[1][:, :], w["rw_low"][:, :], rhs, start=False, stop=True).then_inc(logit_ready, 1)

                def turn(c, first):
                    pe.wait_ge(logit_copied, c + 1)
                    if not first:
                        pe.wait_ge(turned_used, c)
                    for t in range(TILES):
                        last = nc.tensor.transpose(bank[2][:, t * P:(t + 1) * P], logit_t[:, t * P:(t + 1) * P],
                                                   w["ident"][:, :])
                    last.then_inc(turned, 1)

                hidden(0, True)
                hidden(1, False)
                logit(0, True)
                turn(0, True)
                with pe.Fori(2, CHUNKS) as c:
                    hidden(c, False)
                    logit(c - 1, False)
                    turn(c - 1, False)
                logit(CHUNKS - 1, False)
                turn(CHUNKS - 1, False)

            @block.scalar
            def _(act):
                def high(c):
                    act.wait_ge(hid_scaled, c + 1)
                    nc.scalar.activation(w["hid"][:, bass.ds(c * CH, CH)], hid32[:, :], ACT.Copy).then_inc(hid_high, 1)

                def logit(c, first):
                    act.wait_ge(logit_ready, c + 1)
                    if not first:
                        act.wait_ge(turned, c)
                    nc.scalar.activation(logit_t[:, :], bank[1][:, :], ACT.Identity, bias=w["rb"][:, 0:1]).then_inc(logit_copied, 1)

                high(0)
                high(1)
                logit(0, True)
                with act.Fori(2, CHUNKS) as c:
                    high(c)
                    logit(c - 1, False)
                logit(CHUNKS - 1, False)
                act.wait_ge(gap_ready, 1)
                nc.scalar.activation(wt2[:, :], top[:, :], ACT.Exp).then_inc(exp_ready, 1)

            @block.vector
            def _(v):
                def scale(c, first):
                    v.wait_ge(hid_ready, c + 1)
                    if not first:
                        v.wait_ge(hid_low, c)
                    nc.vector.tensor_tensor(hid32[:, :].rearrange("p (b t) -> p b t", t=SEQ),
                                            bank[0][:, :].rearrange("p (b t) -> p b t", t=SEQ),
                                            bcast_last(w["rank"][:, bass.ds(c * CB, CB)], SEQ), ALU.mult).then_inc(hid_scaled, 1)
                    v.wait_ge(hid_high, c + 1)
                    part = w["hid"][R:P, bass.ds(c * CH, CH)]
                    nc.vector.tensor_tensor(part, hid32[R:P, :], part.bitcast(F32), ALU.subtract).then_inc(hid_low, 1)

                def gather(c):
                    v.wait_ge(turned, c + 1)
                    nc.vector.tensor_copy(logits[:, bass.ds(c * TILES, TILES), :],
                                          bank[2][:, :].rearrange("p (t n) -> p t n", n=P)[:, :, 0:NE]).then_inc(turned_used, 1)

                scale(0, True)
                scale(1, False)
                gather(0)
                with v.Fori(2, CHUNKS) as c:
                    scale(c, False)
                    gather(c - 1)
                gather(CHUNKS - 1)

                me = Order(v, dve)
                v.wait_ge(turned_used, CHUNKS)
                prio = bcast_mid(w["prio"][:, :], n_t)

                def best(values, maximum, pick):
                    me.link(nc.vector.tensor_reduce(maximum[:, :], values[:, :, :], AX_X, ALU.max))
                    me.link(nc.vector.tensor_tensor(a[:, :, :], values[:, :, :], bcast_last(maximum[:, :], NE), ALU.is_equal))
                    me.link(nc.vector.tensor_tensor(a[:, :, :], a[:, :, :], prio, ALU.mult))
                    me.link(nc.vector.tensor_reduce(top[:, :], a[:, :, :], AX_X, ALU.max))
                    me.link(nc.vector.tensor_tensor(pick[:, :, :], a[:, :, :], bcast_last(top[:, :], NE), ALU.is_equal))

                best(logits, max1, pick1)
                me.link(nc.vector.scalar_tensor_tensor(b[:, :, :], pick1[:, :, :], -3.0e38, logits[:, :, :], ALU.mult, ALU.add))
                best(b, max2, pick2)
                me.link(nc.vector.tensor_tensor(top[:, :], max2[:, :], max1[:, :], ALU.subtract))
                nc.vector.sem_inc(gap_ready, 1)
                v.wait_ge(exp_ready, 1)
                me.link(nc.vector.tensor_scalar(wt1[:, :], wt2[:, :], 1.0, None, ALU.add))
                me.link(nc.vector.reciprocal(wt1[:, :], wt1[:, :]))
                me.link(nc.vector.tensor_tensor(wt2[:, :], wt2[:, :], wt1[:, :], ALU.mult))
                me.link(nc.vector.tensor_tensor(pick1[:, :, :], pick1[:, :, :], bcast_last(wt1[:, :], NE), ALU.mult))
                me.link(nc.vector.tensor_tensor(pick2[:, :, :], pick2[:, :, :], bcast_last(wt2[:, :], NE), ALU.mult))
                me.link(nc.vector.tensor_tensor(a[:, :, :], pick1[:, :, :], pick2[:, :, :], ALU.add))
                me.link(nc.vector.tensor_copy(w["gate_high"][:, :, :], a[:, :, :]))
                me.link(nc.vector.tensor_tensor(w["gate_low"][:, :, :], a[:, :, :], w["gate_high"][:, :, :].bitcast(F32), ALU.subtract))


def experts(nc, w):
    with ExitStack() as scope:
        s = Memory(nc, scope, "moe_")
        bank = s.banks(8)
        out_bank, h1_bank, gate_bank, qkv_bank = bank[0:2], bank[2:4], bank[4:6], bank[6:8]
        gate_t = s.sb("gate_t", [P, CH], F32R)
        act_h = s.sb("act_h", [P, 2, CH])
        high, low = s.sb("high", [P, 2, CH], F32R), s.sb("low", [P, 2, CH], F32R)
        x2_high, x2_low = s.sb("x2_high", [P, KT, CH], F32R), s.sb("x2_low", [P, KT, CH], F32R)
        names = ("mask_ready", "mask_turned", "gate_copied", "h1_ready", "act_ready", "gate_ready", "gated_ready",
                 "high_ready", "low_ready", "gated_used", "out_ready", "x2_ready", "x2_high_ready", "x2_low_ready",
                 "qkv_ready", "qk_copied", "v_copied")
        (mask_ready, mask_turned, gate_copied, h1_ready, act_ready, gate_ready, gated_ready,
         high_ready, low_ready, gated_used, out_ready, x2_ready, x2_high_ready, x2_low_ready,
         qkv_ready, qk_copied, v_copied) = (s.sem(n) for n in names)
        big = w["big"]
        q_all = big[:, 0:KT * TOK].rearrange("p (t k n) -> p t k n", t=PAIRS, k=KT)
        k_all = big[:, KT * TOK:2 * KT * TOK].rearrange("p (t k n) -> p t k n", t=PAIRS, k=KT)
        v_all = big[:, 2 * KT * TOK:3 * KT * TOK].rearrange("p (t b h d) -> p t b h d", t=PAIRS, b=2, d=DH)
        AHEAD = 3
        BANK_STEPS = (1, 2, 3, 4, 6, 7)
        BANK_OF = (0, 1, 0, 1, 1, 0)
        V_BANKS = (2, 3)

        def chunks(engine, body):
            body(0, True, True)
            body(1, False, True)
            with engine.Fori(2, CHUNKS - 1) as c:
                body(c, False, True)
            body(CHUNKS - 1, False, False)

        def ahead(c, n, more, do):
            if n + AHEAD < NE:
                do(c, n + AHEAD)
            elif more:
                do(c + 1, n + AHEAD - NE)

        def parts_free(engine, c, n):
            if n == 1:
                need(engine, out_ready, c * KT)
            else:
                need(engine, gated_used, c * (NE - 1) + max(n - 1, 0))

        with nc.Block() as block:

            @block.tensor
            def _(pe):
                def mask_turn(c):
                    pe.wait_ge(mask_ready, c + 1)
                    need(pe, v_copied, (c - 2) * 2 + 1)
                    for t in range(TILES):
                        last = nc.tensor.transpose(qkv_bank[0][:, t * P:(t + 1) * P],
                                                   w["mask_pad"][:, t, :, :].rearrange("p g n -> p (g n)"), w["ident"][:, :])
                    last.then_inc(mask_turned, 1)

                def first_layer(c, n):
                    need(pe, act_ready, c * NE + n - 1)
                    rhs = w["hid"][:, bass.ds(c * CH, CH)]
                    nc.tensor.matmul(h1_bank[n % 2][:, :], w["w1_high"][:, n * P:(n + 1) * P], rhs, start=True, stop=False)
                    nc.tensor.matmul(h1_bank[n % 2][:, :], w["w1_low"][:, n * P:(n + 1) * P], rhs,
                                     start=False, stop=True).then_inc(h1_ready, 1)
                    if n == 0:
                        pe.wait_ge(gate_copied, c + 1)
                    need(pe, gated_ready, c * NE + n - 1)
                    nc.tensor.matmul(gate_bank[n % 2][:, :], w["select"][:, n:n + 1].to_broadcast([P, P]), gate_t[:, :],
                                     start=True, stop=True).then_inc(gate_ready, 1)

                def second_layer(c, n):
                    pe.wait_ge(low_ready, c * NE + n + 1)
                    for f in range(KT):
                        cols = slice(f * P, (f + 1) * P)
                        if n == 0:
                            need(pe, x2_ready, (c - 1) * KT + f + 1)
                            nc.tensor.matmul(out_bank[f][:, :], w["b2_high"][:, cols], gate_t[:, :],
                                             start=True, stop=False, skip_group_check=True)
                        for weight, rows in ((w["w2_high"], high), (w["w2_high"], low), (w["w2_low"], high)):
                            last = nc.tensor.matmul(out_bank[f][:, :], weight[:, n, cols], rows[:, n % 2, :], start=False,
                                                    stop=n == NE - 1 and weight is w["w2_low"], skip_group_check=True)
                        if n == NE - 1:
                            last.then_inc(out_ready, 1)
                    if n < NE - 1:
                        last.then_inc(gated_used, 1)

                def qkv(c, i):
                    if i < 2:
                        need(pe, qk_copied, c * 4 - (i == 1))
                    elif i < 4:
                        pe.wait_ge(qk_copied, c * 4 + i - 1)
                    elif i == 4:
                        pe.wait_ge(v_copied, c * 2 + 2)
                    elif not isinstance(c, int) or c + 2 < CHUNKS:
                        pe.wait_ge(gate_copied, c + 3)
                    else:
                        pe.wait_ge(v_copied, c * 2 + 1)
                    passes = ((0, x2_high), (0, x2_low), (1, x2_high))
                    if i in V_BANKS:
                        for t in range(2):
                            at = (2 * (i - 2) + t) * P
                            for k in range(KT):
                                for part, x2 in passes:
                                    last = nc.tensor.matmul(qkv_bank[BANK_OF[i]][:, t * D:(t + 1) * D], x2[:, k, at:at + P],
                                                            w["wv"][:, part, k, :], start=k == 0 and x2 is x2_high and part == 0,
                                                            stop=k == KT - 1 and part == 1)
                    else:
                        for k in range(KT):
                            if i == 0:
                                pe.wait_ge(x2_low_ready, c * KT + k + 1)
                            for part, x2 in passes:
                                weight = w["wq"] if i < 2 else w["wk"]
                                last = nc.tensor.matmul(qkv_bank[BANK_OF[i]][:, :], weight[:, part, k, (i % 2) * P:(i % 2 + 1) * P],
                                                        x2[:, k, :], start=k == 0 and x2 is x2_high and part == 0,
                                                        stop=k == KT - 1 and part == 1)
                    last.then_inc(qkv_ready, 1)

                def body(c, first, more):
                    for n in range(NE):
                        if n == 5 and more:
                            mask_turn(c + 1)
                        second_layer(c, n)
                        if n in BANK_STEPS and not first:
                            qkv(c - 1, BANK_STEPS.index(n))
                        ahead(c, n, more, first_layer)

                mask_turn(0)
                for n in range(AHEAD):
                    first_layer(0, n)
                chunks(pe, body)
                for i in range(6):
                    qkv(CHUNKS - 1, i)

            @block.scalar
            def _(act):
                def gates(c):
                    act.wait_ge(mask_turned, c + 1)
                    need(act, gate_ready, c * NE)
                    nc.scalar.activation(gate_t[:, :], qkv_bank[0][:, :], ACT.Copy).then_inc(gate_copied, 1)

                def high_part(c, n):
                    act.wait_ge(gated_ready, c * NE + n + 1)
                    parts_free(act, c, n)
                    nc.scalar.activation(high[:, n % 2, :], act_h[:, n % 2, :], ACT.Copy).then_inc(high_ready, 1)

                def high_before(c, n):
                    if n > 0:
                        high_part(c, n - 1)
                    elif not isinstance(c, int) or c > 0:
                        high_part(c - 1, NE - 1)

                def gelu(c, n):
                    act.wait_ge(h1_ready, c * NE + n + 1)
                    need(act, low_ready, c * NE + n - 1)
                    nc.scalar.activation(act_h[:, n % 2, :], h1_bank[n % 2][:, :], ACT.Gelu,
                                         bias=w["b1"][:, n:n + 1]).then_inc(act_ready, 1)

                def x2_part(c):
                    for f in range(KT):
                        act.wait_ge(x2_ready, c * KT + f + 1)
                        need(act, qkv_ready, c * 6)
                        nc.scalar.activation(x2_high[:, f, :], w["x"][:, f, bass.ds(c * CH, CH)],
                                             ACT.Copy).then_inc(x2_high_ready, 1)

                def copy(c, i):
                    act.wait_ge(qkv_ready, c * 6 + i + 1)
                    dst = (q_all if i < 2 else k_all)[:, bass.ds(c * TILES, TILES), i % 2, :]
                    nc.scalar.activation(dst, qkv_bank[BANK_OF[i]][:, :].rearrange("p (t n) -> p t n", n=P),
                                         ACT.Copy).then_inc(qk_copied, 1)

                def body(c, first, more):
                    for n in range(NE):
                        if n == 5 and more:
                            gates(c + 1)
                        ahead(c, n, more, high_before)
                        if n in BANK_STEPS and BANK_STEPS.index(n) not in V_BANKS and not first:
                            copy(c - 1, BANK_STEPS.index(n))
                        ahead(c, n, more, gelu)
                        if n + AHEAD == NE and not more:
                            high_part(c, NE - 1)
                    x2_part(c)

                gates(0)
                for n in range(AHEAD):
                    high_before(0, n)
                    gelu(0, n)
                chunks(act, body)
                for i in (0, 1, 4, 5):
                    copy(CHUNKS - 1, i)

            @block.vector
            def _(v):
                def low_part(c, n):
                    v.wait_ge(high_ready, c * NE + n + 1)
                    parts_free(v, c, n)
                    nc.vector.tensor_tensor(low[:, n % 2, :], act_h[:, n % 2, :], high[:, n % 2, :].bitcast(F32),
                                            ALU.subtract).then_inc(low_ready, 1)

                def low_before(c, n):
                    if n > 0:
                        low_part(c, n - 1)
                    elif not isinstance(c, int) or c > 0:
                        low_part(c - 1, NE - 1)

                def weigh(c, n):
                    v.wait_ge(act_ready, c * NE + n + 1)
                    v.wait_ge(gate_ready, c * NE + n + 1)
                    nc.vector.tensor_tensor(act_h[:, n % 2, :], act_h[:, n % 2, :], gate_bank[n % 2][:, :],
                                            ALU.mult).then_inc(gated_ready, 1)

                def add(c, f):
                    v.wait_ge(out_ready, c * KT + f + 1)
                    x = w["x"][:, f, bass.ds(c * CH, CH)]
                    nc.vector.tensor_tensor(x, out_bank[f][:, :], x, ALU.add).then_inc(x2_ready, 1)

                def x2_part(c):
                    for f in range(KT):
                        v.wait_ge(x2_high_ready, c * KT + f + 1)
                        v.wait_ge(x2_ready, c * KT + f + 1)
                        nc.vector.tensor_tensor(x2_low[:, f, :], w["x"][:, f, bass.ds(c * CH, CH)],
                                                x2_high[:, f, :].bitcast(F32), ALU.subtract).then_inc(x2_low_ready, 1)

                def copy(c, i):
                    v.wait_ge(qkv_ready, c * 6 + i + 1)
                    src = qkv_bank[BANK_OF[i]][:, :].rearrange("p (t h j d) -> p t h j d", t=2, j=2, d=DH)
                    for b in range(2):
                        for j in range(2):
                            dst = v_all[j * SEQ:(j + 1) * SEQ, bass.ds(c * TILES + 2 * (i - 2), 2), b, :, :]
                            last = nc.vector.tensor_copy(dst, src[b * SEQ:(b + 1) * SEQ, :, :, j, :])
                    last.then_inc(v_copied, 1)

                def body(c, first, more):
                    for n in range(NE):
                        if n in BANK_STEPS and BANK_STEPS.index(n) in V_BANKS and not first:
                            copy(c - 1, BANK_STEPS.index(n))
                        if n == NE - 1:
                            add(c, 1)
                        ahead(c, n, more, low_before)
                        if n + AHEAD == NE and not more:
                            low_part(c, NE - 1)
                        if n == NE - 2:
                            add(c, 0)
                        ahead(c, n, more, weigh)
                    x2_part(c)

                for n in range(AHEAD):
                    low_before(0, n)
                    weigh(0, n)
                chunks(v, body)
                for i in V_BANKS:
                    copy(CHUNKS - 1, i)

            @block.gpsimd
            def _(pool):
                def masks(c):
                    need(pool, mask_turned, c)
                    for part, g in ((w["gate_high"], 0), (w["gate_low"], 2)):
                        src = part[:, bass.ds(c * TILES, TILES), :].bitcast(F32)
                        for i in range(2):
                            last = nc.gpsimd.tensor_copy(w["mask_pad"][:, :, g + i, 0:NE], src)
                    last.then_inc(mask_ready, 1)

                masks(0)
                with pool.Fori(1, CHUNKS) as c:
                    masks(c)


def attention(nc, w):
    with ExitStack() as scope:
        s = Memory(nc, scope, "att_")
        bank = s.banks(8)
        score_bank, prob_bank, val_bank, proj_bank = bank[0:2], bank[2:4], bank[4:6], bank[6]
        q_s = s.sb("q_s", [P, KT, P])
        k_bd = s.sb("k_bd", [P, KT, 2, HH, SEQ])
        v_bd = s.sb("v_bd", [P, KT, 2, HP, 2, DH])
        neg_max = s.sb("neg_max", [P, KT, HH], BF16)
        probs = s.sb("probs", [P, KT, CH])
        sums = s.sb("sums", [P, KT, HH])
        inv = s.sb("inv", [P, KT, HH])
        normed = s.sb("normed", [P, KT, CH])
        probs_t = s.sb("probs_t", [P, KT, CH])
        heads_t = s.sb("heads_t", [P, KT, P])
        squares = s.sb("squares", [P, D])
        names = ("q_copied", "k_ready_v", "k_ready_g", "v_copied", "v_cleared", "score_ready", "max_ready", "shift_ready",
                 "exp_ready", "sum_ready", "inv_ready", "norm_ready", "turned", "turned_copied", "val_ready",
                 "heads_v", "heads_a", "out_ready", "out_copied", "squared")
        (q_copied, k_ready_v, k_ready_g, v_copied, v_cleared, score_ready, max_ready, shift_ready,
         exp_ready, sum_ready, inv_ready, norm_ready, turned, turned_copied, val_ready,
         heads_v, heads_a, out_ready, out_copied, squared) = (s.sem(n) for n in names)
        big = w["big"]
        q_all = big[:, 0:KT * TOK].rearrange("p (t k n) -> p t k n", t=PAIRS, k=KT)
        out_all = big[:, 0:KT * TOK].rearrange("p (t n) -> p t n", t=PAIRS)
        k_all = big[:, KT * TOK:2 * KT * TOK].rearrange("p (t k b n) -> p t k b n", t=PAIRS, k=KT, b=2)
        v_all = big[:, 2 * KT * TOK:3 * KT * TOK].rearrange("p (t b h d) -> p t b h d", t=PAIRS, b=2, d=DH)
        lag = 3

        def live(t):
            return not isinstance(t, int) or 0 <= t < PAIRS

        def every_pair(engine, step):
            for t in range(lag):
                step(t)
            with engine.Fori(lag, PAIRS - 1) as t:
                step(t)
            for t in range(PAIRS - 1, PAIRS + lag):
                step(t)

        def unit(t, h):
            return 2 * t + h + 1

        def k_of(t, h, b):
            return k_all[:, bass.ds(t, 1), h, b, :].rearrange("p a n -> p (a n)")

        def value_part(h, i):
            return val_bank[h][:, :].rearrange("p (b i q) -> p i b q", b=2, i=HP)[32 * i:32 * i + 32, i, :, :]

        def heads_part(h, i):
            return heads_t[32 * i:32 * i + 32, h, :].rearrange("p (b q) -> p b q", b=2)

        with nc.Block() as block:

            @block.tensor
            def _(pe):
                def scores(t, h):
                    pe.wait_ge(q_copied, unit(t, h))
                    pe.wait_ge(k_ready_v if h == 0 else k_ready_g, t + 1)
                    need(pe, exp_ready, unit(t - 1, h))
                    for b in range(2):
                        half = slice(b * SEQ, (b + 1) * SEQ)
                        nc.tensor.matmul(score_bank[h][half, :], q_s[:, h, half],
                                         k_bd[:, h, b, :, :].rearrange("p h n -> p (h n)"),
                                         start=True, stop=False, skip_group_check=True)
                    nc.tensor.matmul(score_bank[h][:, :], w["ident_b"][:, :], bcast_mid(w["mask_neg"][:, :], HH),
                                     start=False, stop=False, skip_group_check=True).then_inc(score_ready, 1)

                def shift(t, h):
                    pe.wait_ge(max_ready, unit(t, h))
                    nc.tensor.matmul(score_bank[h][:, :], w["ident_b"][:, :], bcast_last(neg_max[:, h, :], SEQ),
                                     start=False, stop=True, skip_group_check=True).then_inc(shift_ready, 1)

                def turn(t, h):
                    pe.wait_ge(norm_ready, unit(t, h))
                    need(pe, turned_copied, unit(t - 1, h))
                    for i in range(HP):
                        last = nc.tensor.transpose(prob_bank[h][:, i * P:(i + 1) * P], normed[:, h, i * P:(i + 1) * P],
                                                   w["ident"][:, :])
                    last.then_inc(turned, 1)

                def values(t, h):
                    pe.wait_ge(turned_copied, unit(t, h))
                    pe.wait_ge(v_copied, unit(t, h))
                    need(pe, heads_v, unit(t - 1, h))
                    need(pe, heads_a, unit(t - 1, h))
                    prob = probs_t[:, h, :].rearrange("p (i b q) -> p b i q", i=HP, b=2)
                    for b in range(2):
                        last = nc.tensor.matmul(val_bank[h][:, b * 256:(b + 1) * 256],
                                                v_bd[:, h, b, :, :, :].rearrange("p i j d -> p (i j d)"),
                                                prob[:, b, :, :], start=True, stop=True)
                    last.then_inc(val_ready, 1)

                def project(t):
                    pe.wait_ge(heads_v, unit(t, 1))
                    pe.wait_ge(heads_a, unit(t, 1))
                    need(pe, squared, t)
                    for h in range(KT):
                        last = nc.tensor.matmul(proj_bank[:, 0:D], heads_t[:, h, :], w["wo"][:, h, :],
                                                start=h == 0, stop=h == KT - 1)
                    last.then_inc(out_ready, 1)

                def step(t):
                    if live(t - 2):
                        turn(t - 2, 1)
                    if live(t):
                        scores(t, 0)
                    if live(t - 1):
                        shift(t - 1, 1)
                    if live(t - 3):
                        project(t - 3)
                    if live(t - 2):
                        values(t - 2, 0)
                    if live(t):
                        scores(t, 1)
                        shift(t, 0)
                    if live(t - 2):
                        values(t - 2, 1)
                    if live(t - 1):
                        turn(t - 1, 0)

                every_pair(pe, step)

            @block.vector
            def _(v):
                def keys(t):
                    need(v, score_ready, unit(t - 1, 0))
                    for b in range(2):
                        last = nc.vector.tensor_tensor(k_bd[:, 0, b, :, :], bcast_mid(k_of(t, 0, b), HH),
                                                       bcast_last(w["heads"][:, :], SEQ), ALU.mult)
                    last.then_inc(k_ready_v, 1)

                def maximum(t, h):
                    v.wait_ge(score_ready, unit(t, h))
                    need(v, shift_ready, unit(t - 1, h))
                    nc.vector.tensor_reduce(neg_max[:, h, :], score_bank[h][:, :].rearrange("p (h n) -> p h n", n=SEQ),
                                            AX_X, ALU.max, negate=True).then_inc(max_ready, 1)

                def sum_up(t, h):
                    v.wait_ge(exp_ready, unit(t, h))
                    nc.vector.tensor_reduce(sums[:, h, :], probs[:, h, :].rearrange("p (h n) -> p h n", n=SEQ),
                                            AX_X, ALU.add).then_inc(sum_ready, 1)
                    v.wait_ge(sum_ready, unit(t, h))
                    need(v, norm_ready, unit(t - 1, h))
                    nc.vector.reciprocal(inv[:, h, :], sums[:, h, :]).then_inc(inv_ready, 1)

                def heads(t, h):
                    v.wait_ge(val_ready, unit(t, h))
                    need(v, out_ready, t)
                    for i in range(2):
                        last = nc.vector.tensor_copy(heads_part(h, i), value_part(h, i))
                    last.then_inc(heads_v, 1)

                def keep(t):
                    v.wait_ge(out_ready, t + 1)
                    v.wait_ge(q_copied, unit(t, 1))
                    nc.vector.tensor_copy(out_all[:, bass.ds(t, 1), :].rearrange("p a n -> p (a n)"),
                                          proj_bank[:, 0:D]).then_inc(out_copied, 1)

                def step(t):
                    if live(t):
                        maximum(t, 0)
                    if live(t - 3):
                        keep(t - 3)
                    if live(t - 1):
                        sum_up(t - 1, 1)
                    if live(t - 2):
                        heads(t - 2, 0)
                    if live(t + 1):
                        keys(t + 1)
                    if live(t):
                        maximum(t, 1)
                    if live(t - 2):
                        heads(t - 2, 1)
                    if live(t):
                        sum_up(t, 0)

                keys(0)
                every_pair(v, step)

            @block.gpsimd
            def _(pool):
                def keys(t):
                    need(pool, score_ready, unit(t - 1, 1))
                    for b in range(2):
                        last = nc.gpsimd.tensor_tensor(k_bd[:, 1, b, :, :], bcast_mid(k_of(t, 1, b), HH),
                                                       bcast_last(w["heads"][:, :], SEQ), ALU.mult)
                    last.then_inc(k_ready_g, 1)

                def normalise(t, h):
                    pool.wait_ge(inv_ready, unit(t, h))
                    need(pool, turned, unit(t - 1, h))
                    nc.gpsimd.tensor_tensor(normed[:, h, :].rearrange("p (h n) -> p h n", n=SEQ),
                                            probs[:, h, :].rearrange("p (h n) -> p h n", n=SEQ),
                                            bcast_last(inv[:, h, :], SEQ), ALU.mult).then_inc(norm_ready, 1)

                def step(t):
                    if live(t - 1):
                        normalise(t - 1, 1)
                    if live(t + 1):
                        keys(t + 1)
                    if live(t):
                        normalise(t, 0)

                keys(0)
                nc.gpsimd.memset(v_bd[:, :, :, :, :, :], 0.0).then_inc(v_cleared, 1)
                every_pair(pool, step)

            @block.scalar
            def _(act):
                def queries(t, h):
                    need(act, score_ready, unit(t - 1, h))
                    nc.scalar.activation(q_s[:, h, :], q_all[:, bass.ds(t, 1), h, :].rearrange("p a n -> p (a n)"),
                                         ACT.Copy).then_inc(q_copied, 1)

                def values(t, h):
                    need(act, val_ready, unit(t - 1, h))
                    for j in range(2):
                        half = slice(j * SEQ, (j + 1) * SEQ)
                        for b in range(2):
                            src = v_all[half, bass.ds(t, 1), b, h * HP:(h + 1) * HP, :].rearrange("p a i d -> p (a i) d")
                            last = nc.scalar.activation(v_bd[half, h, b, :, j, :], src, ACT.Copy)
                    last.then_inc(v_copied, 1)

                def exponent(t, h):
                    act.wait_ge(shift_ready, unit(t, h))
                    need(act, norm_ready, unit(t - 1, h))
                    nc.scalar.activation(probs[:, h, :], score_bank[h][:, :], ACT.Exp, scale=SCALE).then_inc(exp_ready, 1)

                def turned_copy(t, h):
                    act.wait_ge(turned, unit(t, h))
                    need(act, val_ready, unit(t - 1, h))
                    nc.scalar.activation(probs_t[:, h, :], prob_bank[h][:, :], ACT.Copy).then_inc(turned_copied, 1)

                def heads(t, h):
                    act.wait_ge(val_ready, unit(t, h))
                    need(act, out_ready, t)
                    for i in range(2, HP):
                        last = nc.scalar.activation(heads_part(h, i), value_part(h, i), ACT.Copy)
                    last.then_inc(heads_a, 1)

                def square(t):
                    act.wait_ge(out_copied, t + 1)
                    need(act, squared, t)
                    nc.scalar.activation(squares[:, :], proj_bank[:, 0:D], ACT.Square,
                                         accum_out=w["sq_sum"][:, bass.ds(t, 1)]).then_inc(squared, 1)

                def step(t):
                    if live(t - 1):
                        exponent(t - 1, 1)
                    if live(t + 1):
                        queries(t + 1, 0)
                    if live(t - 2):
                        turned_copy(t - 2, 1)
                        heads(t - 2, 0)
                    if live(t - 3):
                        square(t - 3)
                    if live(t - 1):
                        values(t - 1, 0)
                    if live(t):
                        exponent(t, 0)
                    if live(t - 2):
                        heads(t - 2, 1)
                    if live(t - 1):
                        turned_copy(t - 1, 0)
                    if live(t + 1):
                        queries(t + 1, 1)
                    if live(t - 1):
                        values(t - 1, 1)

                queries(0, 0)
                queries(0, 1)
                act.wait_ge(v_cleared, 1)
                every_pair(act, step)


def normalise(nc, w):
    with ExitStack() as scope:
        s = Memory(nc, scope, "norm_")
        bank = s.banks(4)
        ms, root, inv = s.sb("ms", [P, PAIRS]), s.sb("root", [P, PAIRS]), s.sb("inv", [P, PAIRS])
        scaled = s.sb("scaled", [P, 2, TILES, D])
        gained = s.sb("gained", [P, 2, KT, CH])
        part_max = s.sb("part_max", [P, CHUNKS])
        top = s.sb("top", [P, 2])
        nan_sum = s.sb("nan_sum", [P, 1])
        names = ("dve", "ms_ready", "root_ready", "inv_ready", "scaled_ready", "turned", "gained_ready", "shifted",
                 "max_ready", "top_ready", "all_ready")
        (dve, ms_ready, root_ready, inv_ready, scaled_ready, turned, gained_ready, shifted,
         max_ready, top_ready, all_ready) = (s.sem(n) for n in names)
        big = w["big"]
        out_all = big[:, 0:KT * TOK].rearrange("p (t n) -> p t n", t=PAIRS)
        xn = big[:, 2 * KT * TOK:3 * KT * TOK].rearrange("p (c k n) -> p c k n", c=CHUNKS, k=KT)

        def chunks(engine, body):
            body(0, 0)
            body(1, 1)
            with engine.Fori(1, CHUNKS // 2) as i:
                body(2 * i, 0)
                body(2 * i + 1, 1)

        with nc.Block() as block:

            @block.scalar
            def _(act):
                act.wait_ge(ms_ready, 1)
                nc.scalar.activation(root[:, :], ms[:, :], ACT.Sqrt).then_inc(root_ready, 1)
                act.wait_ge(inv_ready, 1)

                def body(c, k):
                    need(act, turned, (c - 1) * KT)
                    for t in range(TILES):
                        at = c * TILES + t
                        last = nc.scalar.activation(scaled[:, k, t, :], out_all[:, bass.ds(at, 1), :].rearrange("p a n -> p (a n)"),
                                                    ACT.Copy, scale=inv[:, bass.ds(at, 1)])
                    last.then_inc(scaled_ready, 1)

                chunks(act, body)

            @block.tensor
            def _(pe):
                def body(c, k):
                    pe.wait_ge(scaled_ready, c + 1)
                    for f in range(KT):
                        need(pe, gained_ready, (c - 2) * KT + f + 1)
                        for t in range(TILES):
                            last = nc.tensor.transpose(bank[2 * k + f][:, t * P:(t + 1) * P], scaled[:, k, t, f * P:(f + 1) * P],
                                                       w["ident"][:, :])
                        last.then_inc(turned, 1)

                chunks(pe, body)

            @block.vector
            def _(v):
                me = Order(v, dve)
                nc.vector.tensor_scalar(ms[:, :], w["sq_sum"][:, :], 1.0 / D, EPS_RMS, ALU.mult, ALU.add).then_inc(ms_ready, 1)
                v.wait_ge(root_ready, 1)
                me.link(nc.vector.reciprocal(inv[:, :], root[:, :]))
                me.link(nc.vector.tensor_tensor(ms[:, :], ms[:, :], inv[:, :], ALU.mult))
                me.link(nc.vector.tensor_tensor(root[:, :], root[:, :], ms[:, :], ALU.add))
                me.link(nc.vector.tensor_scalar(root[:, :], root[:, :], 0.5, None, ALU.mult))
                me.link(nc.vector.reciprocal(inv[:, :], root[:, :]))
                nc.vector.tensor_scalar(inv[:, :], inv[:, :], w["no_key"][:, 0:1], None, ALU.add).then_inc(inv_ready, 1)

                def body(c, k):
                    for f in range(KT):
                        v.wait_ge(turned, c * KT + f + 1)
                        need(v, shifted, (c - 2) * KT + f + 1)
                        nc.vector.tensor_tensor(gained[:, k, f, :].rearrange("p (b t) -> p b t", t=SEQ),
                                                bank[2 * k + f][:, :].rearrange("p (b t) -> p b t", t=SEQ),
                                                bcast_last(w["gain"][:, f, bass.ds(c * CB, CB)], SEQ),
                                                ALU.mult).then_inc(gained_ready, 1)
                    if not isinstance(c, int) or c > 0:
                        largest(c - 1)

                def largest(c):
                    v.wait_ge(shifted, (c + 1) * KT)
                    nc.vector.tensor_reduce(part_max[:, bass.ds(c, 1)], xn[:, bass.ds(c, 1), :, :].rearrange("p a k n -> p (a k n)"),
                                            AX_X, ALU.max, apply_absolute_value=True).then_inc(max_ready, 1)

                chunks(v, body)
                largest(CHUNKS - 1)
                v.wait_ge(max_ready, CHUNKS)
                nc.vector.tensor_reduce(top[:, 0:1], part_max[:, :], AX_X, ALU.max).then_inc(top_ready, 1)
                v.wait_ge(all_ready, 2)
                me.link(nc.vector.tensor_tensor(top[:, 1:2], top[:, 1:2], nan_sum[:, :], ALU.add))
                quant_scale(nc, me, w, top[:, 1:2], 0)

            @block.gpsimd
            def _(pool):
                def body(c, k):
                    for f in range(KT):
                        pool.wait_ge(gained_ready, c * KT + f + 1)
                        nc.gpsimd.tensor_tensor(xn[:, bass.ds(c, 1), f, :].rearrange("p a (b t) -> p (a b) t", t=SEQ),
                                                gained[:, k, f, :].rearrange("p (b t) -> p b t", t=SEQ),
                                                bcast_last(w["shift"][:, f, bass.ds(c * CB, CB)], SEQ),
                                                ALU.add).then_inc(shifted, 1)

                chunks(pool, body)
                nc.gpsimd.partition_all_reduce(nan_sum[:, :], w["no_key"][:, :], P, RADD).then_inc(all_ready, 1)
                pool.wait_ge(top_ready, 1)
                nc.gpsimd.partition_all_reduce(top[:, 1:2], top[:, 0:1], P, RMAX).then_inc(all_ready, 1)


def quant_scale(nc, me, w, largest, which):
    scale, inv = w["quant"][:, 2 * which:2 * which + 1], w["quant"][:, 2 * which + 1:2 * which + 2]
    me.link(nc.vector.tensor_scalar(scale, largest, w["clips"][:, which:which + 1], 1.0 / QMAX, ALU.mult, ALU.mult))
    me.link(nc.vector.reciprocal(inv, scale))
    at = slice(0, 2 * MT) if which == 0 else slice(2 * MT, 2 * MT + KT)
    me.link(nc.vector.tensor_scalar(w["out_scale"][:, at], w["row_scale"][:, at], scale, None, ALU.mult))


def ffn_in(nc, w):
    with ExitStack() as scope:
        s = Memory(nc, scope, "ffi_")
        bank = s.banks(6)
        gate_bank, up_bank = bank[0:3], bank[3:6]
        shifted = s.sb("shifted", [P, 2, KT, CH])
        xq = s.sb("xq", [P, 2, KT, CH], BF16)
        silu = s.sb("silu", [P, MT, CH])
        up = s.sb("up", [P, 2, CH])
        part_max = s.sb("part_max", [P, CHUNKS, MT])
        top = s.sb("top", [P, 2])
        names = ("magic_added", "clipped", "xq_ready", "gate_ready", "up_ready", "silu_ready", "up_copied",
                 "h_ready_v", "h_ready_g", "max_ready", "top_ready", "all_ready", "dve")
        (magic_added, clipped, xq_ready, gate_ready, up_ready, silu_ready, up_copied,
         h_ready_v, h_ready_g, max_ready, top_ready, all_ready, dve) = (s.sem(n) for n in names)
        big = w["big"]
        h_all = big[:, :].rearrange("p (c m n) -> p c m n", c=CHUNKS, m=MT)
        xn = big[:, 2 * KT * TOK:3 * KT * TOK].rearrange("p (c k n) -> p c k n", c=CHUNKS, k=KT)
        OF_V, OF_G = (0, 2, 3, 5), (1, 4)

        def rows(i):
            return P if i < MT - 1 else TAIL

        def h_of(c, i):
            return h_all[0:rows(i), bass.ds(c, 1), i, :].rearrange("p a n -> p (a n)")

        def wait_h(engine, c, i):
            if i in OF_V:
                need(engine, h_ready_v, c * len(OF_V) + OF_V.index(i) + 1)
            else:
                need(engine, h_ready_g, c * len(OF_G) + OF_G.index(i) + 1)

        def live(c):
            return not isinstance(c, int) or c < CHUNKS

        def chunks(engine, body):
            body(0, 0)
            body(1, 1)
            with engine.Fori(1, CHUNKS // 2 - 1) as i:
                body(2 * i, 0)
                body(2 * i + 1, 1)
            body(CHUNKS - 2, 0)
            body(CHUNKS - 1, 1)

        with nc.Block() as block:

            @block.scalar
            def _(act):
                def shift(c, k):
                    need(act, xq_ready, c - 1)
                    nc.scalar.activation(shifted[:, k, :, :], xn[:, bass.ds(c, 1), :, :].rearrange("p a k n -> p (a k) n"),
                                         ACT.Identity, scale=w["quant"][:, 1:2], bias=w["magic"][:, 0:1]).then_inc(magic_added, 1)

                def body(c, k):
                    for i in range(MT):
                        act.wait_ge(gate_ready, c * MT + i + 1)
                        wait_h(act, c - 1, i)
                        nc.scalar.activation(silu[0:rows(i), i, :], gate_bank[i % 3][0:rows(i), :], ACT.Silu,
                                             scale=w["out_scale"][0:rows(i), i:i + 1]).then_inc(silu_ready, 1)
                        if i in OF_G:
                            act.wait_ge(up_ready, c * MT + i + 1)
                            nc.scalar.activation(up[:, OF_G.index(i), :], up_bank[i % 3][:, :], ACT.Copy,
                                                 scale=w["out_scale"][:, MT + i:MT + i + 1]).then_inc(up_copied, 1)
                        if i == 2 and live(c + 2):
                            shift(c + 2, k)

                shift(0, 0)
                shift(1, 1)
                chunks(act, body)

            @block.tensor
            def _(pe):
                def body(c, k):
                    pe.wait_ge(xq_ready, c + 1)
                    for i in range(MT):
                        for side in range(2):
                            if side == 0:
                                out, ready = gate_bank, gate_ready
                                need(pe, silu_ready, c * MT + i - 2)
                            else:
                                out, ready = up_bank, up_ready
                                if i in OF_G:
                                    need(pe, up_copied, c * len(OF_G) + OF_G.index(i))
                                else:
                                    need(pe, h_ready_v, c * len(OF_V) + OF_V.index(i) - 1)
                            for f in range(KT):
                                at = (f * 2 * MT + side * MT + i) * P
                                last = nc.tensor.matmul(out[i % 3][0:rows(i), :], w["gu_t"][:, at:at + rows(i)],
                                                        xq[:, k, f, :], start=f == 0, stop=f == KT - 1)
                            last.then_inc(ready, 1)

                chunks(pe, body)

            @block.vector
            def _(v):
                def clip(c, k):
                    v.wait_ge(magic_added, c + 1)
                    nc.vector.tensor_scalar(shifted[:, k, :, :], shifted[:, k, :, :], MAGIC + QMAX, MAGIC - QMAX - 1,
                                            ALU.min, ALU.max).then_inc(clipped, 1)

                def multiply(c, i):
                    v.wait_ge(silu_ready, c * MT + i + 1)
                    v.wait_ge(up_ready, c * MT + i + 1)
                    nc.vector.scalar_tensor_tensor(h_of(c, i), up_bank[i % 3][0:rows(i), :],
                                                   w["out_scale"][0:rows(i), MT + i:MT + i + 1], silu[0:rows(i), i, :],
                                                   ALU.mult, ALU.mult).then_inc(h_ready_v, 1)

                def largest(c, i):
                    wait_h(v, c, i)
                    nc.vector.tensor_reduce(part_max[0:rows(i), bass.ds(c, 1), i], h_of(c, i), AX_X, ALU.max,
                                            apply_absolute_value=True).then_inc(max_ready, 1)

                def body(c, k):
                    if live(c + 1):
                        clip(c + 1, 1 - k)
                    multiply(c, 0)
                    if not isinstance(c, int) or c > 0:
                        largest(c - 1, 5)
                        largest(c - 1, 4)
                    largest(c, 0)
                    multiply(c, 2)
                    multiply(c, 3)
                    largest(c, 2)
                    largest(c, 1)
                    multiply(c, 5)
                    largest(c, 3)

                me = Order(v, dve)
                me.link(nc.vector.memset(part_max[:, :, :], 0.0))
                clip(0, 0)
                chunks(v, body)
                largest(CHUNKS - 1, 5)
                largest(CHUNKS - 1, 4)
                v.wait_ge(max_ready, CHUNKS * MT)
                nc.vector.tensor_reduce(top[:, 0:1], part_max[:, :, :].rearrange("p c m -> p (c m)"), AX_X,
                                        ALU.max).then_inc(top_ready, 1)
                v.wait_ge(all_ready, 1)
                quant_scale(nc, me, w, top[:, 1:2], 1)

            @block.gpsimd
            def _(pool):
                def integers(c, k):
                    pool.wait_ge(clipped, c + 1)
                    need(pool, up_ready, (c - 1) * MT)
                    nc.gpsimd.tensor_tensor(xq[:, k, :, :], shifted[:, k, :, :], bcast_last(w["magic"][:, 0:1].to_broadcast([P, KT]), CH),
                                            ALU.subtract).then_inc(xq_ready, 1)

                def body(c, k):
                    if live(c + 1):
                        integers(c + 1, 1 - k)
                    for i in OF_G:
                        pool.wait_ge(silu_ready, c * MT + i + 1)
                        pool.wait_ge(up_copied, c * len(OF_G) + OF_G.index(i) + 1)
                        nc.gpsimd.tensor_tensor(h_of(c, i), up[:, OF_G.index(i), :], silu[:, i, :], ALU.mult).then_inc(h_ready_g, 1)

                integers(0, 0)
                chunks(pool, body)
                pool.wait_ge(top_ready, 1)
                nc.gpsimd.partition_all_reduce(top[:, 1:2], top[:, 0:1], P, RMAX).then_inc(all_ready, 1)


def ffn_out(nc, w, out):
    with ExitStack() as scope:
        s = Memory(nc, scope, "ffo_")
        bank = s.banks(4)
        HT = MT // 2
        hq = s.sb("hq", [P, 2, MT, CH], BF16)
        y = s.sb("y", [P, 2, KT, CH])
        names = ("magic_added", "clipped", "ints_v", "ints_g", "ints_a", "half_used", "down_ready", "y_ready")
        magic_added, clipped, ints_v, ints_g, ints_a, half_used, down_ready, y_ready = (s.sem(n) for n in names)
        stored = [s.sem("stored0"), s.sem("stored1")]
        h_all = w["big"][:, :].rearrange("p (c m n) -> p c m n", c=CHUNKS, m=MT)

        def h_of(c, first, last):
            return h_all[:, bass.ds(c, 1), first:last, :].rearrange("p a m n -> p (a m) n")

        def free(engine, c, half):
            if half == 0:
                need(engine, half_used, c - 1)
            else:
                need(engine, down_ready, (c - 1) * KT)

        def chunks(engine, body):
            body(0, 0, 0)
            body(1, 1, 0)
            with engine.Fori(1, CHUNKS // 2) as i:
                body(2 * i, 0, i)
                body(2 * i + 1, 1, i)

        with nc.Block() as block:

            @block.scalar
            def _(act):
                def shift(c, half):
                    h = h_of(c, half * HT, (half + 1) * HT)
                    nc.scalar.activation(h, h, ACT.Identity, scale=w["quant"][:, 3:4],
                                         bias=w["magic"][:, 0:1]).then_inc(magic_added, 1)

                def integers(c, k):
                    act.wait_ge(clipped, 2 * c + 1)
                    free(act, c, 0)
                    nc.scalar.activation(hq[:, k, 2:3, :], h_of(c, 2, 3), ACT.Copy, bias=-MAGIC).then_inc(ints_a, 1)

                def body(c, k, i):
                    shift(c, 1)
                    integers(c, k)
                    if not isinstance(c, int) or c + 1 < CHUNKS:
                        shift(c + 1, 0)

                shift(0, 0)
                body(0, 0, 0)
                body(1, 1, 0)
                with act.Fori(1, CHUNKS // 2 - 1) as i:
                    body(2 * i, 0, i)
                    body(2 * i + 1, 1, i)
                body(CHUNKS - 2, 0, 0)
                body(CHUNKS - 1, 1, 0)

            @block.gpsimd
            def _(pool):
                def body(c, k, i):
                    for half in range(2):
                        pool.wait_ge(clipped, 2 * c + half + 1)
                        free(pool, c, half)
                        j, to = half * HT + 1, 2 * HT if half == 1 else 2
                        nc.gpsimd.tensor_tensor(hq[:, k, j:to, :], h_of(c, j, to),
                                                bcast_last(w["magic"][:, 0:1].to_broadcast([P, to - j]), CH),
                                                ALU.subtract).then_inc(ints_g, 1)

                chunks(pool, body)

            @block.vector
            def _(v):
                def quantise(c, k, half):
                    v.wait_ge(magic_added, 2 * c + half + 1)
                    h = h_of(c, half * HT, (half + 1) * HT)
                    nc.vector.tensor_scalar(h, h, MAGIC + QMAX, MAGIC - QMAX - 1, ALU.min, ALU.max).then_inc(clipped, 1)
                    v.wait_ge(clipped, 2 * c + half + 1)
                    free(v, c, half)
                    nc.vector.tensor_scalar(hq[:, k, half * HT:half * HT + 1, :], h_of(c, half * HT, half * HT + 1),
                                            MAGIC, None, ALU.subtract).then_inc(ints_v, 1)

                def finish(c, k, i):
                    need(v, stored[k], 16 * i)
                    for f in range(KT):
                        v.wait_ge(down_ready, c * KT + f + 1)
                        at = 2 * MT + f
                        nc.vector.scalar_tensor_tensor(y[:, k, f, :], bank[2 * k + f][:, :], w["out_scale"][:, at:at + 1],
                                                       w["x"][:, f, bass.ds(c * CH, CH)], ALU.mult, ALU.add).then_inc(y_ready, 1)

                quantise(0, 0, 0)
                quantise(0, 0, 1)
                quantise(1, 1, 0)
                quantise(1, 1, 1)
                finish(0, 0, 0)
                quantise(2, 0, 0)
                quantise(2, 0, 1)
                finish(1, 1, 0)
                with v.Fori(2, CHUNKS // 2) as i:
                    quantise(2 * i - 1, 1, 0)
                    quantise(2 * i - 1, 1, 1)
                    finish(2 * i - 2, 0, i - 1)
                    quantise(2 * i, 0, 0)
                    quantise(2 * i, 0, 1)
                    finish(2 * i - 1, 1, i - 1)
                quantise(CHUNKS - 1, 1, 0)
                quantise(CHUNKS - 1, 1, 1)
                finish(CHUNKS - 2, 0, CHUNKS // 2 - 1)
                finish(CHUNKS - 1, 1, CHUNKS // 2 - 1)

            @block.tensor
            def _(pe):
                def body(c, k, i):
                    for half in range(2):
                        pe.wait_ge(ints_v, 2 * c + half + 1)
                        pe.wait_ge(ints_g, 2 * c + half + 1)
                        if half == 0:
                            pe.wait_ge(ints_a, c + 1)
                        for f in range(KT):
                            if half == 0:
                                need(pe, y_ready, (c - 2) * KT + f + 1)
                            for j in range(half * HT, (half + 1) * HT):
                                at = (j * KT + f) * P
                                last = nc.tensor.matmul(bank[2 * k + f][:, :], w["down_t"][:, at:at + P], hq[:, k, j, :],
                                                        start=j == 0, stop=j == MT - 1)
                            if half == 1:
                                last.then_inc(down_ready, 1)
                        if half == 0:
                            last.then_inc(half_used, 1)

                chunks(pe, body)

            @block.sync
            def _(sp):
                def body(c, k, i):
                    sp.wait_ge(y_ready, (c + 1) * KT)
                    sp.dma_start(out[bass.ds(c, 1)].rearrange("a p k n -> p (a k) n"), y[:, k, :, :]).then_inc(stored[k], 16)

                chunks(sp, body)
                sp.wait_ge(stored[0], 16 * CHUNKS // 2)
                sp.wait_ge(stored[1], 16 * CHUNKS // 2)


def build(nc, io, out):
    with ExitStack() as whole:
        m = Memory(nc, whole, "")
        x_all = m.sb("x_all", [P, KT, TOK])
        big = m.sb("big", [P, CHUNKS * MT * CH])
        big_end = nc.sbuf_base
        w = {
            "x": x_all,
            "big": big,
            "ident": m.sb("ident", [P, P]),
            "ident_b": m.sb("ident_b", [P, P], BF16),
            "magic": m.sb("magic", [P, 1]),
            "clips": m.sb("clips", [P, 2]),
            "quant": m.sb("quant", [P, 4]),
            "row_scale": m.sb("row_scale", [P, 2 * MT + KT]),
            "out_scale": m.sb("out_scale", [P, 2 * MT + KT]),
            "gain": m.sb("gain", [P, KT, BATCH]),
            "shift": m.sb("shift", [P, KT, BATCH]),
            "no_key": m.sb("no_key", [P, 1]),
            "mask_neg": m.sb("mask_neg", [P, SEQ], BF16),
            "heads": m.sb("heads", [P, HH]),
            "sq_sum": m.sb("sq_sum", [P, PAIRS]),
            "gu_t": m.sb("gu_t", [P, KT * 2 * MT * P], BF16),
            "down_t": m.sb("down_t", [P, MT * KT * P], BF16),
            "wo": m.sb("wo", [P, KT, D]),
        }
        with ExitStack() as first:
            f = Memory(nc, first, "")
            w |= {
                "hid": nc.alloc_sbuf_tensor_at("hid", [P, TOK], F32R, offset=big_end - 4 * TOK),
                "mix_high": f.sb("mix_high", [P, P], F32R),
                "mix_low": f.sb("mix_low", [P, P], F32R),
                "rw_high": f.sb("rw_high", [P, P], F32R),
                "rw_low": f.sb("rw_low", [P, P], F32R),
                "w1_high": f.sb("w1_high", [P, NE * P], F32R),
                "w1_low": f.sb("w1_low", [P, NE * P], F32R),
                "w2_high": f.sb("w2_high", [P, NE, D], F32R),
                "w2_low": f.sb("w2_low", [P, NE, D], F32R),
                "b1": f.sb("b1", [P, NE]),
                "rb": f.sb("rb", [P, 1]),
                "b2_high": f.sb("b2_high", [P, D], F32R),
                "select": f.sb("select", [P, NE], F32R),
                "gate_high": f.sb("gate_high", [P, CHUNKS * TILES, NE], F32R),
                "gate_low": f.sb("gate_low", [P, CHUNKS * TILES, NE], F32R),
                "mask_pad": f.sb("mask_pad", [P, TILES, 4, 32]),
                "spec": f.sb("spec", [P, BATCH]),
                "rank": f.sb("rank", [P, BATCH]),
                "prio": f.sb("prio", [P, NE]),
                "below": f.sb("below", [R, R]),
                "wq": f.sb("wq", [P, 2, KT, D], F32R),
                "wk": f.sb("wk", [P, 2, KT, D], F32R),
                "wv": f.sb("wv", [P, 2, KT, D], F32R),
            }
            prepare(nc, w, io)
            route(nc, w)
            experts(nc, w)
        attention(nc, w)
        normalise(nc, w)
        ffn_in(nc, w)
        ffn_out(nc, w, out)


def kernel(**inputs):
    import numpy as np
    import concourse.bacc as bacc
    from concourse.bass_utils import run_bass_kernel_spmd

    a = {name: np.asarray(value) for name, value in inputs.items()}

    def tiles(x):
        return x.reshape(-1, P, x.shape[-1]).transpose(1, 0, 2)

    main = (MT - 1) * P
    gate, up = a["L1_ffn_w_gate"], a["L1_ffn_w_up"]
    row = np.arange(P)
    select = np.zeros((P, NE), np.float32)
    for n in range(NE):
        select[[n, 64 + n], n] = 1.0
    arrays = {
        "x": a["x"].reshape(CHUNKS, CH, KT, P).transpose(0, 3, 2, 1),
        "cond_t": a["cond_256"].T,
        "rank_t": a["cond_64"].T,
        "raw": a["L0_cond_mode_to_rank"],
        "raw_t": a["L0_cond_mode_to_rank"].T,
        "ib_t": tiles(a["L0_cond_input_basis"].T),
        "ob_t": tiles(a["L0_cond_output_basis"].T),
        "rw": tiles(a["L0_ffn_router_w"]),
        "rb": a["L0_ffn_router_b"].reshape(NE, 1),
        "w1": tiles(a["L0_ffn_W1"].transpose(1, 0, 2).reshape(D, NE * P)),
        "b1": a["L0_ffn_b1"].T,
        "w2": a["L0_ffn_W2"].transpose(1, 0, 2),
        "b2": a["L0_ffn_b2"],
        "wq": tiles(a["L1_cond_Wq"].T),
        "wk": tiles(a["L1_cond_Wk"].T),
        "wv": tiles(a["L1_cond_Wv"].T),
        "wo": tiles(a["L1_cond_Wo"].T),
        "wc_t": a["L1_cond_Wc"].T.reshape(R, 4, P),
        "bc": a["L1_cond_bc"].reshape(4, P).T,
        "rms_w": a["L1_cond_rms_scale"].reshape(KT, P).T,
        "mask": a["mask_SxS_bk1"],
        "clips": np.concatenate([a["L1_ffn_clip_x"], a["L1_ffn_clip_down"]]),
        "gate": tiles(gate[:main]),
        "gate_tail": gate[main:],
        "up": tiles(up[:main]),
        "up_tail": up[main:],
        "down": tiles(a["L1_ffn_w_down"]),
        "ident": np.eye(P, dtype=np.float32),
        "below": -np.tril(np.ones((R, R), np.float32), -1),
        "heads": (row[:, None] // DH == np.arange(HH)[None, :]).astype(np.float32),
        "prio": np.ascontiguousarray(np.broadcast_to(np.arange(NE, 0, -1, dtype=np.float32), (P, NE))),
        "select": select,
    }
    nc = bacc.Bacc("TRN2", target_bir_lowering=False, num_devices=1)
    arrays = {f"in_{name}": np.ascontiguousarray(value) for name, value in arrays.items()}
    io = {name[3:]: nc.dram_tensor(name, v.shape, mybir.dt.from_np(v.dtype), kind="ExternalInput").ap()
          for name, v in arrays.items()}
    out = nc.dram_tensor("out", (CHUNKS, P, KT, CH), F32, kind="ExternalOutput").ap()
    build(nc, io, out)
    r = run_bass_kernel_spmd(nc, [arrays], core_ids=[0])
    y = r.results[0]["out"]
    return y.transpose(0, 3, 2, 1).reshape(BATCH, SEQ, D)
```

```python
from contextlib import ExitStack

import concourse.bass as bass
from concourse import mybir

F32 = mybir.dt.float32
F32R = mybir.dt.float32r
BF16 = mybir.dt.bfloat16
U8 = mybir.dt.uint8
ALU = mybir.AluOpType
ACT = mybir.ActivationFunctionType
AX_X = mybir.AxisListType.X
RMAX = bass.bass_isa.ReduceOp.max
RADD = bass.bass_isa.ReduceOp.add

P = 128
D = 256
KT = D // P
BATCH = 64
SEQ = 64
TOK = BATCH * SEQ
CH = 512
CHUNKS = TOK // CH
CB = CH // SEQ
TILES = CH // P
R = 64
NE = 8
HEADS = 16
DH = D // HEADS
HH = HEADS // KT
HP = HH // 2
PAIRS = BATCH // 2
FF = 704
MT = -(-FF // P)
TAIL = FF - (MT - 1) * P
EPS_GRAM = 1e-4
EPS_RMS = 1e-6
SCALE = DH ** -0.5
QMAX = 127.0
MAGIC = 12582912.0
MASKED = -2.0 ** 127


class Order:

    def __init__(self, engine, sem, base=0):
        self.engine, self.sem, self.base, self.n = engine, sem, base, 0

    def add(self, instruction):
        self.n += 1
        instruction.then_inc(self.sem, 1)
        return self.n

    def wait(self, n=None):
        self.engine.wait_ge(self.sem, self.base + (self.n if n is None else n))

    def link(self, instruction):
        self.add(instruction)
        self.wait()


def need(engine, sem, value):
    if not isinstance(value, int) or value > 0:
        engine.wait_ge(sem, value)


def bcast_mid(ap, n):
    return ap.unsqueeze(1).to_broadcast([ap.shape[0], n, ap.shape[1]])


def bcast_last(ap, n):
    return ap.unsqueeze(2).to_broadcast([ap.shape[0], ap.shape[1], n])


class Memory:

    def __init__(self, nc, scope, prefix):
        self.nc, self.scope, self.prefix = nc, scope, prefix

    def sb(self, name, shape, dt=F32):
        return self.scope.enter_context(self.nc.sbuf_tensor(self.prefix + name, shape, dt))

    def banks(self, n):
        return [self.scope.enter_context(self.nc.psum_tensor(f"{self.prefix}bank{i}", [P, CH], F32)) for i in range(n)]

    def sem(self, name):
        return self.scope.enter_context(self.nc.semaphore(self.prefix + name))


def prepare(nc, w, io):
    with ExitStack() as scope:
        s = Memory(nc, scope, "prep_")
        bank = s.banks(8)
        raw, raw_t = s.sb("raw", [R, R]), s.sb("raw_t", [R, R])
        elim = s.sb("elim", [R, 2 * R])
        second = s.sb("second", [R, R + 2])
        col = s.sb("col", [R, 8])
        q_t = s.sb("q_t", [R, 2, R])
        inv_t = s.sb("inv_t", [R, R])
        scratch = s.sb("scratch", [R, R])
        ib_t = s.sb("ib_t", [P, KT, 2, R])
        ob_t = s.sb("ob_t", [P, KT, 2, R])
        proj = s.sb("proj", [P, CH])
        b2_pad = s.sb("b2_pad", [P, D])
        cond = s.sb("cond", [R, BATCH])
        wc_t = s.sb("wc_t", [R, 4, P])
        bc = s.sb("bc", [P, 4])
        rms_w = s.sb("rms_w", [P, KT])
        mask8 = s.sb("mask8", [P, SEQ], U8)
        maskf = s.sb("maskf", [P, SEQ])
        count = s.sb("count", [P, 2])
        select = s.sb("select", [P, NE])

        used = 0

        def carve(n):
            nonlocal used
            used += n
            assert used <= 3 * KT * TOK - TOK
            return w["big"][:, used - n:used]

        rows_gu = carve(2 * MT * D).rearrange("p (m h) -> p m h", h=D)
        rows_d = carve(KT * FF).rearrange("p (m h) -> p m h", h=FF)
        int_gu = carve(MT * D).bitcast(BF16).rearrange("p (m h) -> p m h", h=D)
        int_d = carve(MT * P).bitcast(BF16).rearrange("p (m i) -> p m i", m=KT)
        w1 = carve(KT * NE * P).rearrange("p (k n) -> p k n", k=KT)
        rw = carve(KT * P).rearrange("p (k n) -> p k n", k=KT)
        w2_raw = carve(NE * D).rearrange("p (n d) -> p n d", n=NE)
        qkv_raw = carve(3 * KT * D).rearrange("p (i k n) -> p i k n", i=3, k=KT)
        absmax = s.sb("absmax", [P, 2 * MT + KT])
        inv = s.sb("inv", [P, 2 * MT + KT])

        ld_chol, ld_const, ld_proj, ld_fold = s.sem("ld_chol"), s.sem("ld_const"), s.sem("ld_proj"), s.sem("ld_fold")
        ld_raw_t, ld_b2, ld_split = s.sem("ld_raw_t"), s.sem("ld_b2"), s.sem("ld_split")
        split_high, split_low = s.sem("split_high"), s.sem("split_low")
        ld_mod, ld_ffn, ld_late = s.sem("ld_mod"), s.sem("ld_ffn"), s.sem("ld_late")
        ld_x = [s.sem(f"ld_x{c}") for c in range(CHUNKS)]
        pads_set, b2_set = s.sem("pads_set"), s.sem("b2_set")
        dve = s.sem("dve")
        gram_ready, row_ready, row_used = s.sem("gram_ready"), s.sem("row_ready"), s.sem("row_used")
        proj_ready, proj_scaled, proj_high, proj_low = (s.sem(n) for n in ("proj_ready", "proj_scaled", "proj_high", "proj_low"))
        fold_ready, fold_high, fold_used = (s.sem(n) for n in ("fold_ready", "fold_high", "fold_used"))
        silu_ready, mod_ready = s.sem("silu_ready"), s.sem("mod_ready")
        inv_ready, shifted, clipped, ints_ready, turned, turned_used = (
            s.sem(n) for n in ("inv_ready", "shifted", "clipped", "ints_ready", "turned", "turned_used"))
        chol_done, root_ready, m_turned, m_copied, q_ready, q_signed, q_turned = (
            s.sem(n) for n in ("chol_done", "root_ready", "m_turned", "m_copied", "q_ready", "q_signed", "q_turned"))
        ident = w["ident"]
        row_bank, proj_bank = (bank[0], bank[5]), (bank[1], bank[7])
        quant_parts = [(rows_gu[:, 4 * i:4 * i + 4, :], int_gu[:, 4 * i:4 * i + 4, :], 4 * i + 4) for i in range(3)]
        quant_parts += [(rows_d[:, i, :], int_d[:, i, 0:FF], 2 * MT + i + 1) for i in range(KT)]
        slots = [("project", 0), ("project", 1), ("fold", 0), ("fold", 1), ("project", 2), ("fold", 2), ("modulation", 0),
                 ("project", 3), ("project", 4), ("project", 5), ("project", 6), ("project", 7)]
        at, slot_of = 0, {}
        for kind, n in slots:
            slot_of[kind, n] = at
            at += 1 if kind == "modulation" or (kind, n) == ("fold", 0) else TILES
        for i in range(5):
            slot_of["turn", i] = at + 2 * i
        FIRST_SLOT = 12

        with nc.Block() as block:

            @block.sync
            def _(sp):
                sp.dma_start(raw[:, :], io["raw"]).then_inc(ld_chol, 16)
                sp.dma_start(ident[:, :], io["ident"]).then_inc(ld_chol, 16)
                sp.dma_start(w["below"][:, :], io["below"]).then_inc(ld_chol, 16)
                for i in range(2):
                    half = slice(i * R, (i + 1) * R)
                    sp.dma_start(ib_t[:, :, i, :], io["ib_t"]).then_inc(ld_proj, 16)
                    sp.dma_start(w["spec"][half, :], io["cond_t"]).then_inc(ld_proj, 16)
                for c in range(CHUNKS):
                    if c == 2:
                        sp.dma_start(raw_t[:, :], io["raw_t"]).then_inc(ld_raw_t, 16)
                        sp.wait_ge(ld_ffn, 16 * 7)
                    sp.dma_start(w["x"][:, :, c * CH:(c + 1) * CH], io["x"][c]).then_inc(ld_x[c], 16)
                sp.dma_start(w2_raw, io["w2"]).then_inc(ld_split, 16)
                for i, name in enumerate(("wq", "wk", "wv")):
                    sp.dma_start(qkv_raw[:, i, :, :], io[name]).then_inc(ld_split, 16)
                sp.dma_start(w["wo"][:, :, :], io["wo"]).then_inc(ld_late, 16)
                sp.wait_ge(ld_late, 16)

            @block.gpsimd
            def _(pool):
                nc.gpsimd.memset(b2_pad[:, :], 0.0).then_inc(b2_set, 1)
                nc.gpsimd.memset(w["rb"][:, :], 0.0).then_inc(pads_set, 1)
                nc.gpsimd.memset(rw[:, :, :], 0.0).then_inc(pads_set, 1)
                nc.gpsimd.memset(rows_gu[:, MT - 1, :], 1.0).then_inc(pads_set, 1)
                nc.gpsimd.memset(rows_gu[:, 2 * MT - 1, :], 1.0).then_inc(pads_set, 1)
                nc.gpsimd.memset(int_d[:, :, FF:MT * P], 0.0).then_inc(pads_set, 1)
                nc.gpsimd.memset(w["magic"][:, :], MAGIC).then_inc(pads_set, 1)
                nc.gpsimd.memset(w["mask_pad"][:, :, :, :], 0.0).then_inc(pads_set, 1)
                pool.wait_ge(b2_set, 1)
                for g in range(4):
                    pool.dma_start(b2_pad[32 * g:32 * g + NE, :], io["b2"]).then_inc(ld_b2, 16)
                def low(c):
                    if c == 0:
                        pool.wait_ge(pads_set, 7)
                    if c == 7:
                        pool.wait_ge(split_low, 1)
                    pool.wait_ge(proj_high, c + 1)
                    part = w["hid"][R:P, c * CH:(c + 1) * CH]
                    nc.gpsimd.tensor_tensor(part, proj[R:P, :], part.bitcast(F32), ALU.subtract).then_inc(proj_low, 1)

                for c in range(7):
                    low(c)
                pool.wait_ge(split_high, 1)
                pool.wait_ge(proj_low, 7)
                nc.gpsimd.tensor_tensor(w["w2_low"][:, :, :], w2_raw, w["w2_high"][:, :, :].bitcast(F32),
                                        ALU.subtract).then_inc(split_low, 1)
                low(7)
                pool.wait_ge(proj_low, 8)
                for i, name in enumerate(("wq", "wk", "wv")):
                    pool.wait_ge(split_high, 2 + i)
                    nc.gpsimd.tensor_tensor(w[name][:, 1, :, :], qkv_raw[:, i, :, :], w[name][:, 0, :, :].bitcast(F32),
                                            ALU.subtract).then_inc(split_low, 1)

            @block.scalar
            def _(act):
                act.wait_ge(pads_set, 7)
                for i in range(2):
                    half = slice(i * R, (i + 1) * R)
                    act.dma_start(w["rank"][half, :], io["rank_t"]).then_inc(ld_const, 16)
                    act.dma_start(ob_t[:, :, i, :], io["ob_t"]).then_inc(ld_fold, 16)
                act.dma_start(rw[:, :, 0:NE], io["rw"]).then_inc(ld_fold, 16)
                act.dma_start(w1[:, :, :], io["w1"]).then_inc(ld_fold, 16)
                act.dma_start(select[:, :], io["select"]).then_inc(ld_const, 16)
                act.dma_start(w["rb"][0:NE, :], io["rb"]).then_inc(ld_const, 16)
                act.dma_start(w["b1"][:, :], io["b1"]).then_inc(ld_const, 16)
                act.dma_start(w["heads"][:, :], io["heads"]).then_inc(ld_const, 16)
                act.dma_start(w["prio"][:, :], io["prio"]).then_inc(ld_const, 16)
                act.dma_start(cond[:, :], io["cond_t"]).then_inc(ld_mod, 16)
                act.dma_start(wc_t[:, :, :], io["wc_t"]).then_inc(ld_mod, 16)
                act.dma_start(bc[:, :], io["bc"]).then_inc(ld_mod, 16)
                act.dma_start(rms_w[:, :], io["rms_w"]).then_inc(ld_mod, 16)
                act.dma_start(w["clips"][:, :], io["clips"].partition_broadcast(P)).then_inc(ld_mod, 16)
                act.dma_start(rows_gu[:, 0:MT - 1, :], io["gate"]).then_inc(ld_ffn, 16)
                act.dma_start(rows_gu[0:TAIL, MT - 1, :], io["gate_tail"]).then_inc(ld_ffn, 16)
                act.dma_start(rows_gu[:, MT:2 * MT - 1, :], io["up"]).then_inc(ld_ffn, 16)
                act.dma_start(rows_gu[0:TAIL, 2 * MT - 1, :], io["up_tail"]).then_inc(ld_ffn, 16)
                act.dma_start(rows_d, io["down"]).then_inc(ld_ffn, 16)
                for i in range(2):
                    act.dma_start(mask8[i * SEQ:(i + 1) * SEQ, :], io["mask"]).then_inc(ld_ffn, 16)

                def project(c):
                    act.wait_ge(proj_scaled, c + 1)
                    nc.scalar.activation(w["hid"][:, c * CH:(c + 1) * CH], proj[:, :], ACT.Copy).then_inc(proj_high, 1)

                def fold(i):
                    act.wait_ge(fold_ready, i + 1)
                    n = P if i == 0 else CH
                    high = w["rw_high"][:, :] if i == 0 else w["w1_high"][:, (i - 1) * CH:i * CH]
                    nc.scalar.activation(high, bank[2 + i][:, 0:n], ACT.Copy).then_inc(fold_high, 1)

                def shift(tiles):
                    act.wait_ge(inv_ready, 1)
                    for i in tiles:
                        rows = rows_gu[:, i, :] if i < 2 * MT else rows_d[:, i - 2 * MT, :]
                        nc.scalar.activation(rows, rows, ACT.Identity, scale=inv[:, i:i + 1],
                                             bias=w["magic"][:, 0:1]).then_inc(shifted, 1)

                def split(name, i):
                    nc.scalar.activation(w[name][:, 0, :, :], qkv_raw[:, i, :, :], ACT.Copy).then_inc(split_high, 1)

                def integers(i):
                    rows, ints, _ = quant_parts[i]
                    act.wait_ge(clipped, i + 1)
                    nc.scalar.activation(ints, rows, ACT.Copy, bias=-MAGIC).then_inc(ints_ready, 1)

                project(0)
                project(1)
                fold(0)
                act.wait_ge(ld_mod, 16 * 5)
                nc.scalar.activation(cond[:, :], cond[:, :], ACT.Silu).then_inc(silu_ready, 1)
                nc.scalar.activation(w["clips"][:, :], w["clips"][:, :], ACT.Sigmoid).then_inc(silu_ready, 1)
                fold(1)
                project(2)
                fold(2)
                shift(range(0, 6))
                project(3)
                shift(range(6, 2 * MT))
                project(4)
                shift(range(2 * MT, 2 * MT + KT))
                act.wait_ge(ld_split, 16 * 4)
                nc.scalar.activation(w["w2_high"][:, :, :], w2_raw, ACT.Copy).then_inc(split_high, 1)
                project(5)
                split("wq", 0)
                integers(0)
                integers(1)
                project(6)
                split("wk", 1)
                integers(2)
                integers(3)
                integers(4)
                project(7)
                split("wv", 2)

                def turned_copy(i):
                    act.wait_ge(turned, i + 1)
                    n = 1024 if i < 4 else 512
                    dst = w["gu_t"][:, i * 1024:i * 1024 + n] if i < 3 else w["down_t"][:, (i - 3) * 1024:(i - 3) * 1024 + n]
                    nc.scalar.activation(dst, bank[3 + i % 2][:, 0:n // 2].bitcast(BF16), ACT.Copy).then_inc(turned_used, 1)

                for i in range(5):
                    turned_copy(i)
                act.wait_ge(chol_done, 1)
                nc.scalar.activation(col[:, 4:5], col[:, 3:4], ACT.Sqrt).then_inc(root_ready, 1)

            @block.tensor
            def _(pe):
                def project(c, q):
                    if q == 0:
                        pe.wait_ge(ld_x[c], 16)
                        if c == 0:
                            pe.wait_ge(ld_proj, 16 * 4)
                        need(pe, proj_scaled, c - 1)
                    cols = slice(q * P, (q + 1) * P)
                    for k in range(KT):
                        last = nc.tensor.matmul(proj_bank[c % 2][:, cols], ib_t[:, k, :, :].rearrange("p a r -> p (a r)"),
                                                w["x"][:, k, c * CH + q * P:c * CH + (q + 1) * P], start=k == 0, stop=k == KT - 1)
                    if q == TILES - 1:
                        last.then_inc(proj_ready, 1)

                def fold(i, q):
                    if i == 0:
                        pe.wait_ge(ld_fold, 16 * 4)
                    cols = slice(q * P, (q + 1) * P)
                    for k in range(KT):
                        rhs = rw[:, k, :] if i == 0 else w1[:, k, (i - 1) * CH + q * P:(i - 1) * CH + (q + 1) * P]
                        last = nc.tensor.matmul(bank[2 + i][:, cols], ob_t[:, k, :, :].rearrange("p a r -> p (a r)"), rhs,
                                                start=k == 0, stop=k == KT - 1)
                    if i == 0 or q == TILES - 1:
                        last.then_inc(fold_ready, 1)

                def modulation():
                    pe.wait_ge(fold_used, 1)
                    pe.wait_ge(silu_ready, 1)
                    for i in range(4):
                        last = nc.tensor.matmul(bank[2][:, i * BATCH:(i + 1) * BATCH], wc_t[:, i, :], cond[:, :],
                                                start=True, stop=True)
                    last.then_inc(mod_ready, 1)

                def turn(i):
                    pe.wait_ge(ints_ready, (2, 3, 3, 5, 5)[i])
                    if i >= 2:
                        pe.wait_ge(turned_used, i - 1)
                    if i < 2:
                        pe.wait_ge(fold_used, 2 + i)
                    out = bank[3 + i % 2][:, :].bitcast(BF16)
                    for b in range(8 if i < 4 else 4):
                        n = 8 * i + b
                        if i < 3:
                            src = int_gu[:, n % (2 * MT), (n // (2 * MT)) * P:(n // (2 * MT) + 1) * P]
                        else:
                            n -= 24
                            src = int_d[:, n % KT, (n // KT) * P:(n // KT + 1) * P]
                        last = nc.tensor.transpose(out[:, b * P:(b + 1) * P], src, w["ident_b"][:, :])
                    last.then_inc(turned, 1)

                pe.wait_ge(ld_chol, 16 * 3)
                nc.tensor.matmul(bank[0][0:R, 0:R], raw[:, :], raw[:, :], start=True, stop=True).then_inc(gram_ready, 1)
                def slot(n):
                    for c in range(CHUNKS):
                        if 0 <= n - slot_of["project", c] < TILES:
                            project(c, n - slot_of["project", c])
                    for i in range(3):
                        if 0 <= n - slot_of["fold", i] < (TILES if i else 1):
                            fold(i, n - slot_of["fold", i])
                    if n == slot_of["modulation", 0]:
                        modulation()
                    for i in range(5):
                        if n == slot_of["turn", i]:
                            turn(i)

                for j in range(0, R, 2):
                    pe.wait_ge(row_used, j // 2 + 1)
                    for i in range(2):
                        nc.tensor.matmul(row_bank[i][0:R, 0:R + 2],
                                         ident[0:R, j + i:j + i + 1].to_broadcast([R, R]),
                                         elim[:, j:j + R + 2], start=True, stop=True).then_inc(row_ready, 1)
                    slot(j - FIRST_SLOT)
                    slot(j - FIRST_SLOT + 1)
                pe.wait_ge(m_copied, 1)
                nc.tensor.transpose(bank[0][0:R, 0:R], elim[:, R:2 * R], ident[0:R, 0:R]).then_inc(m_turned, 1)
                pe.wait_ge(m_copied, 2)
                nc.tensor.matmul(bank[1][0:R, 0:R], inv_t[:, :], raw_t[:, :], start=True, stop=True).then_inc(q_ready, 1)
                pe.wait_ge(q_signed, 1)
                nc.tensor.transpose(bank[2][:, 0:R], q_t[:, :, :].rearrange("p a r -> p (a r)"),
                                    ident[0:R, 0:R]).then_inc(q_turned, 1)

            @block.vector
            def _(v):
                me = Order(v, dve)

                def scale(c):
                    v.wait_ge(proj_ready, c + 1)
                    if c:
                        v.wait_ge(proj_low, c)
                    nc.vector.tensor_tensor(proj[:, :].rearrange("p (b t) -> p b t", t=SEQ),
                                            proj_bank[c % 2][:, :].rearrange("p (b t) -> p b t", t=SEQ),
                                            bcast_last(w["spec"][:, c * CB:(c + 1) * CB], SEQ),
                                            ALU.mult).then_inc(proj_scaled, 1)

                def fold_low(i):
                    v.wait_ge(fold_high, i + 1)
                    n = P if i == 0 else CH
                    high = w["rw_high"][:, :] if i == 0 else w["w1_high"][:, (i - 1) * CH:i * CH]
                    out = w["rw_low"][:, :] if i == 0 else w["w1_low"][:, (i - 1) * CH:i * CH]
                    nc.vector.tensor_tensor(out, bank[2 + i][:, 0:n], high.bitcast(F32), ALU.subtract).then_inc(fold_used, 1)

                def modulation(i):
                    v.wait_ge(mod_ready, 1)
                    me.add(nc.vector.tensor_scalar(w["shift"][:, i, :], bank[2][:, i * BATCH:(i + 1) * BATCH], bc[:, i:i + 1],
                                                   None, ALU.add))
                    me.link(nc.vector.tensor_scalar(w["gain"][:, i, :], bank[2][:, (KT + i) * BATCH:(KT + i + 1) * BATCH],
                                                    bc[:, KT + i:KT + i + 1], 1.0, ALU.add, ALU.add))
                    me.add(nc.vector.tensor_scalar(w["gain"][:, i, :], w["gain"][:, i, :], rms_w[:, i:i + 1], None,
                                                   ALU.mult))

                def masks(i):
                    if i == 0:
                        me.link(nc.vector.tensor_copy(maskf[:, :], mask8[:, :]))
                        me.add(nc.vector.tensor_scalar(w["mask_neg"][:, :], maskf[:, :], MASKED, None, ALU.mult))
                        me.add(nc.vector.tensor_reduce(count[:, 0:1], maskf[:, :], AX_X, ALU.add))
                    else:
                        me.link(nc.vector.tensor_scalar(count[:, 0:1], count[:, 0:1], -1.0, float(SEQ), ALU.mult, ALU.add))
                        me.link(nc.vector.reciprocal(count[:, 1:2], count[:, 0:1]))
                        me.add(nc.vector.tensor_scalar(w["no_key"][:, :], count[:, 1:2], 0.0, None, ALU.mult))

                def largest(i):
                    if i == 0:
                        v.wait_ge(ld_ffn, 16 * 7)
                    out, rows = ((absmax[:, 2 * i:2 * i + 2], rows_gu[:, 2 * i:2 * i + 2, :]) if i < MT
                                 else (absmax[:, MT + i:MT + i + 1], rows_d[:, i - MT, :]))
                    me.add(nc.vector.tensor_reduce(out, rows, AX_X, ALU.max, apply_absolute_value=True))

                def row_scales():
                    me.wait()
                    me.link(nc.vector.tensor_scalar(w["row_scale"][:, :], absmax[:, :], 1.0 / QMAX, None, ALU.mult))
                    nc.vector.reciprocal(inv[:, :], w["row_scale"][:, :]).then_inc(inv_ready, 1)

                def clip(i):
                    rows, _, tiles = quant_parts[i]
                    v.wait_ge(shifted, tiles)
                    nc.vector.tensor_scalar(rows, rows, MAGIC + QMAX, MAGIC - QMAX - 1, ALU.min, ALU.max).then_inc(clipped, 1)

                def constants(i):
                    if i == 0:
                        v.wait_ge(ld_const, 16 * 7)
                        v.wait_ge(ld_b2, 16 * 4)
                        v.wait_ge(ld_raw_t, 16)
                        v.wait_ge(ld_proj, 16 * 4)
                        me.add(nc.vector.tensor_copy(w["select"][:, :], select[:, :]))
                        me.add(nc.vector.tensor_copy(w["b2_high"][:, :], b2_pad[:, :]))
                    else:
                        me.wait()
                        q = slice(32 * (2 * i - 1), 32 * 2 * i)
                        me.add(nc.vector.tensor_tensor(w["b2_high"][q, :], b2_pad[q, :],
                                                       w["b2_high"][q, :].bitcast(F32), ALU.subtract))

                def side(n):
                    for c in range(CHUNKS):
                        if n == slot_of["project", c] + TILES:
                            scale(c)
                    for i in range(3):
                        if n == slot_of["fold", i] + (TILES if i else 1) + 2:
                            fold_low(i)
                    if n in CONSTANT_SLOTS:
                        constants(CONSTANT_SLOTS.index(n))
                    if n in LARGEST_SLOTS:
                        largest(LARGEST_SLOTS.index(n))
                    if n == LARGEST_SLOTS[-1] + 2:
                        row_scales()
                    if n in CLIP_SLOTS:
                        clip(CLIP_SLOTS.index(n))
                    if n in MODULATION_SLOTS:
                        modulation(MODULATION_SLOTS.index(n))
                    if n in MASK_SLOTS:
                        masks(MASK_SLOTS.index(n))

                CONSTANT_SLOTS = (-4, -2, 0)
                LARGEST_SLOTS = (5, 6, 9, 10, 12, 14, 16, 18)
                CLIP_SLOTS = (25, 28, 32, 36, 40)
                MODULATION_SLOTS = (44, 46)
                MASK_SLOTS = (48, 50)

                v.wait_ge(ld_chol, 16 * 3)
                me.add(nc.vector.tensor_copy(w["ident_b"][:, :], ident[:, :]))
                me.add(nc.vector.tensor_copy(elim[:, R:2 * R], ident[0:R, 0:R]))
                v.wait_ge(gram_ready, 1)
                nc.vector.scalar_tensor_tensor(elim[:, 0:R], ident[0:R, 0:R], EPS_GRAM, bank[0][0:R, 0:R],
                                               ALU.mult, ALU.add).then_inc(row_used, 1)
                me.wait()
                window = R + 2
                first_row, second_row = (b[0:R, 0:window] for b in row_bank)
                for j in range(0, R, 2):
                    rows = elim[:, j:j + window]
                    v.wait_ge(row_ready, j + 1)
                    me.add(nc.vector.reciprocal(col[:, 0:1], first_row[:, 0:1]))
                    v.wait_ge(row_ready, j + 2)
                    me.add(nc.vector.tensor_copy(second[:, :], second_row))
                    me.wait(me.n - 1)
                    me.add(nc.vector.tensor_scalar(col[:, 2:3], second_row[:, 0:1], col[:, 0:1], -1.0, ALU.mult, ALU.mult))
                    me.add(nc.vector.scalar_tensor_tensor(col[:, 1:2], elim[:, j:j + 1], col[:, 0:1],
                                                          w["below"][:, j:j + 1], ALU.mult, ALU.mult))
                    me.wait(me.n - 1)
                    me.add(nc.vector.scalar_tensor_tensor(second[:, :], first_row, col[:, 2:3], second[:, :], ALU.mult, ALU.add))
                    me.wait(me.n - 1)
                    me.add(nc.vector.scalar_tensor_tensor(rows, first_row, col[:, 1:2], rows, ALU.mult, ALU.add))
                    me.wait(me.n - 1)
                    me.link(nc.vector.reciprocal(col[:, 0:1], second[:, 1:2]))
                    me.link(nc.vector.scalar_tensor_tensor(col[:, 1:2], elim[:, j + 1:j + 2], col[:, 0:1],
                                                           w["below"][:, j + 1:j + 2], ALU.mult, ALU.mult))
                    nc.vector.scalar_tensor_tensor(rows, second[:, :], col[:, 1:2], rows, ALU.mult, ALU.add).then_inc(row_used, 1)
                    side(j - FIRST_SLOT)
                    side(j - FIRST_SLOT + 1)
                    v.wait_ge(row_used, j // 2 + 2)
                me.link(nc.vector.tensor_tensor(scratch[:, :], elim[:, 0:R], ident[0:R, 0:R], ALU.mult))
                nc.vector.tensor_reduce(col[:, 3:4], scratch[:, :], AX_X, ALU.add).then_inc(chol_done, 1)
                nc.vector.sem_inc(m_copied, 1)
                v.wait_ge(m_turned, 1)
                nc.vector.tensor_copy(inv_t[:, :], bank[0][0:R, 0:R]).then_inc(m_copied, 1)
                v.wait_ge(root_ready, 1)
                me.link(nc.vector.reciprocal(col[:, 5:6], col[:, 4:5]))
                me.link(nc.vector.scalar_tensor_tensor(col[:, 6:7], col[:, 3:4], col[:, 5:6], col[:, 4:5], ALU.mult, ALU.add))
                me.link(nc.vector.tensor_scalar(col[:, 6:7], col[:, 6:7], 0.5, None, ALU.mult))
                me.link(nc.vector.reciprocal(col[:, 5:6], col[:, 6:7]))
                v.wait_ge(q_ready, 1)
                me.link(nc.vector.tensor_scalar(q_t[:, 0, :], bank[1][0:R, 0:R], col[:, 5:6], None, ALU.mult))
                me.link(nc.vector.tensor_tensor(scratch[:, :], q_t[:, 0, :], raw_t[:, :], ALU.mult))
                me.link(nc.vector.tensor_reduce(col[:, 7:8], scratch[:, :], AX_X, ALU.add))
                me.link(nc.vector.tensor_scalar(col[:, 7:8], col[:, 7:8], 0.0, 2.0, ALU.is_ge, ALU.mult))
                me.link(nc.vector.tensor_scalar(col[:, 7:8], col[:, 7:8], -1.0, None, ALU.add))
                me.link(nc.vector.tensor_scalar(q_t[:, 1, :], q_t[:, 0, :], col[:, 7:8], None, ALU.mult))
                nc.vector.tensor_copy(q_t[:, 0, :], q_t[:, 1, :]).then_inc(q_signed, 1)
                v.wait_ge(q_turned, 1)
                high = w["mix_high"][:, :].rearrange("p (a r) -> p a r", a=2)
                me.link(nc.vector.tensor_copy(high, bcast_mid(bank[2][:, 0:R], 2)))
                me.link(nc.vector.tensor_tensor(w["mix_low"][:, :].rearrange("p (a r) -> p a r", a=2),
                                                bcast_mid(bank[2][:, 0:R], 2), high.bitcast(F32), ALU.subtract))


def route(nc, w):
    with ExitStack() as scope:
        s = Memory(nc, scope, "route_")
        bank = s.banks(6)
        hid_bank, logit_bank, turn_bank = bank[0:2], bank[2:4], bank[4:6]
        hid32 = s.sb("hid32", [P, 2, CH])
        logit_t = s.sb("logit_t", [P, 2, CH])
        n_t = CHUNKS * TILES
        logits = s.sb("logits", [P, n_t, NE])
        a, b, pick1, pick2 = (s.sb(n, [P, n_t, NE]) for n in ("a", "b", "pick1", "pick2"))
        spare = s.sb("spare", [P, 1])
        max1, max2, top, wt1, wt2 = (s.sb(n, [P, n_t]) for n in ("max1", "max2", "top", "wt1", "wt2"))
        hid_ready, hid_scaled, hid_high, hid_low = (s.sem(n) for n in ("hid_ready", "hid_scaled", "hid_high", "hid_low"))
        logit_ready, logit_copied, turned, turned_used = (
            s.sem(n) for n in ("logit_ready", "logit_copied", "turned", "turned_used"))
        dve, gap_ready, exp_ready = s.sem("dve"), s.sem("gap_ready"), s.sem("exp_ready")

        def live(c):
            return not isinstance(c, int) or 0 <= c < CHUNKS

        def chunks(engine, step):
            step(0, 0)
            step(1, 1)
            step(2, 0)
            step(3, 1)
            with engine.Fori(2, CHUNKS // 2) as i:
                step(2 * i, 0)
                step(2 * i + 1, 1)
            step(CHUNKS, 0)
            step(CHUNKS + 1, 1)
            step(CHUNKS + 2, 0)

        with nc.Block() as block:

            @block.tensor
            def _(pe):
                def hidden(c, k):
                    need(pe, hid_scaled, c - 1)
                    rhs = w["hid"][:, bass.ds(c * CH, CH)]
                    nc.tensor.matmul(hid_bank[k][:, :], w["mix_high"][:, :], rhs, start=True, stop=False)
                    nc.tensor.matmul(hid_bank[k][:, :], w["mix_low"][:, :], rhs, start=False, stop=True).then_inc(hid_ready, 1)

                def logit(c, k):
                    pe.wait_ge(hid_low, c + 1)
                    need(pe, logit_copied, c - 1)
                    rhs = w["hid"][:, bass.ds(c * CH, CH)]
                    nc.tensor.matmul(logit_bank[k][:, :], w["rw_high"][:, :], rhs, start=True, stop=False)
                    nc.tensor.matmul(logit_bank[k][:, :], w["rw_low"][:, :], rhs, start=False, stop=True).then_inc(logit_ready, 1)

                def turn(c, k):
                    pe.wait_ge(logit_copied, c + 1)
                    need(pe, turned_used, c - 1)
                    for t in range(TILES):
                        last = nc.tensor.transpose(turn_bank[k][:, t * P:(t + 1) * P], logit_t[:, k, t * P:(t + 1) * P],
                                                   w["ident"][:, :])
                    last.then_inc(turned, 1)

                def step(c, k):
                    if live(c):
                        hidden(c, k)
                    if live(c - 2):
                        logit(c - 2, k)
                    if live(c - 3):
                        turn(c - 3, 1 - k)

                chunks(pe, step)

            @block.scalar
            def _(act):
                def high(c, k):
                    act.wait_ge(hid_scaled, c + 1)
                    nc.scalar.activation(w["hid"][:, bass.ds(c * CH, CH)], hid32[:, k, :], ACT.Copy).then_inc(hid_high, 1)

                def logit(c, k):
                    act.wait_ge(logit_ready, c + 1)
                    need(act, turned, c - 1)
                    nc.scalar.activation(logit_t[:, k, :], logit_bank[k][:, :], ACT.Identity,
                                         bias=w["rb"][:, 0:1]).then_inc(logit_copied, 1)

                def step(c, k):
                    if live(c):
                        high(c, k)
                    if live(c - 2):
                        logit(c - 2, k)

                chunks(act, step)
                act.wait_ge(gap_ready, 1)
                nc.scalar.activation(wt2[:, :], top[:, :], ACT.Exp).then_inc(exp_ready, 1)
                nc.scalar.activation(spare[:, :], w["b1"][:, 0:1], ACT.Gelu)

            @block.vector
            def _(v):
                def scale(c, k):
                    v.wait_ge(hid_ready, c + 1)
                    need(v, hid_low, c - 1)
                    nc.vector.tensor_tensor(hid32[:, k, :].rearrange("p (b t) -> p b t", t=SEQ),
                                            hid_bank[k][:, :].rearrange("p (b t) -> p b t", t=SEQ),
                                            bcast_last(w["rank"][:, bass.ds(c * CB, CB)], SEQ), ALU.mult).then_inc(hid_scaled, 1)

                def low(c, k):
                    v.wait_ge(hid_high, c + 1)
                    part = w["hid"][R:P, bass.ds(c * CH, CH)]
                    nc.vector.tensor_tensor(part, hid32[R:P, k, :], part.bitcast(F32), ALU.subtract).then_inc(hid_low, 1)

                def gather(c, k):
                    v.wait_ge(turned, c + 1)
                    nc.vector.tensor_copy(logits[:, bass.ds(c * TILES, TILES), :],
                                          turn_bank[k][:, :].rearrange("p (t n) -> p t n", n=P)[:, :, 0:NE]).then_inc(turned_used, 1)

                def step(c, k):
                    if live(c):
                        scale(c, k)
                    if live(c - 1):
                        low(c - 1, 1 - k)
                    if live(c - 3):
                        gather(c - 3, 1 - k)

                chunks(v, step)

                me = Order(v, dve)
                v.wait_ge(turned_used, CHUNKS)
                prio = bcast_mid(w["prio"][:, :], n_t)

                def best(values, maximum, pick):
                    me.link(nc.vector.tensor_reduce(maximum[:, :], values[:, :, :], AX_X, ALU.max))
                    me.link(nc.vector.tensor_tensor(a[:, :, :], values[:, :, :], bcast_last(maximum[:, :], NE), ALU.is_equal))
                    me.link(nc.vector.tensor_tensor(a[:, :, :], a[:, :, :], prio, ALU.mult))
                    me.link(nc.vector.tensor_reduce(top[:, :], a[:, :, :], AX_X, ALU.max))
                    me.link(nc.vector.tensor_tensor(pick[:, :, :], a[:, :, :], bcast_last(top[:, :], NE), ALU.is_equal))

                best(logits, max1, pick1)
                me.link(nc.vector.scalar_tensor_tensor(b[:, :, :], pick1[:, :, :], -3.0e38, logits[:, :, :], ALU.mult, ALU.add))
                best(b, max2, pick2)
                me.link(nc.vector.tensor_tensor(top[:, :], max2[:, :], max1[:, :], ALU.subtract))
                nc.vector.sem_inc(gap_ready, 1)
                v.wait_ge(exp_ready, 1)
                me.link(nc.vector.tensor_scalar(wt1[:, :], wt2[:, :], 1.0, None, ALU.add))
                me.link(nc.vector.reciprocal(wt1[:, :], wt1[:, :]))
                me.link(nc.vector.tensor_tensor(wt2[:, :], wt2[:, :], wt1[:, :], ALU.mult))
                me.link(nc.vector.tensor_tensor(pick1[:, :, :], pick1[:, :, :], bcast_last(wt1[:, :], NE), ALU.mult))
                me.link(nc.vector.tensor_tensor(pick2[:, :, :], pick2[:, :, :], bcast_last(wt2[:, :], NE), ALU.mult))
                me.link(nc.vector.tensor_tensor(a[:, :, :], pick1[:, :, :], pick2[:, :, :], ALU.add))
                me.link(nc.vector.tensor_copy(w["gate_high"][:, :, :], a[:, :, :]))
                me.link(nc.vector.tensor_tensor(w["gate_low"][:, :, :], a[:, :, :], w["gate_high"][:, :, :].bitcast(F32), ALU.subtract))


def experts(nc, w):
    with ExitStack() as scope:
        s = Memory(nc, scope, "moe_")
        bank = s.banks(8)
        out_bank, h1_bank, gate_bank, qkv_bank = bank[0:2], bank[2:4], bank[4:6], bank[6:8]
        gate_t = s.sb("gate_t", [P, CH], F32R)
        act_h = s.sb("act_h", [P, 2, CH])
        high, low = s.sb("high", [P, 2, CH], F32R), s.sb("low", [P, 2, CH], F32R)
        x2_high, x2_low = s.sb("x2_high", [P, KT, CH], F32R), s.sb("x2_low", [P, KT, CH], F32R)
        names = ("mask_ready", "mask_turned", "gate_copied", "h1_ready", "act_ready", "gate_ready", "gated_ready",
                 "high_ready", "low_ready", "gated_used", "out_ready", "x2_ready", "x2_high_ready", "x2_low_ready",
                 "qkv_ready", "qk_copied", "v_copied")
        (mask_ready, mask_turned, gate_copied, h1_ready, act_ready, gate_ready, gated_ready,
         high_ready, low_ready, gated_used, out_ready, x2_ready, x2_high_ready, x2_low_ready,
         qkv_ready, qk_copied, v_copied) = (s.sem(n) for n in names)
        big = w["big"]
        q_all = big[:, 0:KT * TOK].rearrange("p (t k n) -> p t k n", t=PAIRS, k=KT)
        k_all = big[:, KT * TOK:2 * KT * TOK].rearrange("p (t k n) -> p t k n", t=PAIRS, k=KT)
        v_all = big[:, 2 * KT * TOK:3 * KT * TOK].rearrange("p (t b h d) -> p t b h d", t=PAIRS, b=2, d=DH)
        AHEAD = 3
        BANK_STEPS = (1, 2, 3, 4, 6, 7)
        BANK_OF = (0, 1, 0, 1, 1, 0)
        V_BANKS = (2, 3)

        def chunks(engine, body):
            body(0, True, True)
            body(1, False, True)
            with engine.Fori(2, CHUNKS - 1) as c:
                body(c, False, True)
            body(CHUNKS - 1, False, False)

        def ahead(c, n, more, do):
            if n + AHEAD < NE:
                do(c, n + AHEAD)
            elif more:
                do(c + 1, n + AHEAD - NE)

        def parts_free(engine, c, n):
            if n == 1:
                need(engine, out_ready, c * KT)
            else:
                need(engine, gated_used, c * (NE - 1) + max(n - 1, 0))

        with nc.Block() as block:

            @block.tensor
            def _(pe):
                def mask_turn(c):
                    pe.wait_ge(mask_ready, c + 1)
                    need(pe, v_copied, (c - 2) * 2 + 1)
                    for t in range(TILES):
                        last = nc.tensor.transpose(qkv_bank[0][:, t * P:(t + 1) * P],
                                                   w["mask_pad"][:, t, :, :].rearrange("p g n -> p (g n)"), w["ident"][:, :])
                    last.then_inc(mask_turned, 1)

                def hidden(c, n):
                    need(pe, act_ready, c * NE + n - 1)
                    rhs = w["hid"][:, bass.ds(c * CH, CH)]
                    nc.tensor.matmul(h1_bank[n % 2][:, :], w["w1_high"][:, n * P:(n + 1) * P], rhs, start=True, stop=False)
                    nc.tensor.matmul(h1_bank[n % 2][:, :], w["w1_low"][:, n * P:(n + 1) * P], rhs,
                                     start=False, stop=True).then_inc(h1_ready, 1)

                def gate(c, n):
                    if n == 0:
                        pe.wait_ge(gate_copied, c + 1)
                    need(pe, gated_ready, c * NE + n - 1)
                    nc.tensor.matmul(gate_bank[n % 2][:, :], w["select"][:, n:n + 1].to_broadcast([P, P]), gate_t[:, :],
                                     start=True, stop=True).then_inc(gate_ready, 1)

                def first_layer(c, n):
                    hidden(c, n)
                    gate(c, n)

                def second_layer(c, n):
                    pe.wait_ge(low_ready, c * NE + n + 1)
                    for f in range(KT):
                        cols = slice(f * P, (f + 1) * P)
                        if n == 0:
                            need(pe, x2_ready, (c - 1) * KT + f + 1)
                            nc.tensor.matmul(out_bank[f][:, :], w["b2_high"][:, cols], gate_t[:, :],
                                             start=True, stop=False, skip_group_check=True)
                        for weight, rows in ((w["w2_high"], high), (w["w2_high"], low), (w["w2_low"], high)):
                            last = nc.tensor.matmul(out_bank[f][:, :], weight[:, n, cols], rows[:, n % 2, :], start=False,
                                                    stop=n == NE - 1 and weight is w["w2_low"], skip_group_check=True)
                        if n == NE - 1:
                            last.then_inc(out_ready, 1)
                    if n < NE - 1:
                        last.then_inc(gated_used, 1)

                def qkv(c, i):
                    if i < 2:
                        need(pe, qk_copied, c * 4 - (i == 1))
                    elif i < 4:
                        pe.wait_ge(qk_copied, c * 4 + i - 1)
                    elif i == 4:
                        pe.wait_ge(v_copied, c * 2 + 2)
                    elif not isinstance(c, int) or c + 2 < CHUNKS:
                        pe.wait_ge(gate_copied, c + 3)
                    else:
                        pe.wait_ge(v_copied, c * 2 + 1)
                    passes = ((0, x2_high), (0, x2_low), (1, x2_high))
                    if i in V_BANKS:
                        for t in range(2):
                            at = (2 * (i - 2) + t) * P
                            for k in range(KT):
                                for part, x2 in passes:
                                    last = nc.tensor.matmul(qkv_bank[BANK_OF[i]][:, t * D:(t + 1) * D], x2[:, k, at:at + P],
                                                            w["wv"][:, part, k, :], start=k == 0 and x2 is x2_high and part == 0,
                                                            stop=k == KT - 1 and part == 1)
                    else:
                        for k in range(KT):
                            if i == 0:
                                pe.wait_ge(x2_low_ready, c * KT + k + 1)
                            for part, x2 in passes:
                                weight = w["wq"] if i < 2 else w["wk"]
                                last = nc.tensor.matmul(qkv_bank[BANK_OF[i]][:, :], weight[:, part, k, (i % 2) * P:(i % 2 + 1) * P],
                                                        x2[:, k, :], start=k == 0 and x2 is x2_high and part == 0,
                                                        stop=k == KT - 1 and part == 1)
                    last.then_inc(qkv_ready, 1)

                def body(c, first, more):
                    for n in range(NE):
                        if n == 5 and more:
                            mask_turn(c + 1)
                        second_layer(c, n)
                        if n in BANK_STEPS and not first:
                            qkv(c - 1, BANK_STEPS.index(n))
                        ahead(c, n, more, first_layer)

                hidden(0, 0)
                hidden(0, 1)
                mask_turn(0)
                gate(0, 0)
                gate(0, 1)
                first_layer(0, 2)
                chunks(pe, body)
                for i in range(6):
                    qkv(CHUNKS - 1, i)

            @block.scalar
            def _(act):
                def gates(c):
                    act.wait_ge(mask_turned, c + 1)
                    need(act, gate_ready, c * NE)
                    nc.scalar.activation(gate_t[:, :], qkv_bank[0][:, :], ACT.Copy).then_inc(gate_copied, 1)

                def high_part(c, n):
                    act.wait_ge(gated_ready, c * NE + n + 1)
                    parts_free(act, c, n)
                    nc.scalar.activation(high[:, n % 2, :], act_h[:, n % 2, :], ACT.Copy).then_inc(high_ready, 1)

                def high_before(c, n):
                    if n > 0:
                        high_part(c, n - 1)
                    elif not isinstance(c, int) or c > 0:
                        high_part(c - 1, NE - 1)

                def gelu(c, n):
                    act.wait_ge(h1_ready, c * NE + n + 1)
                    need(act, low_ready, c * NE + n - 1)
                    nc.scalar.activation(act_h[:, n % 2, :], h1_bank[n % 2][:, :], ACT.Gelu,
                                         bias=w["b1"][:, n:n + 1]).then_inc(act_ready, 1)

                def x2_part(c):
                    for f in range(KT):
                        act.wait_ge(x2_ready, c * KT + f + 1)
                        need(act, qkv_ready, c * 6)
                        nc.scalar.activation(x2_high[:, f, :], w["x"][:, f, bass.ds(c * CH, CH)],
                                             ACT.Copy).then_inc(x2_high_ready, 1)

                def copy(c, i):
                    act.wait_ge(qkv_ready, c * 6 + i + 1)
                    dst = (q_all if i < 2 else k_all)[:, bass.ds(c * TILES, TILES), i % 2, :]
                    nc.scalar.activation(dst, qkv_bank[BANK_OF[i]][:, :].rearrange("p (t n) -> p t n", n=P),
                                         ACT.Copy).then_inc(qk_copied, 1)

                def body(c, first, more):
                    for n in range(NE):
                        if n == 5 and more:
                            gates(c + 1)
                        ahead(c, n, more, high_before)
                        if n in BANK_STEPS and BANK_STEPS.index(n) not in V_BANKS and not first:
                            copy(c - 1, BANK_STEPS.index(n))
                        ahead(c, n, more, gelu)
                        if n + AHEAD == NE and not more:
                            high_part(c, NE - 1)
                    x2_part(c)

                gelu(0, 0)
                gates(0)
                for n in range(1, AHEAD):
                    high_before(0, n)
                    gelu(0, n)
                chunks(act, body)
                for i in (0, 1, 4, 5):
                    copy(CHUNKS - 1, i)

            @block.vector
            def _(v):
                def low_part(c, n):
                    v.wait_ge(high_ready, c * NE + n + 1)
                    parts_free(v, c, n)
                    nc.vector.tensor_tensor(low[:, n % 2, :], act_h[:, n % 2, :], high[:, n % 2, :].bitcast(F32),
                                            ALU.subtract).then_inc(low_ready, 1)

                def low_before(c, n):
                    if n > 0:
                        low_part(c, n - 1)
                    elif not isinstance(c, int) or c > 0:
                        low_part(c - 1, NE - 1)

                def weigh(c, n):
                    v.wait_ge(act_ready, c * NE + n + 1)
                    v.wait_ge(gate_ready, c * NE + n + 1)
                    nc.vector.tensor_tensor(act_h[:, n % 2, :], act_h[:, n % 2, :], gate_bank[n % 2][:, :],
                                            ALU.mult).then_inc(gated_ready, 1)

                def add(c, f):
                    v.wait_ge(out_ready, c * KT + f + 1)
                    x = w["x"][:, f, bass.ds(c * CH, CH)]
                    nc.vector.tensor_tensor(x, out_bank[f][:, :], x, ALU.add).then_inc(x2_ready, 1)

                def x2_part(c):
                    for f in range(KT):
                        v.wait_ge(x2_high_ready, c * KT + f + 1)
                        v.wait_ge(x2_ready, c * KT + f + 1)
                        nc.vector.tensor_tensor(x2_low[:, f, :], w["x"][:, f, bass.ds(c * CH, CH)],
                                                x2_high[:, f, :].bitcast(F32), ALU.subtract).then_inc(x2_low_ready, 1)

                def copy(c, i):
                    v.wait_ge(qkv_ready, c * 6 + i + 1)
                    src = qkv_bank[BANK_OF[i]][:, :].rearrange("p (t h j d) -> p t h j d", t=2, j=2, d=DH)
                    for b in range(2):
                        for j in range(2):
                            dst = v_all[j * SEQ:(j + 1) * SEQ, bass.ds(c * TILES + 2 * (i - 2), 2), b, :, :]
                            last = nc.vector.tensor_copy(dst, src[b * SEQ:(b + 1) * SEQ, :, :, j, :])
                    last.then_inc(v_copied, 1)

                def body(c, first, more):
                    for n in range(NE):
                        if n in BANK_STEPS and BANK_STEPS.index(n) in V_BANKS and not first:
                            copy(c - 1, BANK_STEPS.index(n))
                        if n == NE - 1:
                            add(c, 1)
                        ahead(c, n, more, low_before)
                        if n + AHEAD == NE and not more:
                            low_part(c, NE - 1)
                        if n == NE - 2:
                            add(c, 0)
                        ahead(c, n, more, weigh)
                    x2_part(c)

                for n in range(AHEAD):
                    low_before(0, n)
                    weigh(0, n)
                chunks(v, body)
                for i in V_BANKS:
                    copy(CHUNKS - 1, i)

            @block.gpsimd
            def _(pool):
                def masks(c):
                    need(pool, mask_turned, c)
                    for part, g in ((w["gate_high"], 0), (w["gate_low"], 2)):
                        src = part[:, bass.ds(c * TILES, TILES), :].bitcast(F32)
                        for i in range(2):
                            last = nc.gpsimd.tensor_copy(w["mask_pad"][:, :, g + i, 0:NE], src)
                    last.then_inc(mask_ready, 1)

                masks(0)
                with pool.Fori(1, CHUNKS) as c:
                    masks(c)


def attention(nc, w):
    with ExitStack() as scope:
        s = Memory(nc, scope, "att_")
        bank = s.banks(8)
        score_bank, prob_bank, val_bank, proj_bank = bank[0:2], bank[2:4], bank[4:6], bank[6]
        q_s = s.sb("q_s", [P, KT, P])
        k_bd = s.sb("k_bd", [P, KT, 2, HH, SEQ])
        v_bd = s.sb("v_bd", [P, KT, 2, HP, 2, DH])
        neg_max = s.sb("neg_max", [P, KT, HH], BF16)
        probs = s.sb("probs", [P, KT, CH])
        sums = s.sb("sums", [P, KT, HH])
        inv = s.sb("inv", [P, KT, HH])
        normed = s.sb("normed", [P, KT, CH])
        probs_t = s.sb("probs_t", [P, KT, CH])
        heads_t = s.sb("heads_t", [P, KT, P])
        squares = s.sb("squares", [P, D])
        names = ("q_copied", "k_ready_v", "k_ready_g", "v_copied", "v_cleared", "score_ready", "max_ready", "shift_ready",
                 "exp_ready", "sum_ready", "inv_ready", "norm_ready", "turned", "turned_copied", "val_ready",
                 "heads_v", "heads_a", "out_ready", "out_copied", "squared")
        (q_copied, k_ready_v, k_ready_g, v_copied, v_cleared, score_ready, max_ready, shift_ready,
         exp_ready, sum_ready, inv_ready, norm_ready, turned, turned_copied, val_ready,
         heads_v, heads_a, out_ready, out_copied, squared) = (s.sem(n) for n in names)
        big = w["big"]
        q_all = big[:, 0:KT * TOK].rearrange("p (t k n) -> p t k n", t=PAIRS, k=KT)
        out_all = big[:, 0:KT * TOK].rearrange("p (t n) -> p t n", t=PAIRS)
        k_all = big[:, KT * TOK:2 * KT * TOK].rearrange("p (t k b n) -> p t k b n", t=PAIRS, k=KT, b=2)
        v_all = big[:, 2 * KT * TOK:3 * KT * TOK].rearrange("p (t b h d) -> p t b h d", t=PAIRS, b=2, d=DH)
        lag = 3

        def live(t):
            return not isinstance(t, int) or 0 <= t < PAIRS

        def every_pair(engine, step):
            for t in range(lag):
                step(t)
            with engine.Fori(lag, PAIRS - 1) as t:
                step(t)
            for t in range(PAIRS - 1, PAIRS + lag):
                step(t)

        def unit(t, h):
            return 2 * t + h + 1

        def k_of(t, h, b):
            return k_all[:, bass.ds(t, 1), h, b, :].rearrange("p a n -> p (a n)")

        def value_part(h, i):
            return val_bank[h][:, :].rearrange("p (b i q) -> p i b q", b=2, i=HP)[32 * i:32 * i + 32, i, :, :]

        def heads_part(h, i):
            return heads_t[32 * i:32 * i + 32, h, :].rearrange("p (b q) -> p b q", b=2)

        with nc.Block() as block:

            @block.tensor
            def _(pe):
                def scores(t, h):
                    pe.wait_ge(q_copied, unit(t, h))
                    pe.wait_ge(k_ready_v if h == 0 else k_ready_g, t + 1)
                    need(pe, exp_ready, unit(t - 1, h))
                    for b in range(2):
                        half = slice(b * SEQ, (b + 1) * SEQ)
                        nc.tensor.matmul(score_bank[h][half, :], q_s[:, h, half],
                                         k_bd[:, h, b, :, :].rearrange("p h n -> p (h n)"),
                                         start=True, stop=False, skip_group_check=True)
                    nc.tensor.matmul(score_bank[h][:, :], w["ident_b"][:, :], bcast_mid(w["mask_neg"][:, :], HH),
                                     start=False, stop=False, skip_group_check=True).then_inc(score_ready, 1)

                def shift(t, h):
                    pe.wait_ge(max_ready, unit(t, h))
                    nc.tensor.matmul(score_bank[h][:, :], w["ident_b"][:, :], bcast_last(neg_max[:, h, :], SEQ),
                                     start=False, stop=True, skip_group_check=True).then_inc(shift_ready, 1)

                def turn(t, h):
                    pe.wait_ge(norm_ready, unit(t, h))
                    need(pe, turned_copied, unit(t - 1, h))
                    for i in range(HP):
                        last = nc.tensor.transpose(prob_bank[h][:, i * P:(i + 1) * P], normed[:, h, i * P:(i + 1) * P],
                                                   w["ident"][:, :])
                    last.then_inc(turned, 1)

                def values(t, h):
                    pe.wait_ge(turned_copied, unit(t, h))
                    pe.wait_ge(v_copied, unit(t, h))
                    need(pe, heads_v, unit(t - 1, h))
                    need(pe, heads_a, unit(t - 1, h))
                    prob = probs_t[:, h, :].rearrange("p (i b q) -> p b i q", i=HP, b=2)
                    for b in range(2):
                        last = nc.tensor.matmul(val_bank[h][:, b * 256:(b + 1) * 256],
                                                v_bd[:, h, b, :, :, :].rearrange("p i j d -> p (i j d)"),
                                                prob[:, b, :, :], start=True, stop=True)
                    last.then_inc(val_ready, 1)

                def project(t):
                    pe.wait_ge(heads_v, unit(t, 1))
                    pe.wait_ge(heads_a, unit(t, 1))
                    need(pe, squared, t)
                    for h in range(KT):
                        last = nc.tensor.matmul(proj_bank[:, 0:D], heads_t[:, h, :], w["wo"][:, h, :],
                                                start=h == 0, stop=h == KT - 1)
                    last.then_inc(out_ready, 1)

                def step(t):
                    if live(t - 2):
                        turn(t - 2, 1)
                    if live(t):
                        scores(t, 0)
                    if live(t - 1):
                        shift(t - 1, 1)
                    if live(t - 3):
                        project(t - 3)
                    if live(t - 2):
                        values(t - 2, 0)
                    if live(t):
                        scores(t, 1)
                        shift(t, 0)
                    if live(t - 2):
                        values(t - 2, 1)
                    if live(t - 1):
                        turn(t - 1, 0)

                every_pair(pe, step)

            @block.vector
            def _(v):
                def keys(t):
                    need(v, score_ready, unit(t - 1, 0))
                    for b in range(2):
                        last = nc.vector.tensor_tensor(k_bd[:, 0, b, :, :], bcast_mid(k_of(t, 0, b), HH),
                                                       bcast_last(w["heads"][:, :], SEQ), ALU.mult)
                    last.then_inc(k_ready_v, 1)

                def maximum(t, h):
                    v.wait_ge(score_ready, unit(t, h))
                    need(v, shift_ready, unit(t - 1, h))
                    nc.vector.tensor_reduce(neg_max[:, h, :], score_bank[h][:, :].rearrange("p (h n) -> p h n", n=SEQ),
                                            AX_X, ALU.max, negate=True).then_inc(max_ready, 1)

                def sum_up(t, h):
                    v.wait_ge(exp_ready, unit(t, h))
                    nc.vector.tensor_reduce(sums[:, h, :], probs[:, h, :].rearrange("p (h n) -> p h n", n=SEQ),
                                            AX_X, ALU.add).then_inc(sum_ready, 1)
                    v.wait_ge(sum_ready, unit(t, h))
                    need(v, norm_ready, unit(t - 1, h))
                    nc.vector.reciprocal(inv[:, h, :], sums[:, h, :]).then_inc(inv_ready, 1)

                def heads(t, h):
                    v.wait_ge(val_ready, unit(t, h))
                    need(v, out_ready, t)
                    for i in range(2):
                        last = nc.vector.tensor_copy(heads_part(h, i), value_part(h, i))
                    last.then_inc(heads_v, 1)

                def keep(t):
                    v.wait_ge(out_ready, t + 1)
                    v.wait_ge(q_copied, unit(t, 1))
                    nc.vector.tensor_copy(out_all[:, bass.ds(t, 1), :].rearrange("p a n -> p (a n)"),
                                          proj_bank[:, 0:D]).then_inc(out_copied, 1)

                def step(t):
                    if live(t):
                        maximum(t, 0)
                    if live(t - 3):
                        keep(t - 3)
                    if live(t - 1):
                        sum_up(t - 1, 1)
                    if live(t - 2):
                        heads(t - 2, 0)
                    if live(t + 1):
                        keys(t + 1)
                    if live(t):
                        maximum(t, 1)
                    if live(t - 2):
                        heads(t - 2, 1)
                    if live(t):
                        sum_up(t, 0)

                keys(0)
                every_pair(v, step)

            @block.gpsimd
            def _(pool):
                def keys(t):
                    need(pool, score_ready, unit(t - 1, 1))
                    for b in range(2):
                        last = nc.gpsimd.tensor_tensor(k_bd[:, 1, b, :, :], bcast_mid(k_of(t, 1, b), HH),
                                                       bcast_last(w["heads"][:, :], SEQ), ALU.mult)
                    last.then_inc(k_ready_g, 1)

                def normalise(t, h):
                    pool.wait_ge(inv_ready, unit(t, h))
                    need(pool, turned, unit(t - 1, h))
                    nc.gpsimd.tensor_tensor(normed[:, h, :].rearrange("p (h n) -> p h n", n=SEQ),
                                            probs[:, h, :].rearrange("p (h n) -> p h n", n=SEQ),
                                            bcast_last(inv[:, h, :], SEQ), ALU.mult).then_inc(norm_ready, 1)

                def step(t):
                    if live(t - 1):
                        normalise(t - 1, 1)
                    if live(t + 1):
                        keys(t + 1)
                    if live(t):
                        normalise(t, 0)

                keys(0)
                nc.gpsimd.memset(v_bd[:, :, :, :, :, :], 0.0).then_inc(v_cleared, 1)
                every_pair(pool, step)

            @block.scalar
            def _(act):
                def queries(t, h):
                    need(act, score_ready, unit(t - 1, h))
                    nc.scalar.activation(q_s[:, h, :], q_all[:, bass.ds(t, 1), h, :].rearrange("p a n -> p (a n)"),
                                         ACT.Copy).then_inc(q_copied, 1)

                def values(t, h):
                    need(act, val_ready, unit(t - 1, h))
                    for j in range(2):
                        half = slice(j * SEQ, (j + 1) * SEQ)
                        for b in range(2):
                            src = v_all[half, bass.ds(t, 1), b, h * HP:(h + 1) * HP, :].rearrange("p a i d -> p (a i) d")
                            last = nc.scalar.activation(v_bd[half, h, b, :, j, :], src, ACT.Copy)
                    last.then_inc(v_copied, 1)

                def exponent(t, h):
                    act.wait_ge(shift_ready, unit(t, h))
                    need(act, norm_ready, unit(t - 1, h))
                    nc.scalar.activation(probs[:, h, :], score_bank[h][:, :], ACT.Exp, scale=SCALE).then_inc(exp_ready, 1)

                def turned_copy(t, h):
                    act.wait_ge(turned, unit(t, h))
                    need(act, val_ready, unit(t - 1, h))
                    nc.scalar.activation(probs_t[:, h, :], prob_bank[h][:, :], ACT.Copy).then_inc(turned_copied, 1)

                def heads(t, h):
                    act.wait_ge(val_ready, unit(t, h))
                    need(act, out_ready, t)
                    for i in range(2, HP):
                        last = nc.scalar.activation(heads_part(h, i), value_part(h, i), ACT.Copy)
                    last.then_inc(heads_a, 1)

                def square(t):
                    act.wait_ge(out_copied, t + 1)
                    need(act, squared, t)
                    nc.scalar.activation(squares[:, :], proj_bank[:, 0:D], ACT.Square,
                                         accum_out=w["sq_sum"][:, bass.ds(t, 1)]).then_inc(squared, 1)

                def step(t):
                    if live(t - 1):
                        exponent(t - 1, 1)
                    if live(t + 1):
                        queries(t + 1, 0)
                    if live(t - 2):
                        turned_copy(t - 2, 1)
                        heads(t - 2, 0)
                    if live(t - 3):
                        square(t - 3)
                    if live(t - 1):
                        values(t - 1, 0)
                    if live(t):
                        exponent(t, 0)
                    if live(t - 2):
                        heads(t - 2, 1)
                    if live(t - 1):
                        turned_copy(t - 1, 0)
                    if live(t + 1):
                        queries(t + 1, 1)
                    if live(t - 1):
                        values(t - 1, 1)

                queries(0, 0)
                queries(0, 1)
                act.wait_ge(v_cleared, 1)
                every_pair(act, step)


def normalise(nc, w):
    with ExitStack() as scope:
        s = Memory(nc, scope, "norm_")
        bank = s.banks(4)
        ms, root, inv = s.sb("ms", [P, PAIRS]), s.sb("root", [P, PAIRS]), s.sb("inv", [P, PAIRS])
        scaled = s.sb("scaled", [P, 2, TILES, D])
        gained = s.sb("gained", [P, 2, KT, CH])
        part_max = s.sb("part_max", [P, CHUNKS])
        top = s.sb("top", [P, 2])
        nan_sum = s.sb("nan_sum", [P, 1])
        names = ("dve", "ms_ready", "root_ready", "inv_ready", "scaled_ready", "turned", "gained_ready", "shifted",
                 "max_ready", "top_ready", "all_ready")
        (dve, ms_ready, root_ready, inv_ready, scaled_ready, turned, gained_ready, shifted,
         max_ready, top_ready, all_ready) = (s.sem(n) for n in names)
        big = w["big"]
        out_all = big[:, 0:KT * TOK].rearrange("p (t n) -> p t n", t=PAIRS)
        xn = big[:, 2 * KT * TOK:3 * KT * TOK].rearrange("p (c k n) -> p c k n", c=CHUNKS, k=KT)

        def chunks(engine, body):
            body(0, 0)
            body(1, 1)
            with engine.Fori(1, CHUNKS // 2) as i:
                body(2 * i, 0)
                body(2 * i + 1, 1)

        with nc.Block() as block:

            @block.scalar
            def _(act):
                act.wait_ge(ms_ready, 1)
                nc.scalar.activation(root[:, :], ms[:, :], ACT.Sqrt).then_inc(root_ready, 1)
                act.wait_ge(inv_ready, 1)

                def body(c, k):
                    need(act, turned, (c - 1) * KT)
                    for t in range(TILES):
                        at = c * TILES + t
                        last = nc.scalar.activation(scaled[:, k, t, :], out_all[:, bass.ds(at, 1), :].rearrange("p a n -> p (a n)"),
                                                    ACT.Copy, scale=inv[:, bass.ds(at, 1)])
                    last.then_inc(scaled_ready, 1)

                chunks(act, body)

            @block.tensor
            def _(pe):
                def body(c, k):
                    pe.wait_ge(scaled_ready, c + 1)
                    for f in range(KT):
                        need(pe, gained_ready, (c - 2) * KT + f + 1)
                        for t in range(TILES):
                            last = nc.tensor.transpose(bank[2 * k + f][:, t * P:(t + 1) * P], scaled[:, k, t, f * P:(f + 1) * P],
                                                       w["ident"][:, :])
                        last.then_inc(turned, 1)

                chunks(pe, body)

            @block.vector
            def _(v):
                me = Order(v, dve)
                nc.vector.tensor_scalar(ms[:, :], w["sq_sum"][:, :], 1.0 / D, EPS_RMS, ALU.mult, ALU.add).then_inc(ms_ready, 1)
                v.wait_ge(root_ready, 1)
                me.link(nc.vector.reciprocal(inv[:, :], root[:, :]))
                me.link(nc.vector.tensor_tensor(ms[:, :], ms[:, :], inv[:, :], ALU.mult))
                me.link(nc.vector.tensor_tensor(root[:, :], root[:, :], ms[:, :], ALU.add))
                me.link(nc.vector.tensor_scalar(root[:, :], root[:, :], 0.5, None, ALU.mult))
                me.link(nc.vector.reciprocal(inv[:, :], root[:, :]))
                nc.vector.tensor_scalar(inv[:, :], inv[:, :], w["no_key"][:, 0:1], None, ALU.add).then_inc(inv_ready, 1)

                def body(c, k):
                    for f in range(KT):
                        v.wait_ge(turned, c * KT + f + 1)
                        need(v, shifted, (c - 2) * KT + f + 1)
                        nc.vector.tensor_tensor(gained[:, k, f, :].rearrange("p (b t) -> p b t", t=SEQ),
                                                bank[2 * k + f][:, :].rearrange("p (b t) -> p b t", t=SEQ),
                                                bcast_last(w["gain"][:, f, bass.ds(c * CB, CB)], SEQ),
                                                ALU.mult).then_inc(gained_ready, 1)
                    if not isinstance(c, int) or c > 0:
                        largest(c - 1)

                def largest(c):
                    v.wait_ge(shifted, (c + 1) * KT)
                    nc.vector.tensor_reduce(part_max[:, bass.ds(c, 1)], xn[:, bass.ds(c, 1), :, :].rearrange("p a k n -> p (a k n)"),
                                            AX_X, ALU.max, apply_absolute_value=True).then_inc(max_ready, 1)

                chunks(v, body)
                largest(CHUNKS - 1)
                v.wait_ge(max_ready, CHUNKS)
                nc.vector.tensor_reduce(top[:, 0:1], part_max[:, :], AX_X, ALU.max).then_inc(top_ready, 1)
                v.wait_ge(all_ready, 2)
                me.link(nc.vector.tensor_tensor(top[:, 1:2], top[:, 1:2], nan_sum[:, :], ALU.add))
                quant_scale(nc, me, w, top[:, 1:2], 0)

            @block.gpsimd
            def _(pool):
                def body(c, k):
                    for f in range(KT):
                        pool.wait_ge(gained_ready, c * KT + f + 1)
                        nc.gpsimd.tensor_tensor(xn[:, bass.ds(c, 1), f, :].rearrange("p a (b t) -> p (a b) t", t=SEQ),
                                                gained[:, k, f, :].rearrange("p (b t) -> p b t", t=SEQ),
                                                bcast_last(w["shift"][:, f, bass.ds(c * CB, CB)], SEQ),
                                                ALU.add).then_inc(shifted, 1)

                chunks(pool, body)
                nc.gpsimd.partition_all_reduce(nan_sum[:, :], w["no_key"][:, :], P, RADD).then_inc(all_ready, 1)
                pool.wait_ge(top_ready, 1)
                nc.gpsimd.partition_all_reduce(top[:, 1:2], top[:, 0:1], P, RMAX).then_inc(all_ready, 1)


def quant_scale(nc, me, w, largest, which):
    scale, inv = w["quant"][:, 2 * which:2 * which + 1], w["quant"][:, 2 * which + 1:2 * which + 2]
    me.link(nc.vector.tensor_scalar(scale, largest, w["clips"][:, which:which + 1], 1.0 / QMAX, ALU.mult, ALU.mult))
    me.link(nc.vector.reciprocal(inv, scale))
    at = slice(0, 2 * MT) if which == 0 else slice(2 * MT, 2 * MT + KT)
    me.link(nc.vector.tensor_scalar(w["out_scale"][:, at], w["row_scale"][:, at], scale, None, ALU.mult))


def ffn_in(nc, w):
    with ExitStack() as scope:
        s = Memory(nc, scope, "ffi_")
        bank = s.banks(6)
        gate_bank, up_bank = bank[0:3], bank[3:6]
        shifted = s.sb("shifted", [P, 2, KT, CH])
        xq = s.sb("xq", [P, 2, KT, CH], BF16)
        silu = s.sb("silu", [P, MT, CH])
        up = s.sb("up", [P, MT // 2, CH])
        part_max = s.sb("part_max", [P, CHUNKS, MT])
        top = s.sb("top", [P, 2])
        names = ("magic_added", "clipped", "xq_ready", "gate_ready", "up_ready", "silu_ready", "up_copied",
                 "h_ready_v", "h_ready_g", "max_ready", "top_ready", "all_ready", "dve")
        (magic_added, clipped, xq_ready, gate_ready, up_ready, silu_ready, up_copied,
         h_ready_v, h_ready_g, max_ready, top_ready, all_ready, dve) = (s.sem(n) for n in names)
        big = w["big"]
        h_all = big[:, :].rearrange("p (c m n) -> p c m n", c=CHUNKS, m=MT)
        xn = big[:, 2 * KT * TOK:3 * KT * TOK].rearrange("p (c k n) -> p c k n", c=CHUNKS, k=KT)
        OF_V, OF_G = (0, 3, 5), (1, 2, 4)

        def rows(i):
            return P if i < MT - 1 else TAIL

        def h_of(c, i):
            return h_all[0:rows(i), bass.ds(c, 1), i, :].rearrange("p a n -> p (a n)")

        def wait_h(engine, c, i):
            if i in OF_V:
                need(engine, h_ready_v, c * len(OF_V) + OF_V.index(i) + 1)
            else:
                need(engine, h_ready_g, c * len(OF_G) + OF_G.index(i) + 1)

        def wait_up_read(engine, c, i):
            if i in OF_V:
                wait_h(engine, c, i)
            else:
                need(engine, up_copied, c * len(OF_G) + OF_G.index(i) + 1)

        def live(c):
            return not isinstance(c, int) or c < CHUNKS

        def chunks(engine, body):
            body(0, 0)
            body(1, 1)
            with engine.Fori(1, CHUNKS // 2 - 1) as i:
                body(2 * i, 0)
                body(2 * i + 1, 1)
            body(CHUNKS - 2, 0)
            body(CHUNKS - 1, 1)

        with nc.Block() as block:

            @block.scalar
            def _(act):
                def shift(c, k):
                    need(act, xq_ready, c - 1)
                    nc.scalar.activation(shifted[:, k, :, :], xn[:, bass.ds(c, 1), :, :].rearrange("p a k n -> p (a k) n"),
                                         ACT.Identity, scale=w["quant"][:, 1:2], bias=w["magic"][:, 0:1]).then_inc(magic_added, 1)

                def body(c, k):
                    for i in range(MT):
                        act.wait_ge(gate_ready, c * MT + i + 1)
                        wait_h(act, c - 1, i)
                        nc.scalar.activation(silu[0:rows(i), i, :], gate_bank[i % 3][0:rows(i), :], ACT.Silu,
                                             scale=w["out_scale"][0:rows(i), i:i + 1]).then_inc(silu_ready, 1)
                        if i in OF_G:
                            act.wait_ge(up_ready, c * MT + i + 1)
                            nc.scalar.activation(up[:, OF_G.index(i), :], up_bank[i % 3][:, :], ACT.Copy,
                                                 scale=w["out_scale"][:, MT + i:MT + i + 1]).then_inc(up_copied, 1)
                        if i == 2 and live(c + 2):
                            shift(c + 2, k)

                shift(0, 0)
                shift(1, 1)
                chunks(act, body)

            @block.tensor
            def _(pe):
                def body(c, k):
                    pe.wait_ge(xq_ready, c + 1)
                    for i in range(MT):
                        for side in range(2):
                            if side == 0:
                                out, ready = gate_bank, gate_ready
                                need(pe, silu_ready, c * MT + i - 2)
                            else:
                                out, ready = up_bank, up_ready
                                wait_up_read(pe, c - (i < 3), (i - 3) % MT)
                            for f in range(KT):
                                at = (f * 2 * MT + side * MT + i) * P
                                last = nc.tensor.matmul(out[i % 3][0:rows(i), :], w["gu_t"][:, at:at + rows(i)],
                                                        xq[:, k, f, :], start=f == 0, stop=f == KT - 1)
                            last.then_inc(ready, 1)

                chunks(pe, body)

            @block.vector
            def _(v):
                def clip(c, k):
                    v.wait_ge(magic_added, c + 1)
                    nc.vector.tensor_scalar(shifted[:, k, :, :], shifted[:, k, :, :], MAGIC + QMAX, MAGIC - QMAX - 1,
                                            ALU.min, ALU.max).then_inc(clipped, 1)

                def multiply(c, i):
                    v.wait_ge(silu_ready, c * MT + i + 1)
                    v.wait_ge(up_ready, c * MT + i + 1)
                    nc.vector.scalar_tensor_tensor(h_of(c, i), up_bank[i % 3][0:rows(i), :],
                                                   w["out_scale"][0:rows(i), MT + i:MT + i + 1], silu[0:rows(i), i, :],
                                                   ALU.mult, ALU.mult).then_inc(h_ready_v, 1)

                def largest(c, i):
                    wait_h(v, c, i)
                    nc.vector.tensor_reduce(part_max[0:rows(i), bass.ds(c, 1), i], h_of(c, i), AX_X, ALU.max,
                                            apply_absolute_value=True).then_inc(max_ready, 1)

                def body(c, k):
                    if live(c + 1):
                        clip(c + 1, 1 - k)
                    multiply(c, 0)
                    if not isinstance(c, int) or c > 0:
                        largest(c - 1, 5)
                        largest(c - 1, 2)
                    largest(c, 0)
                    multiply(c, 3)
                    if not isinstance(c, int) or c > 0:
                        largest(c - 1, 4)
                    largest(c, 1)
                    multiply(c, 5)
                    largest(c, 3)

                me = Order(v, dve)
                me.link(nc.vector.memset(part_max[:, :, :], 0.0))
                clip(0, 0)
                chunks(v, body)
                largest(CHUNKS - 1, 5)
                largest(CHUNKS - 1, 2)
                largest(CHUNKS - 1, 4)
                v.wait_ge(max_ready, CHUNKS * MT)
                nc.vector.tensor_reduce(top[:, 0:1], part_max[:, :, :].rearrange("p c m -> p (c m)"), AX_X,
                                        ALU.max).then_inc(top_ready, 1)
                v.wait_ge(all_ready, 1)
                quant_scale(nc, me, w, top[:, 1:2], 1)

            @block.gpsimd
            def _(pool):
                def integers(c, k):
                    pool.wait_ge(clipped, c + 1)
                    need(pool, up_ready, (c - 1) * MT)
                    nc.gpsimd.tensor_tensor(xq[:, k, :, :], shifted[:, k, :, :], bcast_last(w["magic"][:, 0:1].to_broadcast([P, KT]), CH),
                                            ALU.subtract).then_inc(xq_ready, 1)

                def body(c, k):
                    for i in OF_G:
                        if i == OF_G[1] and live(c + 1):
                            integers(c + 1, 1 - k)
                        pool.wait_ge(silu_ready, c * MT + i + 1)
                        pool.wait_ge(up_copied, c * len(OF_G) + OF_G.index(i) + 1)
                        nc.gpsimd.tensor_tensor(h_of(c, i), up[:, OF_G.index(i), :], silu[:, i, :], ALU.mult).then_inc(h_ready_g, 1)

                integers(0, 0)
                chunks(pool, body)
                pool.wait_ge(top_ready, 1)
                nc.gpsimd.partition_all_reduce(top[:, 1:2], top[:, 0:1], P, RMAX).then_inc(all_ready, 1)


def ffn_out(nc, w, out):
    with ExitStack() as scope:
        s = Memory(nc, scope, "ffo_")
        bank = s.banks(4)
        HT = MT // 2
        hq = s.sb("hq", [P, 2, MT, CH], BF16)
        y = s.sb("y", [P, 2, KT, CH])
        names = ("magic_added", "clipped", "ints_v", "ints_g", "ints_a", "half_used", "down_ready", "y_ready")
        magic_added, clipped, ints_v, ints_g, ints_a, half_used, down_ready, y_ready = (s.sem(n) for n in names)
        stored = [s.sem("stored0"), s.sem("stored1")]
        h_all = w["big"][:, :].rearrange("p (c m n) -> p c m n", c=CHUNKS, m=MT)

        def h_of(c, first, last):
            return h_all[:, bass.ds(c, 1), first:last, :].rearrange("p a m n -> p (a m) n")

        def free(engine, c, half):
            if half == 0:
                need(engine, half_used, c - 1)
            else:
                need(engine, down_ready, (c - 1) * KT)

        def chunks(engine, body):
            body(0, 0, 0)
            body(1, 1, 0)
            with engine.Fori(1, CHUNKS // 2) as i:
                body(2 * i, 0, i)
                body(2 * i + 1, 1, i)

        with nc.Block() as block:

            @block.scalar
            def _(act):
                def shift(c, half):
                    h = h_of(c, half * HT, (half + 1) * HT)
                    nc.scalar.activation(h, h, ACT.Identity, scale=w["quant"][:, 3:4],
                                         bias=w["magic"][:, 0:1]).then_inc(magic_added, 1)

                def integers(c, k):
                    act.wait_ge(clipped, 2 * c + 1)
                    free(act, c, 0)
                    nc.scalar.activation(hq[:, k, 2:3, :], h_of(c, 2, 3), ACT.Copy, bias=-MAGIC).then_inc(ints_a, 1)

                def body(c, k, i):
                    shift(c, 1)
                    integers(c, k)
                    if not isinstance(c, int) or c + 1 < CHUNKS:
                        shift(c + 1, 0)

                shift(0, 0)
                body(0, 0, 0)
                body(1, 1, 0)
                with act.Fori(1, CHUNKS // 2 - 1) as i:
                    body(2 * i, 0, i)
                    body(2 * i + 1, 1, i)
                body(CHUNKS - 2, 0, 0)
                body(CHUNKS - 1, 1, 0)

            @block.gpsimd
            def _(pool):
                def body(c, k, i):
                    for half in range(2):
                        pool.wait_ge(clipped, 2 * c + half + 1)
                        free(pool, c, half)
                        j, to = half * HT + 1, 2 * HT if half == 1 else 2
                        nc.gpsimd.tensor_tensor(hq[:, k, j:to, :], h_of(c, j, to),
                                                bcast_last(w["magic"][:, 0:1].to_broadcast([P, to - j]), CH),
                                                ALU.subtract).then_inc(ints_g, 1)

                chunks(pool, body)

            @block.vector
            def _(v):
                def quantise(c, k, half):
                    v.wait_ge(magic_added, 2 * c + half + 1)
                    h = h_of(c, half * HT, (half + 1) * HT)
                    nc.vector.tensor_scalar(h, h, MAGIC + QMAX, MAGIC - QMAX - 1, ALU.min, ALU.max).then_inc(clipped, 1)
                    v.wait_ge(clipped, 2 * c + half + 1)
                    free(v, c, half)
                    nc.vector.tensor_scalar(hq[:, k, half * HT:half * HT + 1, :], h_of(c, half * HT, half * HT + 1),
                                            MAGIC, None, ALU.subtract).then_inc(ints_v, 1)

                def finish(c, k, i):
                    need(v, stored[k], 16 * i)
                    for f in range(KT):
                        v.wait_ge(down_ready, c * KT + f + 1)
                        at = 2 * MT + f
                        nc.vector.scalar_tensor_tensor(y[:, k, f, :], bank[2 * k + f][:, :], w["out_scale"][:, at:at + 1],
                                                       w["x"][:, f, bass.ds(c * CH, CH)], ALU.mult, ALU.add).then_inc(y_ready, 1)

                quantise(0, 0, 0)
                quantise(0, 0, 1)
                quantise(1, 1, 0)
                quantise(1, 1, 1)
                finish(0, 0, 0)
                quantise(2, 0, 0)
                quantise(2, 0, 1)
                finish(1, 1, 0)
                with v.Fori(2, CHUNKS // 2) as i:
                    quantise(2 * i - 1, 1, 0)
                    quantise(2 * i - 1, 1, 1)
                    finish(2 * i - 2, 0, i - 1)
                    quantise(2 * i, 0, 0)
                    quantise(2 * i, 0, 1)
                    finish(2 * i - 1, 1, i - 1)
                quantise(CHUNKS - 1, 1, 0)
                quantise(CHUNKS - 1, 1, 1)
                finish(CHUNKS - 2, 0, CHUNKS // 2 - 1)
                finish(CHUNKS - 1, 1, CHUNKS // 2 - 1)

            @block.tensor
            def _(pe):
                def body(c, k, i):
                    for half in range(2):
                        pe.wait_ge(ints_v, 2 * c + half + 1)
                        pe.wait_ge(ints_g, 2 * c + half + 1)
                        if half == 0:
                            pe.wait_ge(ints_a, c + 1)
                        for f in range(KT):
                            if half == 0:
                                need(pe, y_ready, (c - 2) * KT + f + 1)
                            for j in range(half * HT, (half + 1) * HT):
                                at = (j * KT + f) * P
                                last = nc.tensor.matmul(bank[2 * k + f][:, :], w["down_t"][:, at:at + P], hq[:, k, j, :],
                                                        start=j == 0, stop=j == MT - 1)
                            if half == 1:
                                last.then_inc(down_ready, 1)
                        if half == 0:
                            last.then_inc(half_used, 1)

                chunks(pe, body)

            @block.sync
            def _(sp):
                def body(c, k, i):
                    sp.wait_ge(y_ready, (c + 1) * KT)
                    sp.dma_start(out[bass.ds(c, 1)].rearrange("a p k n -> p (a k) n"), y[:, k, :, :]).then_inc(stored[k], 16)

                chunks(sp, body)
                sp.wait_ge(stored[0], 16 * CHUNKS // 2)
                sp.wait_ge(stored[1], 16 * CHUNKS // 2)


def build(nc, io, out):
    with ExitStack() as whole:
        m = Memory(nc, whole, "")
        x_all = m.sb("x_all", [P, KT, TOK])
        big = m.sb("big", [P, CHUNKS * MT * CH])
        big_end = nc.sbuf_base
        w = {
            "x": x_all,
            "big": big,
            "ident": m.sb("ident", [P, P]),
            "ident_b": m.sb("ident_b", [P, P], BF16),
            "magic": m.sb("magic", [P, 1]),
            "clips": m.sb("clips", [P, 2]),
            "quant": m.sb("quant", [P, 4]),
            "row_scale": m.sb("row_scale", [P, 2 * MT + KT]),
            "out_scale": m.sb("out_scale", [P, 2 * MT + KT]),
            "gain": m.sb("gain", [P, KT, BATCH]),
            "shift": m.sb("shift", [P, KT, BATCH]),
            "no_key": m.sb("no_key", [P, 1]),
            "mask_neg": m.sb("mask_neg", [P, SEQ], BF16),
            "heads": m.sb("heads", [P, HH]),
            "sq_sum": m.sb("sq_sum", [P, PAIRS]),
            "gu_t": m.sb("gu_t", [P, KT * 2 * MT * P], BF16),
            "down_t": m.sb("down_t", [P, MT * KT * P], BF16),
            "wo": m.sb("wo", [P, KT, D]),
        }
        with ExitStack() as first:
            f = Memory(nc, first, "")
            w |= {
                "hid": nc.alloc_sbuf_tensor_at("hid", [P, TOK], F32R, offset=big_end - 4 * TOK),
                "mix_high": f.sb("mix_high", [P, P], F32R),
                "mix_low": f.sb("mix_low", [P, P], F32R),
                "rw_high": f.sb("rw_high", [P, P], F32R),
                "rw_low": f.sb("rw_low", [P, P], F32R),
                "w1_high": f.sb("w1_high", [P, NE * P], F32R),
                "w1_low": f.sb("w1_low", [P, NE * P], F32R),
                "w2_high": f.sb("w2_high", [P, NE, D], F32R),
                "w2_low": f.sb("w2_low", [P, NE, D], F32R),
                "b1": f.sb("b1", [P, NE]),
                "rb": f.sb("rb", [P, 1]),
                "b2_high": f.sb("b2_high", [P, D], F32R),
                "select": f.sb("select", [P, NE], F32R),
                "gate_high": f.sb("gate_high", [P, CHUNKS * TILES, NE], F32R),
                "gate_low": f.sb("gate_low", [P, CHUNKS * TILES, NE], F32R),
                "mask_pad": f.sb("mask_pad", [P, TILES, 4, 32]),
                "spec": f.sb("spec", [P, BATCH]),
                "rank": f.sb("rank", [P, BATCH]),
                "prio": f.sb("prio", [P, NE]),
                "below": f.sb("below", [R, R]),
                "wq": f.sb("wq", [P, 2, KT, D], F32R),
                "wk": f.sb("wk", [P, 2, KT, D], F32R),
                "wv": f.sb("wv", [P, 2, KT, D], F32R),
            }
            prepare(nc, w, io)
            route(nc, w)
            experts(nc, w)
        attention(nc, w)
        normalise(nc, w)
        ffn_in(nc, w)
        ffn_out(nc, w, out)


def kernel(**inputs):
    import numpy as np
    import concourse.bacc as bacc
    from concourse.bass_utils import run_bass_kernel_spmd

    a = {name: np.asarray(value) for name, value in inputs.items()}

    def tiles(x):
        return x.reshape(-1, P, x.shape[-1]).transpose(1, 0, 2)

    main = (MT - 1) * P
    gate, up = a["L1_ffn_w_gate"], a["L1_ffn_w_up"]
    row = np.arange(P)
    select = np.zeros((P, NE), np.float32)
    for n in range(NE):
        select[[n, 64 + n], n] = 1.0
    arrays = {
        "x": a["x"].reshape(CHUNKS, CH, KT, P).transpose(0, 3, 2, 1),
        "cond_t": a["cond_256"].T,
        "rank_t": a["cond_64"].T,
        "raw": a["L0_cond_mode_to_rank"],
        "raw_t": a["L0_cond_mode_to_rank"].T,
        "ib_t": tiles(a["L0_cond_input_basis"].T),
        "ob_t": tiles(a["L0_cond_output_basis"].T),
        "rw": tiles(a["L0_ffn_router_w"]),
        "rb": a["L0_ffn_router_b"].reshape(NE, 1),
        "w1": tiles(a["L0_ffn_W1"].transpose(1, 0, 2).reshape(D, NE * P)),
        "b1": a["L0_ffn_b1"].T,
        "w2": a["L0_ffn_W2"].transpose(1, 0, 2),
        "b2": a["L0_ffn_b2"],
        "wq": tiles(a["L1_cond_Wq"].T),
        "wk": tiles(a["L1_cond_Wk"].T),
        "wv": tiles(a["L1_cond_Wv"].T),
        "wo": tiles(a["L1_cond_Wo"].T),
        "wc_t": a["L1_cond_Wc"].T.reshape(R, 4, P),
        "bc": a["L1_cond_bc"].reshape(4, P).T,
        "rms_w": a["L1_cond_rms_scale"].reshape(KT, P).T,
        "mask": a["mask_SxS_bk1"],
        "clips": np.concatenate([a["L1_ffn_clip_x"], a["L1_ffn_clip_down"]]),
        "gate": tiles(gate[:main]),
        "gate_tail": gate[main:],
        "up": tiles(up[:main]),
        "up_tail": up[main:],
        "down": tiles(a["L1_ffn_w_down"]),
        "ident": np.eye(P, dtype=np.float32),
        "below": -np.tril(np.ones((R, R), np.float32), -1),
        "heads": (row[:, None] // DH == np.arange(HH)[None, :]).astype(np.float32),
        "prio": np.ascontiguousarray(np.broadcast_to(np.arange(NE, 0, -1, dtype=np.float32), (P, NE))),
        "select": select,
    }
    nc = bacc.Bacc("TRN2", target_bir_lowering=False, num_devices=1)
    arrays = {f"in_{name}": np.ascontiguousarray(value) for name, value in arrays.items()}
    io = {name[3:]: nc.dram_tensor(name, v.shape, mybir.dt.from_np(v.dtype), kind="ExternalInput").ap()
          for name, v in arrays.items()}
    out = nc.dram_tensor("out", (CHUNKS, P, KT, CH), F32, kind="ExternalOutput").ap()
    build(nc, io, out)
    r = run_bass_kernel_spmd(nc, [arrays], core_ids=[0])
    y = r.results[0]["out"]
    return y.transpose(0, 3, 2, 1).reshape(BATCH, SEQ, D)
```
